# Optimizing a Trainium2 kernel written in Bass

```python
import numpy as np
import jax
import jax.numpy as jnp

def _softmax(x, axis=-1):
    return jax.nn.softmax(x, axis=axis)

def _gelu(x):
    return jax.nn.gelu(x, approximate=True)

def _silu(x):
    return jax.nn.silu(x)

def _sigmoid(x):
    return jax.nn.sigmoid(x)

def _layernorm(x, axis=-1, eps=1e-05):
    m = jnp.mean(x, axis=axis, keepdims=True)
    v = jnp.var(x, axis=axis, keepdims=True)
    return (x - m) / jnp.sqrt(v + eps)

def _scatter_add(tgt, idx, src, axis=0):
    return tgt.at[idx].add(src)

def _segment_sum(src, seg, n):
    return jax.ops.segment_sum(src, seg, n)
kernel_name = 'mk_adj_resnorm_d4_adj_r2_622e81'

def setup_inputs(seed: int=0):
    np.random.seed(seed)
    _w = jnp.asarray

    def _rec_inputs():
        import jax
        import jax.numpy as jnp
        _gk = jax.random.key(seed)
        x = -0.0002928 + 1 * jax.random.normal(jax.random.fold_in(_gk, 1), (2048, 256), jnp.float32)
        _a = jax.random.bernoulli(jax.random.fold_in(_gk, 2), 0.000976562, (2048, 2048))
        _af = _a.astype(jnp.float32)
        adj = _af
        return (x, adj)
    x, adj = _rec_inputs()

    def _L0_gnn_setup():
        import jax, jax.numpy as jnp
        import numpy as np
        N = 4096
        D = 256
        L = 2
        NEG_SLOPE = 0.01

        def _gat_layer(x, W, adj):
            proj = x @ W
            Wh, Ws = jnp.split(proj, 2, axis=-1)
            scores = Wh @ Ws.T
            a = jax.nn.softmax(scores, axis=-1) * adj
            out = a @ Wh
            out = out + x
            return jax.nn.leaky_relu(out, NEG_SLOPE)
        key = jax.random.key(seed)
        k1, k2, k3 = jax.random.split(key, 3)
        inputs = jax.random.normal(k1, (N, D), dtype=jnp.float32)
        adj = jax.random.randint(k2, (N, N), 0, 2).astype(jnp.float32)
        W_stack = jax.random.normal(k3, (L, D, 2 * D), dtype=jnp.float32) * (1.0 / np.sqrt(D))
        return {'inputs': inputs, 'adj': adj, 'W_stack': W_stack}
    _L0_gnn_all = _L0_gnn_setup()
    _L0_gnn_in = {k: v for k, v in _L0_gnn_all.items() if k in ('W_stack',)}
    del _L0_gnn_all

    def _L1_gnn_setup():
        import jax, jax.numpy as jnp
        import numpy as np
        N = 4096
        DIN = 256
        DOUT = 256
        key = jax.random.key(seed)
        k1, k2, k3 = jax.random.split(key, 3)
        H_in = jax.random.normal(k1, (N, DIN), dtype=jnp.float32)
        u = jax.random.uniform(k2, (N, N), dtype=jnp.float32)
        upper = (u < 0.005).astype(jnp.float32)
        upper = jnp.triu(upper, k=1)
        A = upper + upper.T
        limit = np.sqrt(6.0 / (DIN + DOUT)).astype(np.float32)
        W = jax.random.uniform(k3, (DIN, DOUT), dtype=jnp.float32, minval=-limit, maxval=limit)
        return {'H_in': H_in, 'A': A, 'W': W}
    _L1_gnn_all = _L1_gnn_setup()
    _L1_gnn_in = {k: v for k, v in _L1_gnn_all.items() if k in ('W',)}
    del _L1_gnn_all

    def _L2_gnn_setup():
        import jax, jax.numpy as jnp
        import numpy as np
        N = 8192
        F_IN = 256
        F_OUT = 256
        key = jax.random.key(seed)
        k = jax.random.split(key, 6)
        h = jax.random.normal(k[0], (N, F_IN), dtype=jnp.float32)
        adj = jax.random.uniform(k[1], (N, N), dtype=jnp.float32)
        W_neigh = jax.random.normal(k[2], (F_OUT, F_IN), dtype=jnp.float32) * (1.0 / np.sqrt(F_IN))
        b_neigh = jax.random.normal(k[3], (F_OUT,), dtype=jnp.float32) * 0.01
        W_self = jax.random.normal(k[4], (F_OUT, F_IN), dtype=jnp.float32) * (1.0 / np.sqrt(F_IN))
        b_self = jax.random.normal(k[5], (F_OUT,), dtype=jnp.float32) * 0.01
        return {'h': h, 'adj': adj, 'W_neigh': W_neigh, 'b_neigh': b_neigh, 'W_self': W_self, 'b_self': b_self}
    _L2_gnn_all = _L2_gnn_setup()
    _L2_gnn_in = {k: v for k, v in _L2_gnn_all.items() if k in ('W_neigh', 'b_neigh', 'W_self', 'b_self')}
    del _L2_gnn_all

    def _L3_gnn_setup():
        import jax, jax.numpy as jnp
        import numpy as np
        N, NFEAT, NHID = (5000, 256, 128)
        key = jax.random.key(seed)
        k_x, k_adj, k_w1, k_b1, k_w2, k_b2 = jax.random.split(key, 6)
        x = jax.random.normal(k_x, (N, NFEAT), dtype=jnp.float32)
        adj = jax.random.uniform(k_adj, (N, N), dtype=jnp.float32)
        s1 = 1.0 / np.sqrt(NHID)
        s2 = 1.0 / np.sqrt(NFEAT)
        W1 = jax.random.uniform(k_w1, (NFEAT, NHID), minval=-s1, maxval=s1, dtype=jnp.float32)
        b1 = jax.random.uniform(k_b1, (NHID,), minval=-s1, maxval=s1, dtype=jnp.float32)
        W2 = jax.random.uniform(k_w2, (NHID, NFEAT), minval=-s2, maxval=s2, dtype=jnp.float32)
        b2 = jax.random.uniform(k_b2, (NFEAT,), minval=-s2, maxval=s2, dtype=jnp.float32)
        return {'x': x, 'adj': adj, 'W1': W1, 'b1': b1, 'W2': W2, 'b2': b2}
    _L3_gnn_all = _L3_gnn_setup()
    _L3_gnn_in = {k: v for k, v in _L3_gnn_all.items() if k in ('W1', 'b1', 'W2', 'b2')}
    del _L3_gnn_all
    return {'x': x, 'adj': adj, 'L0_gnn_W_stack': _L0_gnn_in['W_stack'], 'L1_gnn_W': _L1_gnn_in['W'], 'L2_gnn_W_neigh': _L2_gnn_in['W_neigh'], 'L2_gnn_b_neigh': _L2_gnn_in['b_neigh'], 'L2_gnn_W_self': _L2_gnn_in['W_self'], 'L2_gnn_b_self': _L2_gnn_in['b_self'], 'L3_gnn_W1': _L3_gnn_in['W1'], 'L3_gnn_b1': _L3_gnn_in['b1'], 'L3_gnn_W2': _L3_gnn_in['W2'], 'L3_gnn_b2': _L3_gnn_in['b2']}

def reference(x, adj, L0_gnn_W_stack, L1_gnn_W, L2_gnn_W_neigh, L2_gnn_b_neigh, L2_gnn_W_self, L2_gnn_b_self, L3_gnn_W1, L3_gnn_b1, L3_gnn_W2, L3_gnn_b2):
    import jax
    import jax.numpy as jnp

    def _L0_gnn_ref(inputs, adj, W_stack):
        import jax, jax.numpy as jnp
        import numpy as np
        N = 4096
        D = 256
        L = 2
        NEG_SLOPE = 0.01

        def _gat_layer(x, W, adj):
            proj = x @ W
            Wh, Ws = jnp.split(proj, 2, axis=-1)
            scores = Wh @ Ws.T
            a = jax.nn.softmax(scores, axis=-1) * adj
            out = a @ Wh
            out = out + x
            return jax.nn.leaky_relu(out, NEG_SLOPE)
        x = inputs
        for l in range(W_stack.shape[0]):
            x = _gat_layer(x, W_stack[l], adj)
        return x

    def _L1_gnn_ref(H_in, A, W):
        import jax, jax.numpy as jnp
        import numpy as np
        N = 4096
        DIN = 256
        DOUT = 256
        A_ = A + jnp.eye(A.shape[0], dtype=A.dtype)
        d_inv_sqrt = jax.lax.rsqrt(A_.sum(axis=1))
        A_norm = A_ * d_inv_sqrt[:, None] * d_inv_sqrt[None, :]
        H_out = jnp.matmul(jnp.matmul(A_norm, H_in), W)
        return jax.nn.relu(H_out)

    def _L2_gnn_ref(h, adj, W_neigh, b_neigh, W_self, b_self):
        import jax, jax.numpy as jnp
        import numpy as np
        N = 8192
        F_IN = 256
        F_OUT = 256
        deg = jnp.sum(adj, axis=1, keepdims=True) + 1e-05
        adj_norm = adj / deg
        h_neigh = adj_norm @ h
        out = h_neigh @ W_neigh.T + b_neigh + h @ W_self.T + b_self
        return jax.nn.relu(out)

    def _L3_gnn_ref(x, adj, W1, b1, W2, b2):
        import jax, jax.numpy as jnp
        import numpy as np
        N, NFEAT, NHID = (5000, 256, 128)
        h = jax.nn.relu(adj @ (x @ W1) + b1)
        out = adj @ (h @ W2) + b2
        return out
    x = _layernorm(x + _L0_gnn_ref(x, adj, L0_gnn_W_stack), axis=-1)
    x = _layernorm(x + _L1_gnn_ref(x, adj, L1_gnn_W), axis=-1)
    x = _layernorm(x + _L2_gnn_ref(x, adj, L2_gnn_W_neigh, L2_gnn_b_neigh, L2_gnn_W_self, L2_gnn_b_self), axis=-1)
    x = _layernorm(x + _L3_gnn_ref(x, adj, L3_gnn_W1, L3_gnn_b1, L3_gnn_W2, L3_gnn_b2), axis=-1)
    return x

_drawn_inputs = setup_inputs


def setup_inputs(seed=0):
    import zlib

    import numpy as np

    out = dict(_drawn_inputs(seed))
    spreads = {}
    factors = {'L0_gnn_W_stack': 4.859, 'L2_gnn_b_neigh': 8.0, 'L2_gnn_b_self': 8.0}
    for name, (base, spread) in spreads.items():
        noise = np.random.default_rng([zlib.crc32(name.encode()), seed]).standard_normal(out[name].shape)
        drawn = base * np.exp(spread * noise) if base else spread * noise
        out[name] = jnp.asarray(drawn.astype(out[name].dtype))
    for name, factor in factors.items():
        out[name] = (out[name] * factor).astype(out[name].dtype)
    return out
```

```python
from contextlib import ExitStack

import concourse.bass as bass
from concourse import mybir

F32 = mybir.dt.float32
F32R = mybir.dt.float32r
ALU = mybir.AluOpType
ACT = mybir.ActivationFunctionType
AX = mybir.AxisListType

P = 128
LN_EPS = 1e-5
DEG_EPS = 1e-5
SLOPE = 0.01



def before(b, u, n=1):
    for _ in range(n):
        b, u = (b, 0) if u else (b - 2, 1)
    return b, u


def after(b, u):
    return (b + 2, 0) if u else (b, 1)


class Signal:

    def __init__(self, sem, base):
        self.sem, self.base = sem, base


def ge(eng, signal, count):
    if isinstance(count, int) and count <= 0:
        return
    if isinstance(signal, Signal):
        eng.wait_ge(signal.sem, count + signal.base)
    else:
        eng.wait_ge(signal, count)


def alone(eng, passed):
    eng.sem_inc(passed, 1)


def adjacency_resnet(nc, x, adj, w_gat, w_gcn, w_neigh, b_neigh, w_self, b_self, w1, b1, w2, b2, out):
    N, D = x.shape
    NT = N // P
    KT = D // P
    CH = 512
    NCH = N // CH
    TPC = CH // P
    LAYERS = w_gat.shape[0]
    HID = w1.shape[1]

    x_rows = x.rearrange("(t p) d -> t p d", p=P)
    x_all = x.rearrange("(t p) d -> p t d", p=P)
    adj_rows = adj.rearrange("(t p) n -> t p n", p=P)
    out_rows = out.rearrange("(t p) d -> t p d", p=P)
    xs_dram = nc.dram_tensor("features_scratch", (N, D), F32, kind="Internal").ap()
    rs_dram = nc.dram_tensor("self_term_scratch", (N, D), F32, kind="Internal").ap()
    xs_rows = xs_dram.rearrange("(t p) d -> t p d", p=P)
    rs_rows = rs_dram.rearrange("(t p) d -> t p d", p=P)

    ctx = ExitStack()
    with ctx:
        def sem(name):
            return ctx.enter_context(nc.semaphore(name))

        def sb(name, shape, dt=F32, scope=ctx):
            return scope.enter_context(nc.sbuf_tensor(name, shape, dt))

        keep = sb("keep", [P, NT, D])
        w2h = sb("w2h", [P, KT, 2 * D], F32R)
        w2l = sb("w2l", [P, KT, 2 * D], F32R)
        w3ah = sb("w3ah", [P, KT, HID], F32R)
        w3al = sb("w3al", [P, KT, HID], F32R)
        w3bh = sb("w3bh", [P, D], F32R)
        w3bl = sb("w3bl", [P, D], F32R)
        ident = sb("ident", [P, P])
        identr = sb("identr", [P, P], F32R)
        ringh = [sb(f"ringh{c}", [P, CH], F32R) for c in range(NCH)]
        ringl = [sb(f"ringl{c}", [P, CH], F32R) for c in range(NCH)]
        xt_h = sb("xt_h", [P, KT, P], F32R)
        xt_l = sb("xt_l", [P, KT, P], F32R)
        xs = [sb(f"xs{u}", [P, D]) for u in range(2)]
        tmp = sb("tmp", [P, D])
        zb = [sb(f"zb{u}", [P, D]) for u in range(2)]
        xres = [sb(f"xres{u}", [P, D]) for u in range(2)]
        bsum = sb("bsum", [P, D])
        deg = sb("deg", [P, NT])
        dinv = sb("dinv", [P, NT])
        rdeg = sb("rdeg", [P, NT])
        stats = [sb(f"stats{u}", [P, 6]) for u in range(2)]
        mvt = [sb(f"mvt{u}", [P, 2]) for u in range(2)]
        mv = sb("mv", [P, NT, 2])
        sd = sb("sd", [P, NT])
        rstd = sb("rstd", [P, NT])
        eps = sb("eps", [P, 1])
        one = sb("one", [P, 1])

        gat = ExitStack()
        wst_h = sb("wst_h", [P, KT, N], F32R, gat)
        wst_l = sb("wst_l", [P, KT, N], F32R, gat)
        val = sb("val", [P, NT, 2 * D], F32R, gat)
        wht = sb("wht", [P, KT, N], F32, gat)
        xtall_h = sb("xtall_h", [P, KT, N], F32R, gat)
        xtall_l = sb("xtall_l", [P, KT, N], F32R, gat)
        prob = [sb(f"prob{u}", [P, N], F32, gat) for u in range(2)]
        arow = [sb(f"arow{u}", [P, N], F32, gat) for u in range(2)]
        wg_h = sb("wg_h", [P, KT, 2 * D], F32R, gat)
        wg_l = sb("wg_l", [P, KT, 2 * D], F32R, gat)
        whs_h = [sb(f"whs_h{u}", [P, KT, P], F32R, gat) for u in range(2)]
        whs_l = [sb(f"whs_l{u}", [P, KT, P], F32R, gat) for u in range(2)]
        mx = [sb(f"mx{u}", [P, NCH], F32, gat) for u in range(2)]
        nmax = [sb(f"nmax{u}", [P, 1], F32, gat) for u in range(2)]
        rs = [sb(f"rs{u}", [P, NCH], F32, gat) for u in range(2)]
        rsum = [sb(f"rsum{u}", [P, 1], F32, gat) for u in range(2)]
        rinv = [sb(f"rinv{u}", [P, 1], F32, gat) for u in range(2)]
        dplus = sb("dplus", [P, NT], F32, gat)
        dsq = sb("dsq", [P, NT], F32, gat)
        wg_raw = prob[0][:, 0:KT * 2 * D].rearrange("p (k n) -> p k n", k=KT)
        wht_g = prob[1][:, 0:KT * CH].rearrange("p (k n) -> p k n", k=KT)
        wn_raw = arow[0][:, 0:KT * D].rearrange("p (k n) -> p k n", k=KT)
        ws_raw = arow[0][:, KT * D:2 * KT * D].rearrange("p (k n) -> p k n", k=KT)
        w1_raw = arow[0][:, 2 * KT * D:3 * KT * D].rearrange("p (k n) -> p k n", k=KT)
        w3a_raw = arow[0][:, 3 * KT * D:3 * KT * D + KT * HID].rearrange("p (k n) -> p k n", k=KT)
        w3b_raw = arow[0][:, 3 * KT * D + KT * HID:3 * KT * D + KT * HID + D]
        bs_raw = arow[1][:, 0:D]
        gat.close()

        adjt = sb("adjt", [P, NT, N])
        pm = sb("pm", [P, NT, 2 * D], F32R)
        rst = sb("rst", [P, D])
        weight = ExitStack()
        w1h = sb("w1h", [P, KT, D], F32R, weight)
        w1l = sb("w1l", [P, KT, D], F32R, weight)
        weight.close()
        first = ExitStack()
        nat = [sb(f"nat{p}", [P, CH], F32, first) for p in range(2)]
        first.close()
        rin = [sb(f"rin{u}", [P, D]) for u in range(2)]
        bout = sb("bout", [P, D])
        bhid = sb("bhid", [P, HID])

        scores = ctx.enter_context(nc.psum_tensor("scores", [P, N], F32))
        tb = [ctx.enter_context(nc.psum_tensor(f"tb{i}", [P, CH], F32)) for i in range(2)]
        ob0 = ctx.enter_context(nc.psum_tensor("ob0", [P, CH], F32))
        xb0 = ctx.enter_context(nc.psum_tensor("xb0", [P, CH], F32))
        ob = [ob0, scores[:, 0:CH]]
        xb = [xb0, scores[:, CH:2 * CH]]
        jb = [scores[:, 2 * CH:3 * CH], scores[:, 3 * CH:4 * CH]]

        passed = {e: sem(f"waits_passed_{e}") for e in ("sync", "gpsimd", "scalar", "vector")}
        s_id = sem("identity_ready")
        s_idr = sem("identity_r_ready")
        s_cst = sem("constants_ready")
        s_x = [sem(f"features_loaded_{g}") for g in range(NCH)]
        s_wraw = sem("weights_loaded")
        s_bias = sem("self_biases_loaded")
        s_bsum = sem("self_bias_sum_ready")
        s_wh = sem("weights_hi_ready")
        s_wl = sem("weights_lo_ready")
        s_w2t = sem("block2_weights_transposed")
        s_w2h = sem("block2_weights_hi_ready")
        s_w2l = sem("block2_weights_lo_ready")
        s_x0t = sem("input_transposed")
        s_x0h = sem("input_transposed_hi")
        s_x0l = sem("input_transposed_lo")
        s_wgraw = [sem(f"gat_weight_loaded_{l}") for l in range(LAYERS)]
        s_wgh = [sem(f"gat_weight_hi_{l}") for l in range(LAYERS)]
        s_wgl = [sem(f"gat_weight_lo_{l}") for l in range(LAYERS)]

        sems, counted = {}, {}

        def counter(name, total):
            if name not in sems:
                sems[name], counted[name] = sem(name), 0
            signal = Signal(sems[name], counted[name])
            counted[name] += total
            return signal

        class Gat:

            def __init__(self, l):
                def s(name, total):
                    return counter(f"gat_{name}", total)
                self.prod = s("projection_done", 4 * NCH + 1)
                self.staged = s("wht_staged", KT * NCH + 1)
                self.kept = s("wht_kept", NCH + 1)
                self.wsh = s("wst_hi", KT * NCH)
                self.wsl = s("wst_lo", KT * NCH + 1)
                self.vt = s("values_transposed", 2 * NCH)
                self.vh = s("values_hi", 2 * NCH)
                self.vl = s("values_lo", 2 * NCH + 1)
                self.adj = [s(f"adjacency_loaded_{u}", 8 * NT) for u in range(2)]
                self.xres = [s(f"residual_loaded_{u}", 8 * NT * (l == LAYERS - 1)) for u in range(2)]
                self.qh = s("query_hi", NT)
                self.q = s("query_ready", NT)
                self.sc = s("scores_ready", 4 * NT)
                self.mx = s("chunk_max", 4 * NT)
                self.nmax = s("row_max", NT)
                self.ex = s("exp_done", 4 * NT)
                self.msk = s("masked", 4 * NT)
                self.deg = s("degree", NT * (l == 0))
                self.tr = s("probs_transposed", 4 * NT)
                self.ah = s("probs_hi", 4 * NT)
                self.al = s("probs_lo", 4 * NT)
                self.av = s("values_summed", 4 * NT)
                self.rsum = s("row_sum", NT)
                self.rinv = s("row_sum_inverse", NT)
                self.tmp = s("lo_half_scaled", NT)
                self.z = s("attention_scaled", NT)
                self.zx = s("residual_added", NT)
                self.new = s("rows_ready", NT)
                self.rows = s("rows_kept", NT)
                self.stat = s("statistics", NT * (l == LAYERS - 1))
                self.aggr = s("tile_mean_variance", NT * (l == LAYERS - 1))
                self.mv = s("mean_variance", NT * (l == LAYERS - 1))
                self.xtr = s("rows_transposed", NT * (l < LAYERS - 1))
                self.xth = s("rows_transposed_hi", NT * (l < LAYERS - 1))
                self.xtl = s("rows_transposed_lo", NT * (l < LAYERS - 1))

        G = [Gat(l) for l in range(LAYERS)]

        s_dpl = sem("degree_plus_eps")
        s_dsq = sem("degree_root")
        s_dinv = sem("degree_inverses")
        s_sd0 = sem("norm0_deviation")
        s_rstd0 = sem("norm0_inverse")
        n_new = sem("norm0_rows")
        n_out = [sem(f"norm0_rows_stored_{u}") for u in range(2)]
        n_xtr = sem("norm0_transposed")
        n_xth = sem("norm0_hi")
        n_xtl = sem("norm0_lo")
        n_prj = sem("block1_projection")
        n_ph = sem("norm0_moving_hi")
        n_pl = sem("norm0_moving_lo")

        class Agg:

            def __init__(self, name, width, proj, norm, load_self, last):
                def s(what, total):
                    return counter(f"agg_{what}", total)
                c = name == "block1"
                self.name, self.w, self.proj, self.norm = name, width, proj, norm
                self.load_self, self.last = load_self, last
                self.nat = [s(f"adjacency_loaded_{p}", 32 * NT * c) for p in range(2)]
                self.xres = [s(f"residual_loaded_{u}", 8 * NT * norm) for u in range(2)]
                self.rin = [s(f"self_term_loaded_{u}", 8 * NT * load_self) for u in range(2)]
                self.tr = s("adjacency_transposed", 4 * NT * c)
                self.kept = s("adjacency_kept", 4 * NT * c)
                self.ah = s("adjacency_hi", 4 * NT)
                self.al = s("adjacency_lo", 4 * NT)
                self.mm = s("sums_done", 4 * NT)
                self.tmp = s("lo_half_ready", NT)
                self.r = s("sum_ready", NT)
                self.rb = s("term_added", NT * (not c))
                self.y = s("residual_added", NT * norm)
                self.stat = s("statistics", NT * norm)
                self.mv = s("mean_variance", NT * norm)
                self.sd = s("deviation", NT * norm)
                self.rstd = s("deviation_inverse", NT * norm)
                self.new = s("rows_ready", NT)
                self.out = [s(f"rows_stored_{u}", 8 * NT * norm) for u in range(2)]
                self.xtr = s("rows_transposed", NT * bool(proj))
                self.xth = s("rows_hi", NT * bool(proj))
                self.xtl = s("rows_lo", NT * bool(proj))
                self.prj = s("projection_done", NT * bool(proj))
                self.pk = s("projection_kept", NT * bool(proj))
                self.rt = s("self_term_ready", NT * c)
                self.rout = s("self_term_stored", 16 * NT * c)
                self.ph = s("moving_hi", NCH * (not c))
                self.pl = s("moving_lo", NCH * (not c))

        C = Agg("block1", D, (w2h, w2l, KT, 2 * D), True, False, False)
        Dg = Agg("block2", D, (w3ah, w3al, KT, HID), True, True, False)
        E = Agg("block3a", HID, (w3bh, w3bl, 1, D), False, False, False)
        F = Agg("block3b", D, None, True, False, True)
        aggs = [C, Dg, E, F]
        s_bt = sem("block3_biases_loaded")

        block = ctx.enter_context(nc.Block())

        @block.sync
        def _(sp):
            per_k = "(k p) n -> p k n"
            for g in range(NCH):
                sp.dma_start(keep[:, g * TPC:(g + 1) * TPC, :], x_all[:, g * TPC:(g + 1) * TPC, :]).then_inc(s_x[g], 16)
                if g == 0:
                    sp.dma_start(wg_raw, w_gat[0].rearrange(per_k, p=P)).then_inc(s_wgraw[0], 16)
            sp.dma_start(wn_raw, w_neigh.rearrange(per_k, p=P)).then_inc(s_wraw, 16)
            sp.dma_start(ws_raw, w_self.rearrange(per_k, p=P)).then_inc(s_wraw, 16)
            sp.dma_start(w1_raw, w_gcn.rearrange(per_k, p=P)).then_inc(s_wraw, 16)
            sp.dma_start(w3a_raw, w1.rearrange(per_k, p=P)).then_inc(s_wraw, 16)
            sp.dma_start(w3b_raw, w2).then_inc(s_wraw, 16)
            sp.dma_start(bsum[:, :], b_neigh[None, :].to_broadcast([P, D])).then_inc(s_bias, 16)
            sp.dma_start(bs_raw, b_self[None, :].to_broadcast([P, D])).then_inc(s_bias, 16)

            for l, g in enumerate(G):
                if l:
                    ge(sp, G[l - 1].tr, 4 * NT)
                    sp.dma_start(wg_raw, w_gat[l].rearrange(per_k, p=P)).then_inc(s_wgraw[l], 16)

                def load(b, u):
                    t = b + u
                    ge(sp, g.msk, 4 * t - 4)
                    if not isinstance(t, int):
                        alone(sp, passed["sync"])
                    if l == 0:
                        ge(sp, g.deg, t - 1)
                    if not isinstance(t, int):
                        alone(sp, passed["sync"])
                    sp.dma_start(arow[u][:, :], adj_rows[t]).then_inc(g.adj[u].sem, 16)
                    if l == LAYERS - 1:
                        ge(sp, g.rows, t - 1)
                        sp.dma_start(xres[u][:, :], x_rows[t]).then_inc(g.xres[u].sem, 16)

                if l == 0:
                    sp.wait_ge(s_wl, 3)
                    sp.wait_ge(s_w2t, 2)
                    sp.wait_ge(s_bsum, 1)
                else:
                    ge(sp, G[l - 1].msk, 4 * NT)
                    ge(sp, G[l - 1].deg, NT)
                load(0, 0)
                load(0, 1)
                with sp.Fori(1, NT // 2) as half:
                    b = 2 * half
                    load(b, 0)
                    load(b, 1)

            def store0(b, u):
                sp.wait_ge(n_new, b + u + 1)
                sp.dma_start(xs_rows[b + u], xs[u][:, :]).then_inc(n_out[u], 16)

            with sp.Fori(0, NT // 2) as half:
                b = 2 * half
                store0(b, 0)
                store0(b, 1)
            for u in range(2):
                sp.wait_ge(n_out[u], 8 * NT)

            for k, a in enumerate(aggs):
                prev = aggs[k - 1] if k else None
                if a.load_self:
                    ge(sp, prev.rout, 16 * NT)
                if k == 1:
                    ge(sp, C.tr, 4 * NT)
                    sp.dma_start(bout[:, :], b2[None, :].to_broadcast([P, D])).then_inc(s_bt, 16)
                    sp.dma_start(bhid[:, :], b1[None, :].to_broadcast([P, HID])).then_inc(s_bt, 16)

                def load_nat(t, c):
                    n = 4 * t + c
                    ge(sp, a.tr, n - 1)
                    sp.dma_start(nat[c % 2][:, :], adj_rows[t][:, c * CH:(c + 1) * CH]).then_inc(a.nat[c % 2].sem, 16)

                def load_res(b, u):
                    t = b + u
                    if a.norm:
                        ge(sp, a.y, t - 1)
                        sp.dma_start(xres[u][:, :], xs_rows[t]).then_inc(a.xres[u].sem, 16)
                    if a.load_self:
                        sp.dma_start(rin[u][:, :], rs_rows[t]).then_inc(a.rin[u].sem, 16)

                def store(b, u):
                    t = b + u
                    if a.norm:
                        ge(sp, a.new, t + 1)
                        dst = out_rows if a.last else xs_rows
                        sp.dma_start(dst[t], xs[u][:, :]).then_inc(a.out[u].sem, 16)
                    if a is C:
                        ge(sp, a.rt, t + 1)
                        sp.dma_start(rs_rows[t], rst[:, :]).then_inc(a.rout.sem, 16)

                if a is C:
                    sp.wait_ge(n_pl, NT)
                    for c in range(NCH):
                        load_nat(0, c)
                if k and a.norm:
                    src = aggs[k - 1] if aggs[k - 1].norm else aggs[k - 2]
                    for u in range(2):
                        ge(sp, src.out[u], 8 * NT)

                def slot(b, u, nxt=True, fin=True):
                    load_res(b, u)
                    if a is C and nxt:
                        for c in range(NCH):
                            load_nat(b + u + 1, c)
                    if fin:
                        store(*before(b, u, 2))

                slot(0, 0, fin=False)
                slot(0, 1, fin=False)
                with sp.Fori(1, NT // 2 - 1) as half:
                    b = 2 * half
                    slot(b, 0)
                    slot(b, 1)
                slot(NT - 2, 0)
                slot(NT - 2, 1, nxt=False)
                store(NT - 2, 0)
                store(NT - 2, 1)
            for u in range(2):
                ge(sp, F.out[u], 8 * NT)
            ge(sp, C.rout, 16 * NT)

        @block.gpsimd
        def _(pool):
            nc.gpsimd.memset(ident[:, :], 0.0).then_inc(s_id, 1)
            pool.wait_ge(s_id, 1)
            nc.gpsimd.affine_select(out=ident[:, :], in_=ident[:, :], compare_op=ALU.not_equal, fill=1.0, base=0,
                                    pattern=[[-1, P]], channel_multiplier=1).then_inc(s_id, 1)
            nc.gpsimd.memset(eps[:, :], LN_EPS).then_inc(s_cst, 1)
            nc.gpsimd.memset(one[:, :], 1.0).then_inc(s_cst, 1)
            pool.wait_ge(s_bias, 32)
            nc.gpsimd.tensor_tensor(bsum[:, :], bsum[:, :], bs_raw, ALU.add).then_inc(s_bsum, 1)

            for l, g in enumerate(G):
                def query(b, u):
                    t = b + u
                    ge(pool, g.sc, 4 * t - 4)
                    if not isinstance(t, int):
                        alone(pool, passed["gpsimd"])
                    src = wht[:, :, bass.ts(t, P)]
                    nc.gpsimd.tensor_copy(whs_h[u][:, :, :], src).then_inc(g.qh.sem, 1)
                    ge(pool, g.qh, t + 1)
                    alone(pool, passed["gpsimd"])
                    nc.gpsimd.tensor_tensor(whs_l[u][:, :, :], src, whs_h[u][:, :, :].bitcast(F32),
                                            ALU.subtract).then_inc(g.q.sem, 1)

                def mask(b, u):
                    t = b + u
                    ge(pool, g.adj[u], 8 * b + 16)
                    for c in range(NCH):
                        ge(pool, g.ex, 4 * t + c + 1)
                        cs = slice(c * CH, (c + 1) * CH)
                        nc.gpsimd.tensor_tensor(prob[u][:, cs], prob[u][:, cs], arow[u][:, cs],
                                                ALU.mult).then_inc(g.msk.sem, 1)

                def residual(b, u):
                    t = b + u
                    ge(pool, g.z, t + 1)
                    alone(pool, passed["gpsimd"])
                    nc.gpsimd.tensor_tensor(zb[u][:, :], zb[u][:, :], keep[:, t, :], ALU.add).then_inc(g.zx.sem, 1)

                def keep_rows(b, u):
                    if l < LAYERS - 1:
                        ge(pool, g.new, b + u + 1)
                        alone(pool, passed["gpsimd"])
                        nc.gpsimd.tensor_copy(keep[:, b + u, :], xs[u][:, :]).then_inc(g.rows.sem, 1)

                def slot(b, u, main=True, nxt=True, av=True, fin=True):
                    if fin:
                        keep_rows(*before(b, u, 2))
                    if nxt:
                        query(*after(b, u))
                    if main:
                        mask(b, u)
                    if av:
                        residual(*before(b, u))

                ge(pool, g.kept, NCH + 1)
                query(0, 0)
                slot(0, 0, av=False, fin=False)
                slot(0, 1, fin=False)
                with pool.Fori(1, NT // 2 - 1) as half:
                    b = 2 * half
                    slot(b, 0)
                    slot(b, 1)
                slot(NT - 2, 0)
                slot(NT - 2, 1, nxt=False)
                slot(NT, 0, main=False, nxt=False)
                slot(NT, 1, main=False, nxt=False, av=False)

            def term(a, b, u):
                t = b + u
                ge(pool, a.r, t + 1)
                if a is Dg:
                    ge(pool, a.rin[u], 8 * b + 16)
                    nc.gpsimd.tensor_tensor(zb[u][:, :], zb[u][:, :], rin[u][:, :], ALU.add).then_inc(a.rb.sem, 1)
                elif a is E:
                    nc.gpsimd.tensor_tensor(zb[u][:, 0:HID], zb[u][:, 0:HID], bhid[:, :], ALU.add).then_inc(a.rb.sem, 1)
                else:
                    nc.gpsimd.tensor_tensor(zb[u][:, :], zb[u][:, :], bout[:, :], ALU.add).then_inc(a.rb.sem, 1)

            pool.wait_ge(s_bt, 32)
            for a in (Dg, E, F):
                with pool.Fori(0, NT // 2) as half:
                    b = 2 * half
                    term(a, b, 0)
                    term(a, b, 1)

        @block.scalar
        def _(act):
            def copy(dst, src, **kw):
                return nc.scalar.activation(dst, src, ACT.Copy, **kw)

            act.wait_ge(s_wgraw[0], 16)
            copy(wg_h[:, :, :], wg_raw).then_inc(s_wgh[0], 1)
            for g in range(NCH):
                for k in range(KT):
                    act.wait_ge(s_x0t, KT * g + k + 1)
                    copy(xtall_h[:, k, g * CH:(g + 1) * CH], tb[k][:, :]).then_inc(s_x0h, 1)
            act.wait_ge(s_wraw, 5 * 16)
            copy(w1h[:, :, :], w1_raw).then_inc(s_wh, 1)
            copy(w3ah[:, :, :], w3a_raw).then_inc(s_wh, 1)
            copy(w3bh[:, :], w3b_raw).then_inc(s_wh, 1)
            for k in range(KT):
                act.wait_ge(s_w2t, k + 1)
                copy(w2h[:, k, :], tb[k][:, :]).then_inc(s_w2h, 1)

            for l, g in enumerate(G):
                if l:
                    act.wait_ge(s_wgraw[l], 16)
                    ge(act, G[l - 1].prod, 4 * NCH + 1)
                    copy(wg_h[:, :, :], wg_raw).then_inc(s_wgh[l], 1)
                    ge(act, G[l - 1].tr, 4 * NT)
                act.sem_inc(g.kept.sem, 1)
                with act.Fori(0, NCH) as i:
                    ge(act, g.kept, i + 1)
                    for o in range(KT):
                        ge(act, g.prod, 4 * i + o + 2)
                        copy(wht_g[:, o, :], scores[:, o * CH:(o + 1) * CH]).then_inc(g.staged.sem, 1)
                    for o in range(KT):
                        ge(act, g.prod, 4 * i + KT + o + 2)
                        alone(act, passed["scalar"])
                        copy(wst_h[:, o, bass.ts(i, CH)], scores[:, (KT + o) * CH:(KT + o + 1) * CH])\
                            .then_inc(g.wsh.sem, 1)
                    for h in range(2):
                        ge(act, g.vt, 2 * i + h + 1)
                        alone(act, passed["scalar"])
                        copy(val[:, bass.ds(i * TPC + 2 * h, 2), 0:D],
                             tb[h][:, :].rearrange("p (a d) -> p a d", a=2)).then_inc(g.vh.sem, 1)

                def hi(b, u, c):
                    n = 4 * (b + u) + c
                    ge(act, g.tr, n + 1)
                    ge(act, g.av, n - 3)
                    copy(ringh[c][:, :], tb[c % 2][:, :]).then_inc(g.ah.sem, 1)

                def exp(b, u, c):
                    t = b + u
                    if c == 0:
                        ge(act, g.nmax, t + 1)
                        ge(act, g.tr, 4 * t - 4)
                        ge(act, g.rsum, t - 1)
                    cs = slice(c * CH, (c + 1) * CH)
                    nc.scalar.activation(prob[u][:, cs], scores[:, cs], ACT.Exp, bias=nmax[u][:, :],
                                         accum_out=rs[u][:, c:c + 1]).then_inc(g.ex.sem, 1)

                def lo_half(b, u):
                    t = b + u
                    ge(act, g.av, 4 * t + 4)
                    ge(act, g.rinv, t + 1)
                    ge(act, g.z, t)
                    copy(tmp[:, :], ob0[:, D:2 * D], scale=rinv[u][:, :]).then_inc(g.tmp.sem, 1)

                def rows_hi(b, u):
                    if l < LAYERS - 1:
                        t = b + u
                        ge(act, g.xtr, t + 1)
                        alone(act, passed["scalar"])
                        copy(xtall_h[:, :, bass.ts(t, P)],
                             xb0[:, 0:D].rearrange("p (k i) -> p k i", k=KT)).then_inc(g.xth.sem, 1)

                def slot(b, u, main=True, av=True, fin=True):
                    p = before(b, u)
                    if av:
                        hi(*p, 0)
                        hi(*p, 1)
                    if fin:
                        rows_hi(*before(b, u, 2))
                    if main:
                        exp(b, u, 0)
                    if av:
                        hi(*p, 2)
                    if main:
                        exp(b, u, 1)
                        exp(b, u, 2)
                    if av:
                        hi(*p, 3)
                    if main:
                        exp(b, u, 3)
                    if av:
                        lo_half(*p)

                slot(0, 0, av=False, fin=False)
                slot(0, 1, fin=False)
                slot(2, 0)
                slot(2, 1)
                with act.Fori(2, NT // 2) as half:
                    b = 2 * half
                    slot(b, 0)
                    slot(b, 1)
                slot(NT, 0, main=False)
                slot(NT, 1, main=False, av=False)

            act.wait_ge(s_cst, 2)
            ge(act, G[0].deg, NT)
            nc.scalar.activation(dsq[:, :], deg[:, :], ACT.Sqrt, bias=one[:, :]).then_inc(s_dsq, 1)
            ge(act, G[-1].mv, NT)
            nc.scalar.activation(sd[:, :], mv[:, :, 1], ACT.Sqrt, bias=eps[:, :]).then_inc(s_sd0, 1)

            def n_hi(b, u):
                t = b + u
                act.wait_ge(n_xtr, t + 1)
                ge(act, n_prj, t)
                copy(xt_h[:, :, :], xb[u][:, 0:D].rearrange("p (k i) -> p k i", k=KT)).then_inc(n_xth, 1)

            def n_moving(b, u):
                t = b + u
                act.wait_ge(n_prj, t + 1)
                alone(act, passed["scalar"])
                copy(pm[:, t, 0:D], jb[u][:, 0:D], scale=dinv[:, bass.ds(t, 1)]).then_inc(n_ph, 1)

            act.wait_ge(s_dinv, 2)
            ge(act, G[-1].av, 4 * NT)
            n_hi(0, 0)
            n_moving(0, 0)
            n_hi(0, 1)
            n_moving(0, 1)
            with act.Fori(1, NT // 2) as half:
                b = 2 * half
                for u in range(2):
                    n_hi(b, u)
                    n_moving(b, u)

            for k, a in enumerate(aggs):
                w = a.w
                if k:
                    prev = aggs[k - 1]
                    ge(act, prev.pk, NT)
                    ge(act, prev.mm, 4 * NT)
                    for q in range(NCH):
                        js = slice(q * TPC, (q + 1) * TPC)
                        copy(pm[:, js, 0:w], keep[:, js, 0:w]).then_inc(a.ph.sem, 1)

                def keep_adj(t, c):
                    ge(act, a.tr, 4 * t + c + 1)
                    alone(act, passed["scalar"])
                    copy(adjt[:, t, c * CH:(c + 1) * CH], tb[c % 2][:, :]).then_inc(a.kept.sem, 1)

                def hi(t, c):
                    n = 4 * t + c
                    if a is C:
                        ge(act, a.kept, n + 1)
                    ge(act, a.mm, n - 3)
                    alone(act, passed["scalar"])
                    copy(ringh[c][:, :], adjt[:, t, c * CH:(c + 1) * CH]).then_inc(a.ah.sem, 1)

                def rows_hi(b, u):
                    t = b + u
                    if a.proj:
                        kt = a.proj[2]
                        ge(act, a.xtr, t + 1)
                        ge(act, a.prj, t)
                        copy(xt_h[:, 0:kt, :], xb[u][:, 0:kt * P].rearrange("p (k i) -> p k i", k=kt))\
                            .then_inc(a.xth.sem, 1)

                def lo_half(b, u):
                    t = b + u
                    ge(act, a.mm, 4 * t + 4)
                    ge(act, a.r, t)
                    alone(act, passed["scalar"])
                    kw = {}
                    if a is C:
                        kw = {"scale": dinv[:, bass.ds(t, 1)]}
                    elif a is Dg:
                        kw = {"scale": rdeg[:, bass.ds(t, 1)]}
                    copy(tmp[:, 0:w], ob[u][:, w:2 * w], **kw).then_inc(a.tmp.sem, 1)

                def deviation(b, u):
                    t = b + u
                    if a.norm:
                        ge(act, a.mv, t + 1)
                        nc.scalar.activation(sd[:, u:u + 1], mv[:, u, 1:2], ACT.Sqrt, bias=eps[:, :])\
                            .then_inc(a.sd.sem, 1)

                def keep_proj(b, u):
                    t = b + u
                    if a.proj:
                        width = min(D, a.proj[3])
                        ge(act, a.prj, t + 1)
                        alone(act, passed["scalar"])
                        copy(keep[:, t, 0:width], jb[u][:, 0:width]).then_inc(a.pk.sem, 1)

                def slot(b, u, main=True, nxt=True, ep=True, fin=True):
                    t = b + u
                    p, pp = before(b, u), before(b, u, 2)
                    fresh = a is C and nxt
                    if fin:
                        rows_hi(*pp)
                    if ep:
                        lo_half(*p)
                    if main:
                        hi(t, 2)
                    if fresh:
                        keep_adj(t + 1, 0)
                    if ep:
                        deviation(*p)
                    if main:
                        hi(t, 3)
                    if fresh:
                        keep_adj(t + 1, 1)
                    if fin:
                        keep_proj(*pp)
                    if nxt:
                        hi(t + 1, 0)
                    if fresh:
                        keep_adj(t + 1, 2)
                    if nxt:
                        hi(t + 1, 1)
                    if fresh:
                        keep_adj(t + 1, 3)

                if a is C:
                    for c in range(NCH):
                        keep_adj(0, c)
                hi(0, 0)
                hi(0, 1)
                slot(0, 0, ep=False, fin=False)
                slot(0, 1, fin=False)
                slot(2, 0)
                slot(2, 1)
                with act.Fori(2, NT // 2 - 1) as half:
                    b = 2 * half
                    slot(b, 0)
                    slot(b, 1)
                slot(NT - 2, 0)
                slot(NT - 2, 1, nxt=False)
                slot(NT, 0, main=False, nxt=False)
                slot(NT, 1, main=False, nxt=False, ep=False)

        @block.vector
        def _(dve):
            dve.wait_ge(s_id, 2)
            nc.vector.tensor_copy(identr[:, :], ident[:, :]).then_inc(s_idr, 1)

            def rest(dst, v, h):
                return nc.vector.tensor_tensor(dst, v, h.bitcast(F32), ALU.subtract)

            dve.wait_ge(s_wgh[0], 1)
            rest(wg_l[:, :, :], wg_raw, wg_h[:, :, :]).then_inc(s_wgl[0], 1)
            for g in range(NCH):
                for k in range(KT):
                    dve.wait_ge(s_x0h, KT * g + k + 1)
                    gs = slice(g * CH, (g + 1) * CH)
                    rest(xtall_l[:, k, gs], tb[k][:, :], xtall_h[:, k, gs]).then_inc(s_x0l, 1)
            dve.wait_ge(s_wh, 3)
            rest(w1l[:, :, :], w1_raw, w1h[:, :, :]).then_inc(s_wl, 1)
            rest(w3al[:, :, :], w3a_raw, w3ah[:, :, :]).then_inc(s_wl, 1)
            rest(w3bl[:, :], w3b_raw, w3bh[:, :]).then_inc(s_wl, 1)
            for k in range(KT):
                dve.wait_ge(s_w2h, k + 1)
                rest(w2l[:, k, :], tb[k][:, :], w2h[:, k, :]).then_inc(s_w2l, 1)

            for l, g in enumerate(G):
                if l:
                    dve.wait_ge(s_wgh[l], 1)
                    rest(wg_l[:, :, :], wg_raw, wg_h[:, :, :]).then_inc(s_wgl[l], 1)
                with dve.Fori(0, NCH) as i:
                    ge(dve, g.staged, KT * i + KT + 1)
                    nc.vector.tensor_copy(wht[:, :, bass.ts(i, CH)], wht_g).then_inc(g.kept.sem, 1)
                    for o in range(KT):
                        ge(dve, g.wsh, KT * i + o + 1)
                        rest(wst_l[:, o, bass.ts(i, CH)], scores[:, (KT + o) * CH:(KT + o + 1) * CH],
                             wst_h[:, o, bass.ts(i, CH)]).then_inc(g.wsl.sem, 1)
                    for h in range(2):
                        ge(dve, g.vh, 2 * i + h + 1)
                        two = bass.ds(i * TPC + 2 * h, 2)
                        rest(val[:, two, D:2 * D], tb[h][:, :].rearrange("p (a d) -> p a d", a=2),
                             val[:, two, 0:D]).then_inc(g.vl.sem, 1)

                def chunk_max(b, u, c):
                    n = 4 * (b + u) + c
                    ge(dve, g.sc, n + 1)
                    if c == 0:
                        ge(dve, g.nmax, b + u - 1)
                    nc.vector.reduce_max(mx[u][:, c:c + 1], scores[:, c * CH:(c + 1) * CH], AX.X)\
                        .then_inc(g.mx.sem, 1)

                def row_max(b, u):
                    t = b + u
                    ge(dve, g.mx, 4 * t + 4)
                    ge(dve, g.ex, 4 * t - 4)
                    nc.vector.reduce_max(nmax[u][:, :], mx[u][:, :], AX.X, negate=True).then_inc(g.nmax.sem, 1)

                def lo(b, u, c):
                    n = 4 * (b + u) + c
                    ge(dve, g.ah, n + 1)
                    ge(dve, g.av, n - 3)
                    rest(ringl[c][:, :], tb[c % 2][:, :], ringh[c][:, :]).then_inc(g.al.sem, 1)

                def row_sum(b, u):
                    t = b + u
                    ge(dve, g.ex, 4 * t + 4)
                    nc.vector.reduce_sum(rsum[u][:, :], rs[u][:, :], AX.X).then_inc(g.rsum.sem, 1)
                    ge(dve, g.rsum, t + 1)
                    ge(dve, g.tmp, t - 1)
                    nc.vector.reciprocal(rinv[u][:, :], rsum[u][:, :]).then_inc(g.rinv.sem, 1)

                def degree(b, u):
                    if l == 0:
                        t = b + u
                        ge(dve, g.adj[u], 8 * b + 16)
                        nc.vector.reduce_sum(deg[:, bass.ds(t, 1)], arow[u][:, :], AX.X).then_inc(g.deg.sem, 1)

                def scaled(b, u):
                    t = b + u
                    ge(dve, g.tmp, t + 1)
                    ge(dve, g.rinv, t + 1)
                    ge(dve, g.new, t - 1)
                    nc.vector.scalar_tensor_tensor(zb[u][:, :], ob0[:, 0:D], rinv[u][:, :], tmp[:, :],
                                                   ALU.mult, ALU.add).then_inc(g.z.sem, 1)

                def finish(b, u):
                    t = b + u
                    ge(dve, g.zx, t + 1)
                    ge(dve, g.rows, t - 1)
                    if l < LAYERS - 1:
                        ge(dve, g.xtr, t - 1)
                    nc.vector.scalar_tensor_tensor(xs[u][:, :], zb[u][:, :], SLOPE, zb[u][:, :],
                                                   ALU.mult, ALU.max).then_inc(g.new.sem, 1)
                    if l == LAYERS - 1:
                        ge(dve, g.new, t + 1)
                        ge(dve, g.xres[u], 8 * b + 16)
                        nc.vector.tensor_tensor(keep[:, t, :], xs[u][:, :], xres[u][:, :], ALU.add)\
                            .then_inc(g.rows.sem, 1)
                        ge(dve, g.rows, t + 1)
                        ge(dve, g.mv, t - 1)
                        alone(dve, passed["vector"])
                        nc.vector.bn_stats(stats[u][:, :], keep[:, t, :]).then_inc(g.stat.sem, 1)
                        ge(dve, g.stat, t + 1)
                        alone(dve, passed["vector"])
                        nc.vector.bn_aggr(mvt[u][:, :], stats[u][:, :]).then_inc(g.aggr.sem, 1)
                        ge(dve, g.aggr, t + 1)
                        nc.vector.tensor_copy(mv[:, t, :], mvt[u][:, :]).then_inc(g.mv.sem, 1)

                def rows_lo(b, u):
                    if l < LAYERS - 1:
                        t = b + u
                        ge(dve, g.xth, t + 1)
                        cols = bass.ts(t, P)
                        rest(xtall_l[:, :, cols], xb0[:, 0:D].rearrange("p (k i) -> p k i", k=KT),
                             xtall_h[:, :, cols]).then_inc(g.xtl.sem, 1)

                def slot(b, u, main=True, av=True, fin=True):
                    p, pp = before(b, u), before(b, u, 2)
                    if fin:
                        finish(*pp)
                    if av:
                        row_sum(*p)
                    if main:
                        chunk_max(b, u, 0)
                        chunk_max(b, u, 1)
                        chunk_max(b, u, 2)
                    if av:
                        lo(*p, 0)
                        lo(*p, 1)
                    if fin:
                        rows_lo(*pp)
                    if main:
                        chunk_max(b, u, 3)
                        row_max(b, u)
                    if av:
                        lo(*p, 2)
                        lo(*p, 3)
                    if main:
                        degree(b, u)
                    if av:
                        scaled(*p)

                slot(0, 0, av=False, fin=False)
                slot(0, 1, fin=False)
                slot(2, 0)
                slot(2, 1)
                with dve.Fori(2, NT // 2) as half:
                    b = 2 * half
                    slot(b, 0)
                    slot(b, 1)
                slot(NT, 0, main=False)
                slot(NT, 1, main=False, av=False)

            nc.vector.tensor_scalar(dplus[:, :], deg[:, :], DEG_EPS, None, ALU.add).then_inc(s_dpl, 1)
            dve.wait_ge(s_dpl, 1)
            nc.vector.reciprocal(rdeg[:, :], dplus[:, :]).then_inc(s_dinv, 1)
            dve.wait_ge(s_dsq, 1)
            nc.vector.reciprocal(dinv[:, :], dsq[:, :]).then_inc(s_dinv, 1)
            dve.wait_ge(s_sd0, 1)
            nc.vector.reciprocal(rstd[:, :], sd[:, :]).then_inc(s_rstd0, 1)
            dve.wait_ge(s_rstd0, 1)
            dve.wait_ge(s_dinv, 2)

            def n_rows(b, u):
                t = b + u
                ge(dve, n_xtr, t - 1)
                ge(dve, n_out[u], 8 * b)
                nc.vector.tensor_scalar(xs[u][:, :], keep[:, t, :], mv[:, t, 0:1], rstd[:, bass.ds(t, 1)],
                                        ALU.subtract, ALU.mult).then_inc(n_new, 1)

            def n_lo(b, u):
                t = b + u
                dve.wait_ge(n_xth, t + 1)
                ge(dve, n_prj, t)
                rest(xt_l[:, :, :], xb[u][:, 0:D].rearrange("p (k i) -> p k i", k=KT), xt_h[:, :, :])\
                    .then_inc(n_xtl, 1)

            def n_moving(b, u):
                t = b + u
                dve.wait_ge(n_ph, t + 1)
                nc.vector.scalar_tensor_tensor(pm[:, t, D:2 * D], jb[u][:, 0:D], dinv[:, bass.ds(t, 1)],
                                               pm[:, t, 0:D].bitcast(F32), ALU.mult, ALU.subtract)\
                    .then_inc(n_pl, 1)

            n_rows(0, 0)
            n_rows(0, 1)
            n_lo(0, 0)
            n_moving(0, 0)
            with dve.Fori(1, NT // 2) as half:
                b = 2 * half
                n_rows(b, 0)
                n_lo(b - 2, 1)
                n_moving(b - 2, 1)
                n_rows(b, 1)
                n_lo(b, 0)
                n_moving(b, 0)
            n_lo(NT - 2, 1)
            n_moving(NT - 2, 1)

            for k, a in enumerate(aggs):
                w = a.w
                prev = aggs[k - 1] if k else None
                if k:
                    for q in range(NCH):
                        js = slice(q * TPC, (q + 1) * TPC)
                        ge(dve, a.ph, q + 1)
                        rest(pm[:, js, w:2 * w], keep[:, js, 0:w], pm[:, js, 0:w]).then_inc(a.pl.sem, 1)

                def lo(t, c):
                    n = 4 * t + c
                    ge(dve, a.ah, n + 1)
                    ge(dve, a.mm, n - 3)
                    rest(ringl[c][:, :], adjt[:, t, c * CH:(c + 1) * CH], ringh[c][:, :]).then_inc(a.al.sem, 1)

                def rows_lo(b, u):
                    t = b + u
                    if a.proj:
                        kt = a.proj[2]
                        ge(dve, a.xth, t + 1)
                        ge(dve, a.prj, t)
                        rest(xt_l[:, 0:kt, :], xb[u][:, 0:kt * P].rearrange("p (k i) -> p k i", k=kt),
                             xt_h[:, 0:kt, :]).then_inc(a.xtl.sem, 1)

                def total(b, u):
                    t = b + u
                    ge(dve, a.tmp, t + 1)
                    dst, o = zb[u][:, 0:w], ob[u][:, 0:w]
                    if a in (C, Dg):
                        d = dinv if a is C else rdeg
                        nc.vector.scalar_tensor_tensor(dst, o, d[:, bass.ds(t, 1)], tmp[:, 0:w],
                                                       ALU.mult, ALU.add).then_inc(a.r.sem, 1)
                    else:
                        nc.vector.tensor_tensor(dst, o, tmp[:, 0:w], ALU.add).then_inc(a.r.sem, 1)

                def rows_free(b, u):
                    if isinstance(b, int) and b == 0:
                        if not k:
                            dve.wait_ge(n_out[u], 8 * NT)
                            dve.wait_ge(n_xtr, NT)
                        else:
                            if prev.norm:
                                ge(dve, prev.out[u], 8 * NT)
                            ge(dve, prev.xtr, NT)

                def residual(b, u):
                    t = b + u
                    if a is C:
                        ge(dve, a.r, t + 1)
                    else:
                        ge(dve, a.rb, t + 1)
                    if not a.norm:
                        rows_free(b, u)
                        ge(dve, a.xtr, t - 1)
                        nc.vector.tensor_scalar(xs[u][:, 0:w], zb[u][:, 0:w], 0.0, None, ALU.max)\
                            .then_inc(a.new.sem, 1)
                        return
                    ge(dve, a.xres[u], 8 * b + 16)
                    if a.last:
                        nc.vector.tensor_tensor(zb[u][:, :], zb[u][:, :], xres[u][:, :], ALU.add).then_inc(a.y.sem, 1)
                    else:
                        nc.vector.scalar_tensor_tensor(zb[u][:, :], zb[u][:, :], 0.0, xres[u][:, :],
                                                       ALU.max, ALU.add).then_inc(a.y.sem, 1)
                    ge(dve, a.y, t + 1)
                    nc.vector.bn_stats(stats[u][:, :], zb[u][:, :]).then_inc(a.stat.sem, 1)
                    ge(dve, a.stat, t + 1)
                    ge(dve, a.sd, t - 1)
                    alone(dve, passed["vector"])
                    nc.vector.bn_aggr(mv[:, u, :], stats[u][:, :]).then_inc(a.mv.sem, 1)

                def norm(b, u):
                    t = b + u
                    if not a.norm:
                        return
                    ge(dve, a.sd, t + 1)
                    nc.vector.reciprocal(rstd[:, u:u + 1], sd[:, u:u + 1]).then_inc(a.rstd.sem, 1)
                    ge(dve, a.rstd, t + 1)
                    rows_free(b, u)
                    if a.proj:
                        ge(dve, a.xtr, t - 1)
                    ge(dve, a.out[u], 8 * b)
                    nc.vector.tensor_scalar(xs[u][:, :], zb[u][:, :], mv[:, u, 0:1], rstd[:, u:u + 1],
                                            ALU.subtract, ALU.mult).then_inc(a.new.sem, 1)

                def self_term(b, u):
                    t = b + u
                    if a is C:
                        ge(dve, a.prj, t + 1)
                        ge(dve, a.pk, t + 1)
                        ge(dve, a.rout, 16 * t)
                        nc.vector.tensor_tensor(rst[:, :], jb[u][:, D:2 * D], bsum[:, :], ALU.add)\
                            .then_inc(a.rt.sem, 1)

                def slot(b, u, main=True, nxt=True, ep=True, fin=True):
                    t = b + u
                    p, pp = before(b, u), before(b, u, 2)
                    if fin:
                        rows_lo(*pp)
                    if ep:
                        total(*p)
                    if main:
                        lo(t, 2)
                    if ep:
                        residual(*p)
                    if main:
                        lo(t, 3)
                    if ep:
                        norm(*p)
                    if fin:
                        self_term(*pp)
                    if nxt:
                        lo(t + 1, 0)
                        lo(t + 1, 1)

                lo(0, 0)
                lo(0, 1)
                slot(0, 0, ep=False, fin=False)
                slot(0, 1, fin=False)
                slot(2, 0)
                slot(2, 1)
                with dve.Fori(2, NT // 2 - 1) as half:
                    b = 2 * half
                    slot(b, 0)
                    slot(b, 1)
                slot(NT - 2, 0)
                slot(NT - 2, 1, nxt=False)
                slot(NT, 0, main=False, nxt=False)
                slot(NT, 1, main=False, nxt=False, ep=False)

        @block.tensor
        def _(pe):
            def mm(o, l, r, start, stop):
                return nc.tensor.matmul(o, l, r, start=start, stop=stop)

            def exact3(o, pairs):
                terms = [p for sh, sl, mh, ml in pairs for p in ((sh, mh), (sh, ml), (sl, mh))]
                for i, (s, m) in enumerate(terms):
                    last = mm(o, s, m, i == 0, i == len(terms) - 1)
                return last

            pe.wait_ge(s_id, 2)
            for g in range(NCH):
                pe.wait_ge(s_x[g], 16)
                for k in range(KT):
                    ge(pe, s_x0l, KT * (g - 1) + k + 1)
                    for a in range(TPC):
                        last = nc.tensor.transpose(tb[k][:, a * P:(a + 1) * P],
                                                   keep[:, g * TPC + a, k * P:(k + 1) * P], ident[:, :])
                    last.then_inc(s_x0t, 1)
            pe.wait_ge(s_wraw, 5 * 16)
            for k in range(KT):
                pe.wait_ge(s_x0l, KT * (NCH - 1) + k + 1)
                for i, raw in enumerate((wn_raw, ws_raw)):
                    for o in range(KT):
                        at = i * D + o * P
                        last = nc.tensor.transpose(tb[k][:, at:at + P], raw[:, o, k * P:(k + 1) * P], ident[:, :])
                last.then_inc(s_w2t, 1)
            pe.wait_ge(s_w2l, KT)

            for l, g in enumerate(G):
                pe.wait_ge(s_wgl[l], 1)
                if l:
                    ge(pe, G[l - 1].xtl, NT)
                    ge(pe, G[l - 1].ex, 4 * NT)
                pe.sem_inc(g.prod.sem, 1)
                pe.sem_inc(g.wsl.sem, 1)
                pe.sem_inc(g.staged.sem, 1)
                pe.sem_inc(g.vl.sem, 1)
                with pe.Fori(0, NCH) as i:
                    gs = bass.ts(i, CH)
                    for o in range(2 * KT):
                        if o < KT:
                            ge(pe, g.staged, KT * i + 1)
                        else:
                            ge(pe, g.wsl, KT * i + 1)
                        os = slice(o * P, (o + 1) * P)
                        exact3(scores[:, o * CH:(o + 1) * CH],
                               [(wg_h[:, k, os], wg_l[:, k, os], xtall_h[:, k, gs], xtall_l[:, k, gs])
                                for k in range(KT)]).then_inc(g.prod.sem, 1)
                    ge(pe, g.staged, KT * i + KT + 1)
                    ge(pe, g.vl, 2 * i + 1)
                    for h in range(2):
                        for a in range(2):
                            for k in range(KT):
                                at = a * D + k * P
                                last = nc.tensor.transpose(tb[h][:, at:at + P],
                                                           wht_g[:, k, (2 * h + a) * P:(2 * h + a + 1) * P],
                                                           ident[:, :])
                        last.then_inc(g.vt.sem, 1)
                ge(pe, g.wsl, KT * NCH + 1)
                ge(pe, g.vl, 2 * NCH + 1)

                def score(b, u, c):
                    t = b + u
                    if c == 0:
                        ge(pe, g.q, t + 1)
                    ge(pe, g.ex, 4 * t + c - 3)
                    cs = slice(c * CH, (c + 1) * CH)
                    exact3(scores[:, cs], [(whs_h[u][:, k, :], whs_l[u][:, k, :], wst_h[:, k, cs], wst_l[:, k, cs])
                                           for k in range(KT)]).then_inc(g.sc.sem, 1)

                def turn(b, u, c):
                    n = 4 * (b + u) + c
                    ge(pe, g.msk, n + 1)
                    ge(pe, g.al, n - 1)
                    for q in range(TPC):
                        j = c * TPC + q
                        last = nc.tensor.transpose(tb[c % 2][:, q * P:(q + 1) * P], prob[u][:, j * P:(j + 1) * P],
                                                   ident[:, :])
                    last.then_inc(g.tr.sem, 1)

                def attend(b, u, c):
                    t = b + u
                    ge(pe, g.al, 4 * t + c + 1)
                    if c == 0:
                        ge(pe, g.z, t)
                    for q in range(TPC):
                        j = c * TPC + q
                        qs = slice(q * P, (q + 1) * P)
                        mm(ob0[:, :], ringh[c][:, qs], val[:, j, :], j == 0, False)
                        last = mm(ob0[:, 0:D], ringl[c][:, qs], val[:, j, 0:D], False, j == NT - 1)
                    last.then_inc(g.av.sem, 1)

                def rows(b, u):
                    if l < LAYERS - 1:
                        t = b + u
                        ge(pe, g.new, t + 1)
                        ge(pe, g.xtl, t)
                        for k in range(KT):
                            last = nc.tensor.transpose(xb0[:, k * P:(k + 1) * P], xs[u][:, k * P:(k + 1) * P],
                                                       ident[:, :])
                        last.then_inc(g.xtr.sem, 1)

                def slot(b, u, main=True, av=True, fin=True):
                    p = before(b, u)
                    if main:
                        for c in range(NCH - 1):
                            score(b, u, c)
                    if av:
                        turn(*p, 0)
                        turn(*p, 1)
                    if fin:
                        rows(*before(b, u, 2))
                    if main:
                        score(b, u, NCH - 1)
                    if av:
                        attend(*p, 0)
                        turn(*p, 2)
                        attend(*p, 1)
                        turn(*p, 3)
                        attend(*p, 2)
                        attend(*p, 3)

                slot(0, 0, av=False, fin=False)
                slot(0, 1, fin=False)
                slot(2, 0)
                slot(2, 1)
                with pe.Fori(2, NT // 2) as half:
                    b = 2 * half
                    slot(b, 0)
                    slot(b, 1)
                slot(NT, 0, main=False)
                slot(NT, 1, main=False, av=False)

            ge(pe, G[-1].ex, 4 * NT)

            def n_rows(b, u):
                t = b + u
                pe.wait_ge(n_new, t + 1)
                ge(pe, n_xtl, t - 1)
                for k in range(KT):
                    last = nc.tensor.transpose(xb[u][:, k * P:(k + 1) * P], xs[u][:, k * P:(k + 1) * P], ident[:, :])
                last.then_inc(n_xtr, 1)

            def n_proj(b, u):
                t = b + u
                pe.wait_ge(n_xtl, t + 1)
                ge(pe, n_pl, t - 1)
                exact3(jb[u][:, 0:D], [(xt_h[:, k, :], xt_l[:, k, :], w1h[:, k, :], w1l[:, k, :])
                                       for k in range(KT)]).then_inc(n_prj, 1)

            n_rows(0, 0)
            n_rows(0, 1)
            n_proj(0, 0)
            n_rows(2, 0)
            n_proj(0, 1)
            n_rows(2, 1)
            n_proj(2, 0)
            with pe.Fori(2, NT // 2) as half:
                b = 2 * half
                n_rows(b, 0)
                n_proj(b - 2, 1)
                n_rows(b, 1)
                n_proj(b, 0)
            n_proj(NT - 2, 1)

            for k, a in enumerate(aggs):
                w = a.w
                pe.wait_ge(s_idr, 1)
                if k == 0:
                    pe.wait_ge(n_pl, NT)
                else:
                    prev = aggs[k - 1]
                    ge(pe, prev.pk, NT)
                    ge(pe, prev.r, NT)

                def turn(t, c):
                    n = 4 * t + c
                    ge(pe, a.nat[c % 2], 32 * t + 16 * (c // 2) + 16)
                    ge(pe, a.kept, n - 1)
                    for q in range(TPC):
                        last = nc.tensor.transpose(tb[c % 2][:, q * P:(q + 1) * P], nat[c % 2][:, q * P:(q + 1) * P],
                                                   ident[:, :])
                    last.then_inc(a.tr.sem, 1)

                def main_sum(b, u, c):
                    t = b + u
                    if k and isinstance(t, int) and t == 0:
                        ge(pe, a.pl, c + 1)
                    ge(pe, a.al, 4 * t + c + 1)
                    if c == 0:
                        ge(pe, a.r, t - 1)
                    for q in range(TPC):
                        j = c * TPC + q
                        qs = slice(q * P, (q + 1) * P)
                        end = j == NT - 1
                        mm(ob[u][:, 0:2 * w], ringh[c][:, qs], pm[:, j, 0:2 * w], j == 0, False)
                        last = mm(ob[u][:, 0:w], ringl[c][:, qs], pm[:, j, 0:w], False, end and a is not C)
                    if c == NCH - 1 and a is C:
                        last = mm(ob[u][:, 0:2 * w], identr[:, :], pm[:, t, :], False, True)
                    last.then_inc(a.mm.sem, 1)

                def rows(b, u):
                    t = b + u
                    if a.proj:
                        ge(pe, a.new, t + 1)
                        ge(pe, a.xtl, t - 1)
                        for h in range(a.proj[2]):
                            hs = slice(h * P, (h + 1) * P)
                            last = nc.tensor.transpose(xb[u][:, hs], xs[u][:, hs], ident[:, :])
                        last.then_inc(a.xtr.sem, 1)

                def project(b, u):
                    t = b + u
                    if a.proj:
                        wh, wl, kt, width = a.proj
                        wh3 = wh[:, :, :] if kt > 1 else wh[:, :].rearrange("p (k n) -> p k n", k=1)
                        wl3 = wl[:, :, :] if kt > 1 else wl[:, :].rearrange("p (k n) -> p k n", k=1)
                        ge(pe, a.xtl, t + 1)
                        ge(pe, a.pk, t - 1)
                        if a is C:
                            ge(pe, a.rt, t - 1)
                        exact3(jb[u][:, 0:width], [(xt_h[:, h, :], xt_l[:, h, :], wh3[:, h, :], wl3[:, h, :])
                                                   for h in range(kt)]).then_inc(a.prj.sem, 1)

                def slot(b, u, main=True, nxt=True, ep=True, fin=True):
                    t = b + u
                    p, pp = before(b, u), before(b, u, 2)
                    for c in range(NCH):
                        if main:
                            main_sum(b, u, c)
                        if a is C and nxt and c != 1:
                            turn(t + 1, c)
                        if c == 1:
                            if a is C and nxt:
                                turn(t + 1, c)
                            if fin:
                                project(*pp)
                    if ep:
                        rows(*p)

                if a is C:
                    for c in range(NCH):
                        turn(0, c)
                slot(0, 0, ep=False, fin=False)
                slot(0, 1, fin=False)
                slot(2, 0)
                slot(2, 1)
                with pe.Fori(2, NT // 2 - 1) as half:
                    b = 2 * half
                    slot(b, 0)
                    slot(b, 1)
                slot(NT - 2, 0)
                slot(NT - 2, 1, nxt=False)
                slot(NT, 0, main=False, nxt=False)
                slot(NT, 1, main=False, nxt=False, ep=False)


_INS = ["x", "adj", "L0_gnn_W_stack", "L1_gnn_W", "L2_gnn_W_neigh", "L2_gnn_b_neigh", "L2_gnn_W_self",
        "L2_gnn_b_self", "L3_gnn_W1", "L3_gnn_b1", "L3_gnn_W2", "L3_gnn_b2"]


def kernel(**inputs):
    import numpy as _np
    import concourse.bacc as _bacc
    from concourse import mybir as _mybir
    from concourse.bass_utils import run_bass_kernel_spmd as _run

    nc = _bacc.Bacc("TRN2", target_bir_lowering=False, num_devices=1, dynamic_dma_scratch_size=1024)
    arrays, args = {}, []
    for name in _INS:
        a = _np.ascontiguousarray(inputs[name])
        arrays[f"in_{name}"] = a
        args.append(nc.dram_tensor(f"in_{name}", a.shape, _mybir.dt.from_np(a.dtype), kind="ExternalInput").ap())
    shape = inputs["x"].shape
    args.append(nc.dram_tensor("out_rows", shape, _mybir.dt.float32, kind="ExternalOutput").ap())
    adjacency_resnet(nc, *args)
    r = _run(nc, [arrays], core_ids=[0])
    return r.results[0]["out_rows"]
```

```python
from contextlib import ExitStack

import concourse.bass as bass
from concourse import mybir

F32 = mybir.dt.float32
F32R = mybir.dt.float32r
I32 = mybir.dt.int32
ALU = mybir.AluOpType
ACT = mybir.ActivationFunctionType
AX = mybir.AxisListType

P = 128
LO_BITS = 0xFFF
LN_EPS = 1e-5
DEG_EPS = 1e-5
SLOPE = 0.01



def before(b, u, n=1):
    for _ in range(n):
        b, u = (b, 0) if u else (b - 2, 1)
    return b, u


def after(b, u):
    return (b + 2, 0) if u else (b, 1)


class Signal:

    def __init__(self, sem, base):
        self.sem, self.base = sem, base


def ge(eng, signal, count):
    if isinstance(count, int) and count <= 0:
        return
    if isinstance(signal, Signal):
        eng.wait_ge(signal.sem, count + signal.base)
    else:
        eng.wait_ge(signal, count)


def alone(eng, passed):
    eng.sem_inc(passed, 1)


def adjacency_resnet(nc, x, adj, w_gat, w_gcn, w_neigh, b_neigh, w_self, b_self, w1, b1, w2, b2, out):
    N, D = x.shape
    NT = N // P
    KT = D // P
    CH = 512
    NCH = N // CH
    TPC = CH // P
    LAYERS = w_gat.shape[0]
    HID = w1.shape[1]

    x_rows = x.rearrange("(t p) d -> t p d", p=P)
    x_all = x.rearrange("(t p) d -> p t d", p=P)
    adj_rows = adj.rearrange("(t p) n -> t p n", p=P)
    out_rows = out.rearrange("(t p) d -> t p d", p=P)
    xs_dram = nc.dram_tensor("features_scratch", (N, D), F32, kind="Internal").ap()
    rs_dram = nc.dram_tensor("self_term_scratch", (N, D), F32, kind="Internal").ap()
    xs_rows = xs_dram.rearrange("(t p) d -> t p d", p=P)
    rs_rows = rs_dram.rearrange("(t p) d -> t p d", p=P)

    ctx = ExitStack()
    with ctx:
        def sem(name):
            return ctx.enter_context(nc.semaphore(name))

        def sb(name, shape, dt=F32, scope=ctx):
            return scope.enter_context(nc.sbuf_tensor(name, shape, dt))

        keep = sb("keep", [P, NT, D])
        w2h = sb("w2h", [P, KT, 2 * D], F32R)
        w2l = sb("w2l", [P, KT, 2 * D], F32R)
        w3ah = sb("w3ah", [P, KT, HID], F32R)
        w3al = sb("w3al", [P, KT, HID], F32R)
        w3bh = sb("w3bh", [P, D], F32R)
        w3bl = sb("w3bl", [P, D], F32R)
        ident = sb("ident", [P, P])
        identr = sb("identr", [P, P], F32R)
        stat = [sb(f"stationary{u}", [P, N], F32R) for u in range(2)]
        ringh = [stat[0][:, c * CH:(c + 1) * CH] for c in range(NCH)]
        ringl = [stat[1][:, c * CH:(c + 1) * CH] for c in range(NCH)]
        xt_h = [sb(f"xt_h{u}", [P, KT, P], F32R) for u in range(2)]
        xt_l = [sb(f"xt_l{u}", [P, KT, P], F32R) for u in range(2)]
        xs = [sb(f"xs{u}", [P, D]) for u in range(2)]
        tmp = sb("tmp", [P, D])
        zb = [sb(f"zb{u}", [P, D]) for u in range(2)]
        xres = [sb(f"xres{u}", [P, D]) for u in range(2)]
        bsum = sb("bsum", [P, D])
        deg = sb("deg", [P, NT])
        dinv = sb("dinv", [P, NT])
        rdeg = sb("rdeg", [P, NT])
        stats = [sb(f"stats{u}", [P, 6]) for u in range(2)]
        mvt = [sb(f"mvt{u}", [P, 2]) for u in range(2)]
        mv = sb("mv", [P, NT, 2])
        sd = sb("sd", [P, NT])
        rstd = sb("rstd", [P, NT])
        bits = sb("bits", [P, NT])
        lowbits = sb("lowbits", [P, 1])
        anylow = sb("anylow", [1, 1], I32)
        eps = sb("eps", [P, 1])
        one = sb("one", [P, 1])

        gat = ExitStack()
        wst_h = sb("wst_h", [P, KT, N], F32R, gat)
        wst_l = sb("wst_l", [P, KT, N], F32R, gat)
        val = sb("val", [P, NT, 2 * D], F32R, gat)
        wht = sb("wht", [P, KT, N], F32, gat)
        xtall_h = sb("xtall_h", [P, KT, N], F32R, gat)
        xtall_l = sb("xtall_l", [P, KT, N], F32R, gat)
        prob = [sb(f"prob{u}", [P, N], F32, gat) for u in range(2)]
        arow = [sb(f"arow{u}", [P, N], F32, gat) for u in range(2)]
        wg_h = sb("wg_h", [P, KT, 2 * D], F32R, gat)
        wg_l = sb("wg_l", [P, KT, 2 * D], F32R, gat)
        whs_h = [sb(f"whs_h{u}", [P, KT, P], F32R, gat) for u in range(2)]
        whs_l = [sb(f"whs_l{u}", [P, KT, P], F32R, gat) for u in range(2)]
        mx = [sb(f"mx{u}", [P, NCH], F32, gat) for u in range(2)]
        nmax = [sb(f"nmax{u}", [P, 1], F32, gat) for u in range(2)]
        rs = [sb(f"rs{u}", [P, NCH], F32, gat) for u in range(2)]
        rsum = [sb(f"rsum{u}", [P, 1], F32, gat) for u in range(2)]
        rinv = [sb(f"rinv{u}", [P, 1], F32, gat) for u in range(2)]
        dplus = sb("dplus", [P, NT], F32, gat)
        dsq = sb("dsq", [P, NT], F32, gat)
        wg_raw = prob[0][:, 0:KT * 2 * D].rearrange("p (k n) -> p k n", k=KT)
        wht_g = prob[1][:, 0:KT * CH].rearrange("p (k n) -> p k n", k=KT)
        wn_raw = arow[0][:, 0:KT * D].rearrange("p (k n) -> p k n", k=KT)
        ws_raw = arow[0][:, KT * D:2 * KT * D].rearrange("p (k n) -> p k n", k=KT)
        w1_raw = arow[0][:, 2 * KT * D:3 * KT * D].rearrange("p (k n) -> p k n", k=KT)
        w3a_raw = arow[0][:, 3 * KT * D:3 * KT * D + KT * HID].rearrange("p (k n) -> p k n", k=KT)
        w3b_raw = arow[0][:, 3 * KT * D + KT * HID:3 * KT * D + KT * HID + D]
        bs_raw = arow[1][:, 0:D]
        gat.close()

        adjt = sb("adjt", [P, NT, N])
        pm = sb("pm", [P, NT, 2 * D], F32R)
        rst = sb("rst", [P, D])
        weight = ExitStack()
        w1h = sb("w1h", [P, KT, D], F32R, weight)
        w1l = sb("w1l", [P, KT, D], F32R, weight)
        weight.close()
        first = ExitStack()
        nat = [sb(f"nat{p}", [P, CH], F32, first) for p in range(2)]
        first.close()
        rin = [sb(f"rin{u}", [P, D]) for u in range(2)]
        bout = sb("bout", [P, D])
        bhid = sb("bhid", [P, HID])

        scores = ctx.enter_context(nc.psum_tensor("scores", [P, N], F32))
        tb = [ctx.enter_context(nc.psum_tensor(f"tb{i}", [P, CH], F32)) for i in range(2)]
        ob0 = ctx.enter_context(nc.psum_tensor("ob0", [P, CH], F32))
        xb0 = ctx.enter_context(nc.psum_tensor("xb0", [P, CH], F32))
        ob = [ob0, scores[:, 0:CH]]
        xb = [xb0, scores[:, CH:2 * CH]]
        jb = [scores[:, 2 * CH:3 * CH], scores[:, 3 * CH:4 * CH]]

        passed = {e: sem(f"waits_passed_{e}") for e in ("sync", "gpsimd", "scalar", "vector")}
        s_id = sem("identity_ready")
        s_idr = sem("identity_r_ready")
        s_cst = sem("constants_ready")
        s_x = [sem(f"features_loaded_{g}") for g in range(NCH)]
        s_wraw = sem("weights_loaded")
        s_bias = sem("self_biases_loaded")
        s_bsum = sem("self_bias_sum_ready")
        s_wh = sem("weights_hi_ready")
        s_wl = sem("weights_lo_ready")
        s_w2t = sem("block2_weights_transposed")
        s_w2h = sem("block2_weights_hi_ready")
        s_w2l = sem("block2_weights_lo_ready")
        s_x0t = sem("input_transposed")
        s_x0h = sem("input_transposed_hi")
        s_x0l = sem("input_transposed_lo")
        s_wgraw = [sem(f"gat_weight_loaded_{l}") for l in range(LAYERS)]
        s_wgh = [sem(f"gat_weight_hi_{l}") for l in range(LAYERS)]
        s_wgl = [sem(f"gat_weight_lo_{l}") for l in range(LAYERS)]

        sems, counted = {}, {}

        def counter(name, total):
            if name not in sems:
                sems[name], counted[name] = sem(name), 0
            signal = Signal(sems[name], counted[name])
            counted[name] += total
            return signal

        class Gat:

            def __init__(self, l):
                def s(name, total):
                    return counter(f"gat_{name}", total)
                self.prod = s("projection_done", 4 * NCH + 1)
                self.staged = s("wht_staged", KT * NCH + 1)
                self.kept = s("wht_kept", NCH + 1)
                self.wsh = s("wst_hi", KT * NCH)
                self.wsl = s("wst_lo", KT * NCH + 1)
                self.vt = s("values_transposed", 2 * NCH)
                self.vh = s("values_hi", 2 * NCH)
                self.vl = s("values_lo", 2 * NCH + 1)
                self.adj = [s(f"adjacency_loaded_{u}", 8 * NT) for u in range(2)]
                self.xres = [s(f"residual_loaded_{u}", 8 * NT * (l == LAYERS - 1)) for u in range(2)]
                self.qh = s("query_hi", NT)
                self.q = s("query_ready", NT)
                self.sc = s("scores_ready", 4 * NT)
                self.mx = s("chunk_max", 4 * NT)
                self.nmax = s("row_max", NT)
                self.ex = s("exp_done", 4 * NT)
                self.msk = s("masked", 4 * NT)
                self.low = s("low_bits_masked", NT * (l == 1))
                self.deg = s("degree_or_low_bits", NT)
                self.tr = s("probs_transposed", 4 * NT)
                self.ah = s("probs_hi", 4 * NT)
                self.al = s("probs_lo", 4 * NT)
                self.av = s("values_summed", 4 * NT)
                self.rsum = s("row_sum", NT)
                self.rinv = s("row_sum_inverse", NT)
                self.tmp = s("lo_half_scaled", NT)
                self.z = s("attention_scaled", NT)
                self.zx = s("residual_added", NT)
                self.new = s("rows_ready", NT)
                self.rows = s("rows_kept", NT)
                self.stat = s("statistics", NT * (l == LAYERS - 1))
                self.aggr = s("tile_mean_variance", NT * (l == LAYERS - 1))
                self.mv = s("mean_variance", NT * (l == LAYERS - 1))
                self.xtr = s("rows_transposed", NT * (l < LAYERS - 1))
                self.xth = s("rows_transposed_hi", NT * (l < LAYERS - 1))
                self.xtl = s("rows_transposed_lo", NT * (l < LAYERS - 1))

        G = [Gat(l) for l in range(LAYERS)]

        s_bits = sem("low_bits_ready")
        s_any = sem("low_bits_summed")
        s_flag = sem("low_bits_flag_ready")
        s_dpl = sem("degree_plus_eps")
        s_dsq = sem("degree_root")
        s_dinv = sem("degree_inverses")
        s_sd0 = sem("norm0_deviation")
        s_rstd0 = sem("norm0_inverse")
        n_new = sem("norm0_rows")
        n_out = [sem(f"norm0_rows_stored_{u}") for u in range(2)]
        n_xtr = sem("norm0_transposed")
        n_xth = sem("norm0_hi")
        n_xtl = sem("norm0_lo")
        n_prj = sem("block1_projection")
        n_ph = sem("norm0_moving_hi")
        n_pl = sem("norm0_moving_lo")

        class Agg:

            def __init__(self, name, width, proj, norm, load_self, last):
                def s(what, total):
                    return counter(f"agg_{what}", total)
                c = name == "block1"
                self.name, self.w, self.proj, self.norm = name, width, proj, norm
                self.load_self, self.last = load_self, last
                self.nat = [s(f"adjacency_loaded_{p}", 32 * NT * c) for p in range(2)]
                self.xres = [s(f"residual_loaded_{u}", 8 * NT * norm) for u in range(2)]
                self.rin = [s(f"self_term_loaded_{u}", 8 * NT * load_self) for u in range(2)]
                self.tr = s("adjacency_transposed", 4 * NT * c)
                self.kept = s("adjacency_kept", 4 * NT * c)
                self.front = s("front_half_ready", NT)
                self.back = s("back_half_ready", NT)
                self.ah = s("adjacency_hi", 4 * NT)
                self.al = s("adjacency_lo", 4 * NT)
                self.mm = s("sums_done", 4 * NT)
                self.tmp = s("lo_half_ready", NT)
                self.r = s("sum_ready", NT)
                self.rb = s("term_added", NT * (not c))
                self.y = s("residual_added", NT * norm)
                self.stat = s("statistics", NT * norm)
                self.mv = s("mean_variance", NT * norm)
                self.sd = s("deviation", NT * norm)
                self.rstd = s("deviation_inverse", NT * norm)
                self.new = s("rows_ready", NT)
                self.out = [s(f"rows_stored_{u}", 8 * NT * norm) for u in range(2)]
                self.xtr = s("rows_transposed", NT * bool(proj))
                self.xth = s("rows_hi", NT * bool(proj))
                self.xtl = s("rows_lo", NT * bool(proj))
                self.prj = s("projection_done", NT * bool(proj))
                self.pk = s("projection_kept", NT * bool(proj))
                self.rt = s("self_term_ready", NT * c)
                self.rout = s("self_term_stored", 16 * NT * c)
                self.ph = s("moving_hi", NCH * (not c))
                self.pl = s("moving_lo", NCH * (not c))

        C = Agg("block1", D, (w2h, w2l, KT, 2 * D), True, False, False)
        Dg = Agg("block2", D, (w3ah, w3al, KT, HID), True, True, False)
        E = Agg("block3a", HID, (w3bh, w3bl, 1, D), False, False, False)
        F = Agg("block3b", D, None, True, False, True)
        aggs = [C, Dg, E, F]
        s_bt = sem("block3_biases_loaded")

        block = ctx.enter_context(nc.Block())

        @block.sync
        def _(sp):
            per_k = "(k p) n -> p k n"
            for g in range(NCH):
                sp.dma_start(keep[:, g * TPC:(g + 1) * TPC, :], x_all[:, g * TPC:(g + 1) * TPC, :]).then_inc(s_x[g], 16)
                if g == 0:
                    sp.dma_start(wg_raw, w_gat[0].rearrange(per_k, p=P)).then_inc(s_wgraw[0], 16)
            sp.dma_start(wn_raw, w_neigh.rearrange(per_k, p=P)).then_inc(s_wraw, 16)
            sp.dma_start(ws_raw, w_self.rearrange(per_k, p=P)).then_inc(s_wraw, 16)
            sp.dma_start(w1_raw, w_gcn.rearrange(per_k, p=P)).then_inc(s_wraw, 16)
            sp.dma_start(w3a_raw, w1.rearrange(per_k, p=P)).then_inc(s_wraw, 16)
            sp.dma_start(w3b_raw, w2).then_inc(s_wraw, 16)
            sp.dma_start(bsum[:, :], b_neigh[None, :].to_broadcast([P, D])).then_inc(s_bias, 16)
            sp.dma_start(bs_raw, b_self[None, :].to_broadcast([P, D])).then_inc(s_bias, 16)

            for l, g in enumerate(G):
                if l:
                    ge(sp, G[l - 1].tr, 4 * NT)
                    sp.dma_start(wg_raw, w_gat[l].rearrange(per_k, p=P)).then_inc(s_wgraw[l], 16)

                def load(b, u):
                    t = b + u
                    ge(sp, g.msk, 4 * t - 4)
                    if not isinstance(t, int):
                        alone(sp, passed["sync"])
                    ge(sp, g.deg, t - 1)
                    if not isinstance(t, int):
                        alone(sp, passed["sync"])
                    sp.dma_start(arow[u][:, :], adj_rows[t]).then_inc(g.adj[u].sem, 16)
                    if l == LAYERS - 1:
                        ge(sp, g.rows, t - 1)
                        sp.dma_start(xres[u][:, :], x_rows[t]).then_inc(g.xres[u].sem, 16)

                if l == 0:
                    sp.wait_ge(s_wl, 3)
                    sp.wait_ge(s_w2t, 2)
                    sp.wait_ge(s_bsum, 1)
                else:
                    ge(sp, G[l - 1].msk, 4 * NT)
                    ge(sp, G[l - 1].deg, NT)
                load(0, 0)
                load(0, 1)
                with sp.Fori(1, NT // 2) as half:
                    b = 2 * half
                    load(b, 0)
                    load(b, 1)

            def store0(b, u):
                sp.wait_ge(n_new, b + u + 1)
                sp.dma_start(xs_rows[b + u], xs[u][:, :]).then_inc(n_out[u], 16)

            with sp.Fori(0, NT // 2) as half:
                b = 2 * half
                store0(b, 0)
                store0(b, 1)
            for u in range(2):
                sp.wait_ge(n_out[u], 8 * NT)

            for k, a in enumerate(aggs):
                prev = aggs[k - 1] if k else None
                if a.load_self:
                    ge(sp, prev.rout, 16 * NT)
                if k == 1:
                    ge(sp, C.tr, 4 * NT)
                    sp.dma_start(bout[:, :], b2[None, :].to_broadcast([P, D])).then_inc(s_bt, 16)
                    sp.dma_start(bhid[:, :], b1[None, :].to_broadcast([P, HID])).then_inc(s_bt, 16)

                def load_nat(t, c):
                    n = 4 * t + c
                    ge(sp, a.tr, n - 1)
                    sp.dma_start(nat[c % 2][:, :], adj_rows[t][:, c * CH:(c + 1) * CH]).then_inc(a.nat[c % 2].sem, 16)

                def load_res(b, u):
                    t = b + u
                    if a.norm:
                        ge(sp, a.y, t - 1)
                        sp.dma_start(xres[u][:, :], xs_rows[t]).then_inc(a.xres[u].sem, 16)
                    if a.load_self:
                        sp.dma_start(rin[u][:, :], rs_rows[t]).then_inc(a.rin[u].sem, 16)

                def store(b, u):
                    t = b + u
                    if a.norm:
                        ge(sp, a.new, t + 1)
                        dst = out_rows if a.last else xs_rows
                        sp.dma_start(dst[t], xs[u][:, :]).then_inc(a.out[u].sem, 16)
                    if a is C:
                        ge(sp, a.rt, t + 1)
                        sp.dma_start(rs_rows[t], rst[:, :]).then_inc(a.rout.sem, 16)

                if a is C:
                    sp.wait_ge(n_pl, NT)
                    for c in range(NCH):
                        load_nat(0, c)
                if k and a.norm:
                    src = aggs[k - 1] if aggs[k - 1].norm else aggs[k - 2]
                    for u in range(2):
                        ge(sp, src.out[u], 8 * NT)

                def slot(b, u, nxt=True, fin=True):
                    load_res(b, u)
                    if a is C and nxt:
                        for c in range(NCH):
                            load_nat(b + u + 1, c)
                    if fin:
                        store(*before(b, u, 2))

                slot(0, 0, fin=False)
                slot(0, 1, fin=False)
                with sp.Fori(1, NT // 2 - 1) as half:
                    b = 2 * half
                    slot(b, 0)
                    slot(b, 1)
                slot(NT - 2, 0)
                slot(NT - 2, 1, nxt=False)
                store(NT - 2, 0)
                store(NT - 2, 1)
            for u in range(2):
                ge(sp, F.out[u], 8 * NT)
            ge(sp, C.rout, 16 * NT)

        @block.gpsimd
        def _(pool):
            nc.gpsimd.memset(ident[:, :], 0.0).then_inc(s_id, 1)
            pool.wait_ge(s_id, 1)
            nc.gpsimd.affine_select(out=ident[:, :], in_=ident[:, :], compare_op=ALU.not_equal, fill=1.0, base=0,
                                    pattern=[[-1, P]], channel_multiplier=1).then_inc(s_id, 1)
            nc.gpsimd.memset(eps[:, :], LN_EPS).then_inc(s_cst, 1)
            nc.gpsimd.memset(one[:, :], 1.0).then_inc(s_cst, 1)
            pool.wait_ge(s_bias, 32)
            nc.gpsimd.tensor_tensor(bsum[:, :], bsum[:, :], bs_raw, ALU.add).then_inc(s_bsum, 1)

            for l, g in enumerate(G):
                def query(b, u):
                    t = b + u
                    ge(pool, g.sc, 4 * t - 4)
                    if not isinstance(t, int):
                        alone(pool, passed["gpsimd"])
                    src = wht[:, :, bass.ts(t, P)]
                    nc.gpsimd.tensor_copy(whs_h[u][:, :, :], src).then_inc(g.qh.sem, 1)
                    ge(pool, g.qh, t + 1)
                    alone(pool, passed["gpsimd"])
                    nc.gpsimd.tensor_tensor(whs_l[u][:, :, :], src, whs_h[u][:, :, :].bitcast(F32),
                                            ALU.subtract).then_inc(g.q.sem, 1)

                def mask(b, u):
                    t = b + u
                    ge(pool, g.adj[u], 8 * b + 16)
                    for c in range(NCH):
                        ge(pool, g.ex, 4 * t + c + 1)
                        cs = slice(c * CH, (c + 1) * CH)
                        nc.gpsimd.tensor_tensor(prob[u][:, cs], prob[u][:, cs], arow[u][:, cs],
                                                ALU.mult).then_inc(g.msk.sem, 1)

                def residual(b, u):
                    t = b + u
                    ge(pool, g.z, t + 1)
                    alone(pool, passed["gpsimd"])
                    nc.gpsimd.tensor_tensor(zb[u][:, :], zb[u][:, :], keep[:, t, :], ALU.add).then_inc(g.zx.sem, 1)

                def keep_rows(b, u):
                    if l < LAYERS - 1:
                        ge(pool, g.new, b + u + 1)
                        alone(pool, passed["gpsimd"])
                        nc.gpsimd.tensor_copy(keep[:, b + u, :], xs[u][:, :]).then_inc(g.rows.sem, 1)

                def slot(b, u, main=True, nxt=True, av=True, fin=True):
                    if fin:
                        keep_rows(*before(b, u, 2))
                    if nxt:
                        query(*after(b, u))
                    if main:
                        mask(b, u)
                    if av:
                        residual(*before(b, u))

                ge(pool, g.kept, NCH + 1)
                query(0, 0)
                slot(0, 0, av=False, fin=False)
                slot(0, 1, fin=False)
                with pool.Fori(1, NT // 2 - 1) as half:
                    b = 2 * half
                    slot(b, 0)
                    slot(b, 1)
                slot(NT - 2, 0)
                slot(NT - 2, 1, nxt=False)
                slot(NT, 0, main=False, nxt=False)
                slot(NT, 1, main=False, nxt=False, av=False)

            def term(a, b, u):
                t = b + u
                ge(pool, a.r, t + 1)
                if a is Dg:
                    ge(pool, a.rin[u], 8 * b + 16)
                    nc.gpsimd.tensor_tensor(zb[u][:, :], zb[u][:, :], rin[u][:, :], ALU.add).then_inc(a.rb.sem, 1)
                elif a is E:
                    nc.gpsimd.tensor_tensor(zb[u][:, 0:HID], zb[u][:, 0:HID], bhid[:, :], ALU.add).then_inc(a.rb.sem, 1)
                else:
                    nc.gpsimd.tensor_tensor(zb[u][:, :], zb[u][:, :], bout[:, :], ALU.add).then_inc(a.rb.sem, 1)

            pool.wait_ge(s_bt, 32)
            for a in (Dg, E, F):
                with pool.Fori(0, NT // 2) as half:
                    b = 2 * half
                    term(a, b, 0)
                    term(a, b, 1)

        @block.scalar
        def _(act):
            def copy(dst, src, **kw):
                return nc.scalar.activation(dst, src, ACT.Copy, **kw)

            act.wait_ge(s_wgraw[0], 16)
            copy(wg_h[:, :, :], wg_raw).then_inc(s_wgh[0], 1)
            for g in range(NCH):
                for k in range(KT):
                    act.wait_ge(s_x0t, KT * g + k + 1)
                    copy(xtall_h[:, k, g * CH:(g + 1) * CH], tb[k][:, :]).then_inc(s_x0h, 1)
            act.wait_ge(s_wraw, 5 * 16)
            copy(w1h[:, :, :], w1_raw).then_inc(s_wh, 1)
            copy(w3ah[:, :, :], w3a_raw).then_inc(s_wh, 1)
            copy(w3bh[:, :], w3b_raw).then_inc(s_wh, 1)
            for k in range(KT):
                act.wait_ge(s_w2t, k + 1)
                copy(w2h[:, k, :], tb[k][:, :]).then_inc(s_w2h, 1)

            for l, g in enumerate(G):
                if l:
                    act.wait_ge(s_wgraw[l], 16)
                    ge(act, G[l - 1].prod, 4 * NCH + 1)
                    copy(wg_h[:, :, :], wg_raw).then_inc(s_wgh[l], 1)
                    ge(act, G[l - 1].tr, 4 * NT)
                act.sem_inc(g.kept.sem, 1)
                with act.Fori(0, NCH) as i:
                    ge(act, g.kept, i + 1)
                    for o in range(KT):
                        ge(act, g.prod, 4 * i + o + 2)
                        copy(wht_g[:, o, :], scores[:, o * CH:(o + 1) * CH]).then_inc(g.staged.sem, 1)
                    for o in range(KT):
                        ge(act, g.prod, 4 * i + KT + o + 2)
                        alone(act, passed["scalar"])
                        copy(wst_h[:, o, bass.ts(i, CH)], scores[:, (KT + o) * CH:(KT + o + 1) * CH])\
                            .then_inc(g.wsh.sem, 1)
                    for h in range(2):
                        ge(act, g.vt, 2 * i + h + 1)
                        alone(act, passed["scalar"])
                        copy(val[:, bass.ds(i * TPC + 2 * h, 2), 0:D],
                             tb[h][:, :].rearrange("p (a d) -> p a d", a=2)).then_inc(g.vh.sem, 1)

                def hi(b, u, c):
                    n = 4 * (b + u) + c
                    ge(act, g.tr, n + 1)
                    ge(act, g.av, n - 3)
                    copy(ringh[c], tb[c % 2][:, :]).then_inc(g.ah.sem, 1)

                def exp(b, u, c):
                    t = b + u
                    if c == 0:
                        ge(act, g.nmax, t + 1)
                        ge(act, g.tr, 4 * t - 4)
                        ge(act, g.rsum, t - 1)
                    cs = slice(c * CH, (c + 1) * CH)
                    nc.scalar.activation(prob[u][:, cs], scores[:, cs], ACT.Exp, bias=nmax[u][:, :],
                                         accum_out=rs[u][:, c:c + 1]).then_inc(g.ex.sem, 1)

                def lo_half(b, u):
                    t = b + u
                    ge(act, g.av, 4 * t + 4)
                    ge(act, g.rinv, t + 1)
                    ge(act, g.z, t)
                    copy(tmp[:, :], ob0[:, D:2 * D], scale=rinv[u][:, :]).then_inc(g.tmp.sem, 1)

                def rows_hi(b, u):
                    if l < LAYERS - 1:
                        t = b + u
                        ge(act, g.xtr, t + 1)
                        alone(act, passed["scalar"])
                        copy(xtall_h[:, :, bass.ts(t, P)],
                             xb0[:, 0:D].rearrange("p (k i) -> p k i", k=KT)).then_inc(g.xth.sem, 1)

                def slot(b, u, main=True, av=True, fin=True):
                    p = before(b, u)
                    if av:
                        hi(*p, 0)
                        hi(*p, 1)
                    if fin:
                        rows_hi(*before(b, u, 2))
                    if av:
                        hi(*p, 2)
                    if main:
                        exp(b, u, 0)
                    if av:
                        hi(*p, 3)
                    if main:
                        exp(b, u, 1)
                        exp(b, u, 2)
                        exp(b, u, 3)
                    if av:
                        lo_half(*p)

                slot(0, 0, av=False, fin=False)
                slot(0, 1, fin=False)
                slot(2, 0)
                slot(2, 1)
                with act.Fori(2, NT // 2) as half:
                    b = 2 * half
                    slot(b, 0)
                    slot(b, 1)
                slot(NT, 0, main=False)
                slot(NT, 1, main=False, av=False)

            act.wait_ge(s_cst, 2)
            ge(act, G[0].deg, NT)
            nc.scalar.activation(dsq[:, :], deg[:, :], ACT.Sqrt, bias=one[:, :]).then_inc(s_dsq, 1)
            ge(act, G[-1].mv, NT)
            nc.scalar.activation(sd[:, :], mv[:, :, 1], ACT.Sqrt, bias=eps[:, :]).then_inc(s_sd0, 1)

            def n_hi(b, u):
                t = b + u
                act.wait_ge(n_xtr, t + 1)
                ge(act, n_prj, t - 1)
                copy(xt_h[u][:, :, :], xb[u][:, 0:D].rearrange("p (k i) -> p k i", k=KT)).then_inc(n_xth, 1)

            def n_moving(b, u):
                t = b + u
                act.wait_ge(n_prj, t + 1)
                alone(act, passed["scalar"])
                copy(pm[:, t, 0:D], jb[u][:, 0:D], scale=dinv[:, bass.ds(t, 1)]).then_inc(n_ph, 1)

            act.wait_ge(s_dinv, 2)
            ge(act, G[-1].av, 4 * NT)
            n_hi(0, 0)
            n_hi(0, 1)
            n_moving(0, 0)
            n_hi(2, 0)
            n_moving(0, 1)
            n_hi(2, 1)
            n_moving(2, 0)
            with act.Fori(2, NT // 2) as half:
                b = 2 * half
                n_hi(b, 0)
                n_moving(b - 2, 1)
                n_hi(b, 1)
                n_moving(b, 0)
            n_moving(NT - 2, 1)

            def parts(k, a):
                w, prev = a.w, aggs[k - 1] if k else None

                def split(q):
                    js = slice(q * TPC, (q + 1) * TPC)
                    ge(act, prev.mm, 4 * NT)
                    ge(act, prev.pk, (q + 1) * TPC)
                    copy(pm[:, js, 0:w], keep[:, js, 0:w]).then_inc(a.ph.sem, 1)

                def keep_adj(t, c):
                    ge(act, a.tr, 4 * t + c + 1)
                    alone(act, passed["scalar"])
                    copy(adjt[:, t, c * CH:(c + 1) * CH], tb[c % 2][:, :]).then_inc(a.kept.sem, 1)

                def rows_hi(b, u):
                    t = b + u
                    if a.proj:
                        kt = a.proj[2]
                        ge(act, a.xtr, t + 1)
                        ge(act, a.prj, t - 1)
                        copy(xt_h[u][:, 0:kt, :], xb[u][:, 0:kt * P].rearrange("p (k i) -> p k i", k=kt))\
                            .then_inc(a.xth.sem, 1)

                def lo_half(b, u):
                    t = b + u
                    ge(act, a.mm, 4 * t + 4)
                    ge(act, a.r, t)
                    alone(act, passed["scalar"])
                    kw = {}
                    if a is C:
                        kw = {"scale": dinv[:, bass.ds(t, 1)]}
                    elif a is Dg:
                        kw = {"scale": rdeg[:, bass.ds(t, 1)]}
                    copy(tmp[:, 0:w], ob[u][:, w:2 * w], **kw).then_inc(a.tmp.sem, 1)

                def deviation(b, u):
                    t = b + u
                    if a.norm:
                        ge(act, a.mv, t + 1)
                        nc.scalar.activation(sd[:, u:u + 1], mv[:, u, 1:2], ACT.Sqrt, bias=eps[:, :])\
                            .then_inc(a.sd.sem, 1)

                def keep_proj(b, u):
                    t = b + u
                    if a.proj:
                        width = min(D, a.proj[3])
                        ge(act, a.prj, t + 1)
                        alone(act, passed["scalar"])
                        copy(keep[:, t, 0:width], jb[u][:, 0:width]).then_inc(a.pk.sem, 1)

                return split, keep_adj, rows_hi, lo_half, deviation, keep_proj

            def general():
                for k, a in enumerate(aggs):
                    split, keep_adj, rows_hi, lo_half, deviation, keep_proj = parts(k, a)

                    def hi(t, c):
                        n = 4 * t + c
                        if a is C:
                            ge(act, a.kept, n + 1)
                        ge(act, a.mm, n - 3)
                        alone(act, passed["scalar"])
                        copy(ringh[c], adjt[:, t, c * CH:(c + 1) * CH]).then_inc(a.ah.sem, 1)

                    def slot(b, u, main=True, nxt=True, ep=True, fin=True):
                        t = b + u
                        p, pp = before(b, u), before(b, u, 2)
                        fresh = a is C and nxt
                        if fin:
                            rows_hi(*pp)
                        if ep:
                            lo_half(*p)
                        if main:
                            hi(t, 2)
                        if fresh:
                            keep_adj(t + 1, 0)
                        if ep:
                            deviation(*p)
                        if main:
                            hi(t, 3)
                        if fresh:
                            keep_adj(t + 1, 1)
                        if fin:
                            keep_proj(*pp)
                        if nxt:
                            hi(t + 1, 0)
                        if fresh:
                            keep_adj(t + 1, 2)
                        if nxt:
                            hi(t + 1, 1)
                        if fresh:
                            keep_adj(t + 1, 3)

                    if k:
                        for q in range(NCH):
                            split(q)
                    else:
                        for c in range(NCH):
                            keep_adj(0, c)
                    hi(0, 0)
                    hi(0, 1)
                    slot(0, 0, ep=False, fin=False)
                    slot(0, 1, fin=False)
                    slot(2, 0)
                    slot(2, 1)
                    with act.Fori(2, NT // 2 - 1) as half:
                        slot(2 * half, 0)
                        slot(2 * half, 1)
                    slot(NT - 2, 0)
                    slot(NT - 2, 1, nxt=False)
                    slot(NT, 0, main=False, nxt=False)
                    slot(NT, 1, main=False, nxt=False, ep=False)

            def exact():
                def front(k, b, u):
                    a, t = aggs[k], b + u
                    if k and isinstance(t, int) and t < 2:
                        ge(act, aggs[k - 1].mm, 4 * (NT - 2 + t) + 2)
                    if a is C:
                        ge(act, a.kept, 4 * t + 2)
                    ge(act, a.mm, 4 * t - 6)
                    alone(act, passed["scalar"])
                    copy(stat[u][:, 0:N // 2], adjt[:, t, 0:N // 2]).then_inc(a.front.sem, 1)

                for k, a in enumerate(aggs):
                    _, keep_adj, rows_hi, lo_half, deviation, keep_proj = parts(k, a)

                    def slot(b, u, nxt=True, ep=True, fin=True):
                        p, pp, n = before(b, u), before(b, u, 2), after(b, u)
                        if fin:
                            rows_hi(*pp)
                        if ep:
                            lo_half(*p)
                        if nxt and a is not C:
                            front(k, *n)
                        if nxt and a is C:
                            keep_adj(b + u + 1, 0)
                        if ep:
                            deviation(*p)
                        if nxt and a is C:
                            keep_adj(b + u + 1, 1)
                        if fin:
                            keep_proj(*pp)
                        if nxt and a is C:
                            keep_adj(b + u + 1, 2)
                            front(k, *n)
                            keep_adj(b + u + 1, 3)

                    if k == 0:
                        for c in range(NCH):
                            keep_adj(0, c)
                        front(k, 0, 0)
                        slot(0, 0, ep=False, fin=False)
                    slot(0, 1, fin=False)
                    slot(2, 0)
                    slot(2, 1)
                    with act.Fori(2, NT // 2 - 1) as half:
                        slot(2 * half, 0)
                        slot(2 * half, 1)
                    slot(NT - 2, 0)
                    slot(NT - 2, 1, nxt=False)
                    if a.last:
                        lo_half(NT - 2, 1)
                        deviation(NT - 2, 1)
                        continue
                    split = parts(k + 1, aggs[k + 1])[0]
                    rows_hi(NT - 2, 0)
                    front(k + 1, 0, 0)
                    lo_half(NT - 2, 1)
                    front(k + 1, 0, 1)
                    split(0)
                    deviation(NT - 2, 1)
                    keep_proj(NT - 2, 0)
                    split(1)
                    rows_hi(NT - 2, 1)
                    split(2)
                    keep_proj(NT - 2, 1)
                    split(3)

            act.wait_ge(s_flag, 1)
            low = act.value_load(anylow[0:1, 0:1])
            with act.If(low > 0):
                general()
            with act.Else():
                exact()

        @block.vector
        def _(dve):
            dve.wait_ge(s_id, 2)
            nc.vector.tensor_copy(identr[:, :], ident[:, :]).then_inc(s_idr, 1)

            def rest(dst, v, h):
                return nc.vector.tensor_tensor(dst, v, h.bitcast(F32), ALU.subtract)

            dve.wait_ge(s_wgh[0], 1)
            rest(wg_l[:, :, :], wg_raw, wg_h[:, :, :]).then_inc(s_wgl[0], 1)
            for g in range(NCH):
                for k in range(KT):
                    dve.wait_ge(s_x0h, KT * g + k + 1)
                    gs = slice(g * CH, (g + 1) * CH)
                    rest(xtall_l[:, k, gs], tb[k][:, :], xtall_h[:, k, gs]).then_inc(s_x0l, 1)
            dve.wait_ge(s_wh, 3)
            rest(w1l[:, :, :], w1_raw, w1h[:, :, :]).then_inc(s_wl, 1)
            rest(w3al[:, :, :], w3a_raw, w3ah[:, :, :]).then_inc(s_wl, 1)
            rest(w3bl[:, :], w3b_raw, w3bh[:, :]).then_inc(s_wl, 1)
            for k in range(KT):
                dve.wait_ge(s_w2h, k + 1)
                rest(w2l[:, k, :], tb[k][:, :], w2h[:, k, :]).then_inc(s_w2l, 1)

            for l, g in enumerate(G):
                if l:
                    dve.wait_ge(s_wgh[l], 1)
                    rest(wg_l[:, :, :], wg_raw, wg_h[:, :, :]).then_inc(s_wgl[l], 1)
                with dve.Fori(0, NCH) as i:
                    ge(dve, g.staged, KT * i + KT + 1)
                    nc.vector.tensor_copy(wht[:, :, bass.ts(i, CH)], wht_g).then_inc(g.kept.sem, 1)
                    for o in range(KT):
                        ge(dve, g.wsh, KT * i + o + 1)
                        rest(wst_l[:, o, bass.ts(i, CH)], scores[:, (KT + o) * CH:(KT + o + 1) * CH],
                             wst_h[:, o, bass.ts(i, CH)]).then_inc(g.wsl.sem, 1)
                    for h in range(2):
                        ge(dve, g.vh, 2 * i + h + 1)
                        two = bass.ds(i * TPC + 2 * h, 2)
                        rest(val[:, two, D:2 * D], tb[h][:, :].rearrange("p (a d) -> p a d", a=2),
                             val[:, two, 0:D]).then_inc(g.vl.sem, 1)

                def chunk_max(b, u, c):
                    n = 4 * (b + u) + c
                    ge(dve, g.sc, n + 1)
                    if c == 0:
                        ge(dve, g.nmax, b + u - 1)
                    nc.vector.reduce_max(mx[u][:, c:c + 1], scores[:, c * CH:(c + 1) * CH], AX.X)\
                        .then_inc(g.mx.sem, 1)

                def row_max(b, u):
                    t = b + u
                    ge(dve, g.mx, 4 * t + 4)
                    ge(dve, g.ex, 4 * t - 4)
                    nc.vector.reduce_max(nmax[u][:, :], mx[u][:, :], AX.X, negate=True).then_inc(g.nmax.sem, 1)

                def lo(b, u, c):
                    n = 4 * (b + u) + c
                    ge(dve, g.ah, n + 1)
                    ge(dve, g.av, n - 3)
                    rest(ringl[c], tb[c % 2][:, :], ringh[c]).then_inc(g.al.sem, 1)

                def row_sum(b, u):
                    t = b + u
                    ge(dve, g.ex, 4 * t + 4)
                    nc.vector.reduce_sum(rsum[u][:, :], rs[u][:, :], AX.X).then_inc(g.rsum.sem, 1)
                    ge(dve, g.rsum, t + 1)
                    ge(dve, g.tmp, t - 1)
                    nc.vector.reciprocal(rinv[u][:, :], rsum[u][:, :]).then_inc(g.rinv.sem, 1)

                def degree(b, u):
                    if l == 0:
                        t = b + u
                        ge(dve, g.adj[u], 8 * b + 16)
                        nc.vector.reduce_sum(deg[:, bass.ds(t, 1)], arow[u][:, :], AX.X).then_inc(g.deg.sem, 1)

                def low_bits(b, u):
                    if l == 1:
                        t = b + u
                        ge(dve, g.msk, 4 * t + 4)
                        raw = arow[u][:, :].bitcast(I32)
                        nc.vector.tensor_scalar(raw, raw, LO_BITS, None, ALU.bitwise_and).then_inc(g.low.sem, 1)
                        ge(dve, g.low, t + 1)
                        nc.vector.tensor_reduce(bits[:, bass.ds(t, 1)], raw, AX.X, ALU.max).then_inc(g.deg.sem, 1)

                def scaled(b, u):
                    t = b + u
                    ge(dve, g.tmp, t + 1)
                    ge(dve, g.rinv, t + 1)
                    ge(dve, g.new, t - 1)
                    nc.vector.scalar_tensor_tensor(zb[u][:, :], ob0[:, 0:D], rinv[u][:, :], tmp[:, :],
                                                   ALU.mult, ALU.add).then_inc(g.z.sem, 1)

                def finish(b, u):
                    t = b + u
                    ge(dve, g.zx, t + 1)
                    ge(dve, g.rows, t - 1)
                    if l < LAYERS - 1:
                        ge(dve, g.xtr, t - 1)
                    nc.vector.scalar_tensor_tensor(xs[u][:, :], zb[u][:, :], SLOPE, zb[u][:, :],
                                                   ALU.mult, ALU.max).then_inc(g.new.sem, 1)

                def finish2(b, u):
                    t = b + u
                    ge(dve, g.new, t + 1)
                    ge(dve, g.xres[u], 8 * b + 16)
                    nc.vector.tensor_tensor(keep[:, t, :], xs[u][:, :], xres[u][:, :], ALU.add)\
                        .then_inc(g.rows.sem, 1)

                def finish3(b, u):
                    t = b + u
                    ge(dve, g.rows, t + 1)
                    ge(dve, g.aggr, t - 1)
                    alone(dve, passed["vector"])
                    nc.vector.bn_stats(stats[u][:, :], keep[:, t, :]).then_inc(g.stat.sem, 1)

                def finish4(b, u):
                    t = b + u
                    ge(dve, g.stat, t + 1)
                    ge(dve, g.mv, t - 1)
                    alone(dve, passed["vector"])
                    nc.vector.bn_aggr(mvt[u][:, :], stats[u][:, :]).then_inc(g.aggr.sem, 1)

                def finish5(b, u):
                    t = b + u
                    ge(dve, g.aggr, t + 1)
                    nc.vector.tensor_copy(mv[:, t, :], mvt[u][:, :]).then_inc(g.mv.sem, 1)

                def rows_lo(b, u):
                    if l < LAYERS - 1:
                        t = b + u
                        ge(dve, g.xth, t + 1)
                        cols = bass.ts(t, P)
                        rest(xtall_l[:, :, cols], xb0[:, 0:D].rearrange("p (k i) -> p k i", k=KT),
                             xtall_h[:, :, cols]).then_inc(g.xtl.sem, 1)

                def slot(b, u, main=True, av=True, fin=True):
                    p, pp = before(b, u), before(b, u, 2)
                    norm = fin and l == LAYERS - 1
                    if main:
                        chunk_max(b, u, 0)
                    if av:
                        lo(*p, 0)
                        lo(*p, 1)
                    if fin:
                        finish(*pp)
                    if main:
                        chunk_max(b, u, 1)
                    if norm:
                        finish2(*pp)
                    if main:
                        chunk_max(b, u, 2)
                    if fin:
                        rows_lo(*pp)
                    if norm:
                        finish3(*pp)
                    if main:
                        chunk_max(b, u, 3)
                        row_max(b, u)
                    if av:
                        lo(*p, 2)
                    if norm:
                        finish4(*pp)
                    if av:
                        lo(*p, 3)
                    if norm:
                        finish5(*pp)
                    if av:
                        row_sum(*p)
                    if main:
                        degree(b, u)
                    if av:
                        low_bits(*p)
                        scaled(*p)

                slot(0, 0, av=False, fin=False)
                slot(0, 1, fin=False)
                slot(2, 0)
                slot(2, 1)
                with dve.Fori(2, NT // 2) as half:
                    b = 2 * half
                    slot(b, 0)
                    slot(b, 1)
                slot(NT, 0, main=False)
                slot(NT, 1, main=False, av=False)

            ge(dve, G[1].deg, NT)
            nc.vector.tensor_reduce(lowbits[:, :], bits[:, :], AX.X, ALU.max).then_inc(s_bits, 1)
            nc.vector.tensor_scalar(dplus[:, :], deg[:, :], DEG_EPS, None, ALU.add).then_inc(s_dpl, 1)
            dve.wait_ge(s_dpl, 1)
            nc.vector.reciprocal(rdeg[:, :], dplus[:, :]).then_inc(s_dinv, 1)
            dve.wait_ge(s_dsq, 1)
            nc.vector.reciprocal(dinv[:, :], dsq[:, :]).then_inc(s_dinv, 1)
            dve.wait_ge(s_sd0, 1)
            nc.vector.reciprocal(rstd[:, :], sd[:, :]).then_inc(s_rstd0, 1)
            dve.wait_ge(s_rstd0, 1)
            dve.wait_ge(s_dinv, 2)

            dve.wait_ge(s_any, 1)
            nc.vector.tensor_copy(anylow[:, :], tb[0][0:1, 0:1]).then_inc(s_flag, 1)

            def n_rows(b, u):
                t = b + u
                ge(dve, n_xtr, t - 1)
                ge(dve, n_out[u], 8 * b)
                nc.vector.tensor_scalar(xs[u][:, :], keep[:, t, :], mv[:, t, 0:1], rstd[:, bass.ds(t, 1)],
                                        ALU.subtract, ALU.mult).then_inc(n_new, 1)

            def n_lo(b, u):
                t = b + u
                dve.wait_ge(n_xth, t + 1)
                ge(dve, n_prj, t - 1)
                rest(xt_l[u][:, :, :], xb[u][:, 0:D].rearrange("p (k i) -> p k i", k=KT), xt_h[u][:, :, :])\
                    .then_inc(n_xtl, 1)

            def n_moving(b, u):
                t = b + u
                dve.wait_ge(n_ph, t + 1)
                nc.vector.scalar_tensor_tensor(pm[:, t, D:2 * D], jb[u][:, 0:D], dinv[:, bass.ds(t, 1)],
                                               pm[:, t, 0:D].bitcast(F32), ALU.mult, ALU.subtract)\
                    .then_inc(n_pl, 1)

            n_rows(0, 0)
            n_rows(0, 1)
            n_lo(0, 0)
            n_rows(2, 0)
            n_lo(0, 1)
            n_moving(0, 0)
            n_rows(2, 1)
            n_lo(2, 0)
            n_moving(0, 1)
            with dve.Fori(2, NT // 2) as half:
                b = 2 * half
                n_rows(b, 0)
                n_lo(b - 2, 1)
                n_moving(b - 2, 0)
                n_rows(b, 1)
                n_lo(b, 0)
                n_moving(b - 2, 1)
            n_lo(NT - 2, 1)
            n_moving(NT - 2, 0)
            n_moving(NT - 2, 1)

            def parts(k, a):
                w, prev = a.w, aggs[k - 1] if k else None

                def split(q):
                    js = slice(q * TPC, (q + 1) * TPC)
                    ge(dve, a.ph, q + 1)
                    rest(pm[:, js, w:2 * w], keep[:, js, 0:w], pm[:, js, 0:w]).then_inc(a.pl.sem, 1)

                def rows_lo(b, u):
                    t = b + u
                    if a.proj:
                        kt = a.proj[2]
                        ge(dve, a.xth, t + 1)
                        ge(dve, a.prj, t - 1)
                        rest(xt_l[u][:, 0:kt, :], xb[u][:, 0:kt * P].rearrange("p (k i) -> p k i", k=kt),
                             xt_h[u][:, 0:kt, :]).then_inc(a.xtl.sem, 1)

                def total(b, u):
                    t = b + u
                    ge(dve, a.tmp, t + 1)
                    dst, o = zb[u][:, 0:w], ob[u][:, 0:w]
                    if a in (C, Dg):
                        d = dinv if a is C else rdeg
                        nc.vector.scalar_tensor_tensor(dst, o, d[:, bass.ds(t, 1)], tmp[:, 0:w],
                                                       ALU.mult, ALU.add).then_inc(a.r.sem, 1)
                    else:
                        nc.vector.tensor_tensor(dst, o, tmp[:, 0:w], ALU.add).then_inc(a.r.sem, 1)

                def rows_free(b, u):
                    if isinstance(b, int) and b == 0:
                        if not k:
                            dve.wait_ge(n_out[u], 8 * NT)
                            dve.wait_ge(n_xtr, NT)
                        else:
                            if prev.norm:
                                ge(dve, prev.out[u], 8 * NT)
                            ge(dve, prev.xtr, NT)

                def residual(b, u):
                    t = b + u
                    if a is C:
                        ge(dve, a.r, t + 1)
                    else:
                        ge(dve, a.rb, t + 1)
                    if not a.norm:
                        rows_free(b, u)
                        ge(dve, a.xtr, t - 1)
                        nc.vector.tensor_scalar(xs[u][:, 0:w], zb[u][:, 0:w], 0.0, None, ALU.max)\
                            .then_inc(a.new.sem, 1)
                        return
                    ge(dve, a.xres[u], 8 * b + 16)
                    if a.last:
                        nc.vector.tensor_tensor(zb[u][:, :], zb[u][:, :], xres[u][:, :], ALU.add).then_inc(a.y.sem, 1)
                    else:
                        nc.vector.scalar_tensor_tensor(zb[u][:, :], zb[u][:, :], 0.0, xres[u][:, :],
                                                       ALU.max, ALU.add).then_inc(a.y.sem, 1)
                    ge(dve, a.y, t + 1)
                    nc.vector.bn_stats(stats[u][:, :], zb[u][:, :]).then_inc(a.stat.sem, 1)
                    ge(dve, a.stat, t + 1)
                    ge(dve, a.sd, t - 1)
                    alone(dve, passed["vector"])
                    nc.vector.bn_aggr(mv[:, u, :], stats[u][:, :]).then_inc(a.mv.sem, 1)

                def norm(b, u):
                    t = b + u
                    if not a.norm:
                        return
                    ge(dve, a.sd, t + 1)
                    nc.vector.reciprocal(rstd[:, u:u + 1], sd[:, u:u + 1]).then_inc(a.rstd.sem, 1)
                    ge(dve, a.rstd, t + 1)
                    rows_free(b, u)
                    if a.proj:
                        ge(dve, a.xtr, t - 1)
                    ge(dve, a.out[u], 8 * b)
                    nc.vector.tensor_scalar(xs[u][:, :], zb[u][:, :], mv[:, u, 0:1], rstd[:, u:u + 1],
                                            ALU.subtract, ALU.mult).then_inc(a.new.sem, 1)

                def self_term(b, u):
                    t = b + u
                    if a is C:
                        ge(dve, a.prj, t + 1)
                        ge(dve, a.pk, t + 1)
                        ge(dve, a.rout, 16 * t)
                        nc.vector.tensor_tensor(rst[:, :], jb[u][:, D:2 * D], bsum[:, :], ALU.add)\
                            .then_inc(a.rt.sem, 1)

                return split, rows_lo, total, residual, norm, self_term

            def general():
                for k, a in enumerate(aggs):
                    split, rows_lo, total, residual, norm, self_term = parts(k, a)

                    def lo(t, c):
                        n = 4 * t + c
                        ge(dve, a.ah, n + 1)
                        ge(dve, a.mm, n - 3)
                        rest(ringl[c], adjt[:, t, c * CH:(c + 1) * CH], ringh[c]).then_inc(a.al.sem, 1)

                    def slot(b, u, main=True, nxt=True, ep=True, fin=True):
                        t = b + u
                        p, pp = before(b, u), before(b, u, 2)
                        if fin:
                            rows_lo(*pp)
                        if ep:
                            total(*p)
                        if main:
                            lo(t, 2)
                        if ep:
                            residual(*p)
                        if main:
                            lo(t, 3)
                        if ep:
                            norm(*p)
                        if fin:
                            self_term(*pp)
                        if nxt:
                            lo(t + 1, 0)
                            lo(t + 1, 1)

                    if k:
                        for q in range(NCH):
                            split(q)
                    lo(0, 0)
                    lo(0, 1)
                    slot(0, 0, ep=False, fin=False)
                    slot(0, 1, fin=False)
                    slot(2, 0)
                    slot(2, 1)
                    with dve.Fori(2, NT // 2 - 1) as half:
                        slot(2 * half, 0)
                        slot(2 * half, 1)
                    slot(NT - 2, 0)
                    slot(NT - 2, 1, nxt=False)
                    slot(NT, 0, main=False, nxt=False)
                    slot(NT, 1, main=False, nxt=False, ep=False)

            def exact():
                def back(k, b, u):
                    a, t = aggs[k], b + u
                    if k and isinstance(t, int) and t < 2:
                        ge(dve, aggs[k - 1].mm, 4 * (NT - 2 + t) + 4)
                    if a is C:
                        ge(dve, a.kept, 4 * t + 4)
                    ge(dve, a.mm, 4 * t - 4)
                    nc.vector.tensor_copy(stat[u][:, N // 2:N], adjt[:, t, N // 2:N]).then_inc(a.back.sem, 1)

                for k, a in enumerate(aggs):
                    _, rows_lo, total, residual, norm, self_term = parts(k, a)

                    def slot(b, u, nxt=True, ep=True, fin=True):
                        p, pp, n = before(b, u), before(b, u, 2), after(b, u)
                        if fin:
                            rows_lo(*pp)
                        if ep:
                            total(*p)
                        if nxt and a is not C:
                            back(k, *n)
                        if ep:
                            residual(*p)
                            norm(*p)
                        if fin:
                            self_term(*pp)
                        if nxt and a is C:
                            back(k, *n)

                    if k == 0:
                        back(k, 0, 0)
                        slot(0, 0, ep=False, fin=False)
                    slot(0, 1, fin=False)
                    slot(2, 0)
                    slot(2, 1)
                    with dve.Fori(2, NT // 2 - 1) as half:
                        slot(2 * half, 0)
                        slot(2 * half, 1)
                    slot(NT - 2, 0)
                    slot(NT - 2, 1, nxt=False)
                    if a.last:
                        total(NT - 2, 1)
                        residual(NT - 2, 1)
                        norm(NT - 2, 1)
                        continue
                    split = parts(k + 1, aggs[k + 1])[0]
                    rows_lo(NT - 2, 0)
                    back(k + 1, 0, 0)
                    total(NT - 2, 1)
                    back(k + 1, 0, 1)
                    split(0)
                    residual(NT - 2, 1)
                    norm(NT - 2, 1)
                    self_term(NT - 2, 0)
                    split(1)
                    rows_lo(NT - 2, 1)
                    split(2)
                    self_term(NT - 2, 1)
                    split(3)

            dve.wait_ge(s_flag, 1)
            low = dve.value_load(anylow[0:1, 0:1])
            with dve.If(low > 0):
                general()
            with dve.Else():
                exact()

        @block.tensor
        def _(pe):
            def mm(o, l, r, start, stop):
                return nc.tensor.matmul(o, l, r, start=start, stop=stop)

            def exact3(o, pairs):
                terms = [p for sh, sl, mh, ml in pairs for p in ((sh, mh), (sh, ml), (sl, mh))]
                for i, (s, m) in enumerate(terms):
                    last = mm(o, s, m, i == 0, i == len(terms) - 1)
                return last

            pe.wait_ge(s_id, 2)
            for g in range(NCH):
                pe.wait_ge(s_x[g], 16)
                for k in range(KT):
                    ge(pe, s_x0l, KT * (g - 1) + k + 1)
                    for a in range(TPC):
                        last = nc.tensor.transpose(tb[k][:, a * P:(a + 1) * P],
                                                   keep[:, g * TPC + a, k * P:(k + 1) * P], ident[:, :])
                    last.then_inc(s_x0t, 1)
            pe.wait_ge(s_wraw, 5 * 16)
            for k in range(KT):
                pe.wait_ge(s_x0l, KT * (NCH - 1) + k + 1)
                for i, raw in enumerate((wn_raw, ws_raw)):
                    for o in range(KT):
                        at = i * D + o * P
                        last = nc.tensor.transpose(tb[k][:, at:at + P], raw[:, o, k * P:(k + 1) * P], ident[:, :])
                last.then_inc(s_w2t, 1)
            pe.wait_ge(s_w2l, KT)

            for l, g in enumerate(G):
                pe.wait_ge(s_wgl[l], 1)
                if l:
                    ge(pe, G[l - 1].xtl, NT)
                    ge(pe, G[l - 1].ex, 4 * NT)
                pe.sem_inc(g.prod.sem, 1)
                pe.sem_inc(g.wsl.sem, 1)
                pe.sem_inc(g.staged.sem, 1)
                pe.sem_inc(g.vl.sem, 1)
                with pe.Fori(0, NCH) as i:
                    gs = bass.ts(i, CH)
                    for o in range(2 * KT):
                        if o < KT:
                            ge(pe, g.staged, KT * i + 1)
                        else:
                            ge(pe, g.wsl, KT * i + 1)
                        os = slice(o * P, (o + 1) * P)
                        exact3(scores[:, o * CH:(o + 1) * CH],
                               [(wg_h[:, k, os], wg_l[:, k, os], xtall_h[:, k, gs], xtall_l[:, k, gs])
                                for k in range(KT)]).then_inc(g.prod.sem, 1)
                    ge(pe, g.staged, KT * i + KT + 1)
                    ge(pe, g.vl, 2 * i + 1)
                    for h in range(2):
                        for a in range(2):
                            for k in range(KT):
                                at = a * D + k * P
                                last = nc.tensor.transpose(tb[h][:, at:at + P],
                                                           wht_g[:, k, (2 * h + a) * P:(2 * h + a + 1) * P],
                                                           ident[:, :])
                        last.then_inc(g.vt.sem, 1)
                ge(pe, g.wsl, KT * NCH + 1)
                ge(pe, g.vl, 2 * NCH + 1)

                def score(b, u, c):
                    t = b + u
                    if c == 0:
                        ge(pe, g.q, t + 1)
                    ge(pe, g.ex, 4 * t + c - 3)
                    cs = slice(c * CH, (c + 1) * CH)
                    exact3(scores[:, cs], [(whs_h[u][:, k, :], whs_l[u][:, k, :], wst_h[:, k, cs], wst_l[:, k, cs])
                                           for k in range(KT)]).then_inc(g.sc.sem, 1)

                def turn(b, u, c):
                    n = 4 * (b + u) + c
                    ge(pe, g.msk, n + 1)
                    ge(pe, g.al, n - 1)
                    for q in range(TPC):
                        j = c * TPC + q
                        last = nc.tensor.transpose(tb[c % 2][:, q * P:(q + 1) * P], prob[u][:, j * P:(j + 1) * P],
                                                   ident[:, :])
                    last.then_inc(g.tr.sem, 1)

                def attend(b, u, c):
                    t = b + u
                    ge(pe, g.al, 4 * t + c + 1)
                    if c == 0:
                        ge(pe, g.z, t)
                    for q in range(TPC):
                        j = c * TPC + q
                        qs = slice(q * P, (q + 1) * P)
                        mm(ob0[:, :], ringh[c][:, qs], val[:, j, :], j == 0, False)
                        last = mm(ob0[:, 0:D], ringl[c][:, qs], val[:, j, 0:D], False, j == NT - 1)
                    last.then_inc(g.av.sem, 1)

                def rows(b, u):
                    if l < LAYERS - 1:
                        t = b + u
                        ge(pe, g.new, t + 1)
                        ge(pe, g.xtl, t)
                        for k in range(KT):
                            last = nc.tensor.transpose(xb0[:, k * P:(k + 1) * P], xs[u][:, k * P:(k + 1) * P],
                                                       ident[:, :])
                        last.then_inc(g.xtr.sem, 1)

                def slot(b, u, main=True, av=True, fin=True):
                    p = before(b, u)
                    if main:
                        score(b, u, 0)
                    if av:
                        turn(*p, 0)
                        turn(*p, 1)
                    if main:
                        score(b, u, 1)
                        score(b, u, 2)
                    if fin:
                        rows(*before(b, u, 2))
                    if main:
                        score(b, u, NCH - 1)
                    if av:
                        attend(*p, 0)
                        turn(*p, 2)
                        attend(*p, 1)
                        turn(*p, 3)
                        attend(*p, 2)
                        attend(*p, 3)

                slot(0, 0, av=False, fin=False)
                slot(0, 1, fin=False)
                slot(2, 0)
                slot(2, 1)
                with pe.Fori(2, NT // 2) as half:
                    b = 2 * half
                    slot(b, 0)
                    slot(b, 1)
                slot(NT, 0, main=False)
                slot(NT, 1, main=False, av=False)

            ge(pe, G[-1].ex, 4 * NT)
            pe.wait_ge(s_bits, 1)
            pe.wait_ge(s_cst, 2)
            mm(tb[0][0:1, 0:1], lowbits[:, :], one[:, :], True, True).then_inc(s_any, 1)

            def n_rows(b, u):
                t = b + u
                pe.wait_ge(n_new, t + 1)
                ge(pe, n_xtl, t - 1)
                for k in range(KT):
                    last = nc.tensor.transpose(xb[u][:, k * P:(k + 1) * P], xs[u][:, k * P:(k + 1) * P], ident[:, :])
                last.then_inc(n_xtr, 1)

            def n_proj(b, u):
                t = b + u
                pe.wait_ge(n_xtl, t + 1)
                ge(pe, n_pl, t - 1)
                exact3(jb[u][:, 0:D], [(xt_h[u][:, k, :], xt_l[u][:, k, :], w1h[:, k, :], w1l[:, k, :])
                                       for k in range(KT)]).then_inc(n_prj, 1)

            n_rows(0, 0)
            n_rows(0, 1)
            n_proj(0, 0)
            n_rows(2, 0)
            n_proj(0, 1)
            n_rows(2, 1)
            n_proj(2, 0)
            with pe.Fori(2, NT // 2) as half:
                b = 2 * half
                n_rows(b, 0)
                n_proj(b - 2, 1)
                n_rows(b, 1)
                n_proj(b, 0)
            n_proj(NT - 2, 1)

            pe.wait_ge(s_idr, 1)
            pe.wait_ge(n_pl, NT)

            def parts(k, a):
                prev = aggs[k - 1] if k else None

                def turn(t, c):
                    n = 4 * t + c
                    ge(pe, a.nat[c % 2], 32 * t + 16 * (c // 2) + 16)
                    ge(pe, a.kept, n - 1)
                    for q in range(TPC):
                        last = nc.tensor.transpose(tb[c % 2][:, q * P:(q + 1) * P], nat[c % 2][:, q * P:(q + 1) * P],
                                                   ident[:, :])
                    last.then_inc(a.tr.sem, 1)

                def begin(b, u, c):
                    t = b + u
                    if k and isinstance(t, int) and t < 2:
                        ge(pe, prev.r, NT - 1 + t)
                        ge(pe, a.pl, c + 1)
                    if c == 0:
                        ge(pe, a.r, t - 1)

                def rows(b, u):
                    t = b + u
                    if a.proj:
                        ge(pe, a.new, t + 1)
                        if k and isinstance(t, int) and t < 2 and prev.proj:
                            ge(pe, prev.xtl, NT)
                        ge(pe, a.xtl, t - 1)
                        for h in range(a.proj[2]):
                            hs = slice(h * P, (h + 1) * P)
                            last = nc.tensor.transpose(xb[u][:, hs], xs[u][:, hs], ident[:, :])
                        last.then_inc(a.xtr.sem, 1)

                def project(b, u):
                    t = b + u
                    if a.proj:
                        wh, wl, kt, width = a.proj
                        wh3 = wh[:, :, :] if kt > 1 else wh[:, :].rearrange("p (k n) -> p k n", k=1)
                        wl3 = wl[:, :, :] if kt > 1 else wl[:, :].rearrange("p (k n) -> p k n", k=1)
                        ge(pe, a.xtl, t + 1)
                        if k and isinstance(t, int) and t < 2 and prev.proj:
                            ge(pe, prev.pk, NT)
                            if prev is C:
                                ge(pe, prev.rt, NT)
                        ge(pe, a.pk, t - 1)
                        if a is C:
                            ge(pe, a.rt, t - 1)
                        exact3(jb[u][:, 0:width], [(xt_h[u][:, h, :], xt_l[u][:, h, :], wh3[:, h, :], wl3[:, h, :])
                                                   for h in range(kt)]).then_inc(a.prj.sem, 1)

                return turn, begin, rows, project

            def general():
                for k, a in enumerate(aggs):
                    turn, begin, rows, project = parts(k, a)
                    w = a.w

                    def main_sum(b, u, c):
                        t = b + u
                        begin(b, u, c)
                        ge(pe, a.al, 4 * t + c + 1)
                        for q in range(TPC):
                            j = c * TPC + q
                            qs = slice(q * P, (q + 1) * P)
                            end = j == NT - 1
                            mm(ob[u][:, 0:2 * w], ringh[c][:, qs], pm[:, j, 0:2 * w], j == 0, False)
                            last = mm(ob[u][:, 0:w], ringl[c][:, qs], pm[:, j, 0:w], False, end and a is not C)
                        if c == NCH - 1 and a is C:
                            last = mm(ob[u][:, 0:2 * w], identr[:, :], pm[:, t, :], False, True)
                        last.then_inc(a.mm.sem, 1)

                    def slot(b, u, main=True, nxt=True, ep=True, fin=True):
                        for c in range(NCH):
                            if main:
                                main_sum(b, u, c)
                            if a is C and nxt:
                                turn(b + u + 1, c)
                            if c == 1 and fin:
                                project(*before(b, u, 2))
                        if ep:
                            rows(*before(b, u))

                    if a is C:
                        for c in range(NCH):
                            turn(0, c)
                    slot(0, 0, ep=False, fin=False)
                    slot(0, 1, fin=False)
                    slot(2, 0)
                    slot(2, 1)
                    with pe.Fori(2, NT // 2 - 1) as half:
                        slot(2 * half, 0)
                        slot(2 * half, 1)
                    slot(NT - 2, 0)
                    slot(NT - 2, 1, nxt=False)
                    slot(NT, 0, main=False, nxt=False)
                    slot(NT, 1, main=False, nxt=False, ep=False)

            def exact():
                def main_sum(k, b, u, c, signals=1):
                    a, t = aggs[k], b + u
                    w = a.w
                    parts(k, a)[1](b, u, c)
                    if c == 0:
                        ge(pe, a.front, t + 1)
                    elif c == NCH // 2:
                        ge(pe, a.back, t + 1)
                    for q in range(TPC):
                        j = c * TPC + q
                        last = mm(ob[u][:, 0:2 * w], stat[u][:, j * P:(j + 1) * P], pm[:, j, 0:2 * w], j == 0,
                                  j == NT - 1 and a is not C)
                        if TPC - signals <= q < TPC - 1:
                            last.then_inc(a.mm.sem, 1)
                    if c == NCH - 1 and a is C:
                        last = mm(ob[u][:, 0:2 * w], identr[:, :], pm[:, t, :], False, True)
                    if signals:
                        last.then_inc(a.mm.sem, 1)

                for k, a in enumerate(aggs):
                    turn, _, rows, project = parts(k, a)

                    def slot(b, u, nxt=True, ep=True, fin=True):
                        for c in range(NCH):
                            main_sum(k, b, u, c)
                            if a is C and nxt:
                                turn(b + u + 1, c)
                            if c == 1 and fin:
                                project(*before(b, u, 2))
                        if ep:
                            rows(*before(b, u))

                    if k == 0:
                        for c in range(NCH):
                            turn(0, c)
                        slot(0, 0, ep=False, fin=False)
                        slot(0, 1, fin=False)
                    slot(2, 0)
                    slot(2, 1)
                    with pe.Fori(2, NT // 2 - 1) as half:
                        slot(2 * half, 0)
                        slot(2 * half, 1)
                    slot(NT - 2, 0)
                    slot(NT - 2, 1, nxt=False)
                    if a.last:
                        continue
                    project(NT - 2, 0)
                    main_sum(k + 1, 0, 0, 0)
                    rows(NT - 2, 1)
                    main_sum(k + 1, 0, 0, 1)
                    main_sum(k + 1, 0, 0, 2)
                    project(NT - 2, 1)
                    for c in range(NCH - 1):
                        main_sum(k + 1, 0, 1, c, signals=0)
                    main_sum(k + 1, 0, 0, NCH - 1)
                    main_sum(k + 1, 0, 1, NCH - 1, signals=NCH)
                    parts(k + 1, aggs[k + 1])[2](0, 0)

            pe.wait_ge(s_flag, 1)
            low = pe.value_load(anylow[0:1, 0:1])
            with pe.If(low > 0):
                general()
            with pe.Else():
                exact()


_INS = ["x", "adj", "L0_gnn_W_stack", "L1_gnn_W", "L2_gnn_W_neigh", "L2_gnn_b_neigh", "L2_gnn_W_self",
        "L2_gnn_b_self", "L3_gnn_W1", "L3_gnn_b1", "L3_gnn_W2", "L3_gnn_b2"]


def kernel(**inputs):
    import numpy as _np
    import concourse.bacc as _bacc
    from concourse import mybir as _mybir
    from concourse.bass_utils import run_bass_kernel_spmd as _run

    nc = _bacc.Bacc("TRN2", target_bir_lowering=False, num_devices=1, dynamic_dma_scratch_size=1024)
    arrays, args = {}, []
    for name in _INS:
        a = _np.ascontiguousarray(inputs[name])
        arrays[f"in_{name}"] = a
        args.append(nc.dram_tensor(f"in_{name}", a.shape, _mybir.dt.from_np(a.dtype), kind="ExternalInput").ap())
    shape = inputs["x"].shape
    args.append(nc.dram_tensor("out_rows", shape, _mybir.dt.float32, kind="ExternalOutput").ap())
    adjacency_resnet(nc, *args)
    r = _run(nc, [arrays], core_ids=[0])
    return r.results[0]["out_rows"]
```

```python
from contextlib import ExitStack

import concourse.bass as bass
from concourse import mybir

F32 = mybir.dt.float32
F32R = mybir.dt.float32r
I32 = mybir.dt.int32
ALU = mybir.AluOpType
ACT = mybir.ActivationFunctionType
AX = mybir.AxisListType

P = 128
LO_BITS = 0xFFF
LN_EPS = 1e-5
DEG_EPS = 1e-5
SLOPE = 0.01



def before(b, u, n=1):
    for _ in range(n):
        b, u = (b, 0) if u else (b - 2, 1)
    return b, u


def inside(b, u, tiles):
    return not isinstance(b, int) or 0 <= b + u < tiles


def after(b, u):
    return (b + 2, 0) if u else (b, 1)


class Signal:

    def __init__(self, sem, base):
        self.sem, self.base = sem, base


def ge(eng, signal, count):
    if isinstance(count, int) and count <= 0:
        return
    if isinstance(signal, Signal):
        eng.wait_ge(signal.sem, count + signal.base)
    else:
        eng.wait_ge(signal, count)


def alone(eng, passed):
    eng.sem_inc(passed, 1)


def adjacency_resnet(nc, x, adj, w_gat, w_gcn, w_neigh, b_neigh, w_self, b_self, w1, b1, w2, b2, out):
    N, D = x.shape
    NT = N // P
    KT = D // P
    CH = 512
    NCH = N // CH
    TPC = CH // P
    LAYERS = w_gat.shape[0]
    AHEAD = NT // NCH
    PIECES = [(q * TPC, (q + 1) * TPC) for q in range(NCH - 1)] + [(NT - TPC, NT - 2), (NT - 2, NT)]
    HID = w1.shape[1]

    x_rows = x.rearrange("(t p) d -> t p d", p=P)
    x_all = x.rearrange("(t p) d -> p t d", p=P)
    adj_rows = adj.rearrange("(t p) n -> t p n", p=P)
    out_rows = out.rearrange("(t p) d -> t p d", p=P)
    xs_dram = nc.dram_tensor("features_scratch", (N, D), F32, kind="Internal").ap()
    rs_dram = nc.dram_tensor("self_term_scratch", (N, D), F32, kind="Internal").ap()
    xs_rows = xs_dram.rearrange("(t p) d -> t p d", p=P)
    rs_rows = rs_dram.rearrange("(t p) d -> t p d", p=P)

    ctx = ExitStack()
    with ctx:
        def sem(name):
            return ctx.enter_context(nc.semaphore(name))

        def sb(name, shape, dt=F32, scope=ctx):
            return scope.enter_context(nc.sbuf_tensor(name, shape, dt))

        keep = sb("keep", [P, NT, D])
        w2h = sb("w2h", [P, KT, 2 * D], F32R)
        w2l = sb("w2l", [P, KT, 2 * D], F32R)
        w3ah = sb("w3ah", [P, KT, HID], F32R)
        w3al = sb("w3al", [P, KT, HID], F32R)
        w3bh = sb("w3bh", [P, D], F32R)
        w3bl = sb("w3bl", [P, D], F32R)
        ident = sb("ident", [P, P])
        identr = sb("identr", [P, P], F32R)
        stat = [sb(f"stationary{u}", [P, N], F32R) for u in range(2)]
        ringh = [stat[0][:, c * CH:(c + 1) * CH] for c in range(NCH)]
        ringl = [stat[1][:, c * CH:(c + 1) * CH] for c in range(NCH)]
        xt_h = [sb(f"xt_h{u}", [P, KT, P], F32R) for u in range(2)]
        xt_l = [sb(f"xt_l{u}", [P, KT, P], F32R) for u in range(2)]
        xs = [sb(f"xs{u}", [P, D]) for u in range(2)]
        tmp = sb("tmp", [P, D])
        zb = [sb(f"zb{u}", [P, D]) for u in range(2)]
        xres = [sb(f"xres{u}", [P, D]) for u in range(2)]
        nrow = xs + zb
        bsum = sb("bsum", [P, D])
        deg = sb("deg", [P, NT])
        dinv = sb("dinv", [P, NT])
        rdeg = sb("rdeg", [P, NT])
        norms = sb("norm_values", [P, 2, 8])
        stats = [norms[:, u, 0:6] for u in range(2)]
        mvt = [norms[:, u, 6:8] for u in range(2)]
        mv = sb("mv", [P, NT, 2])
        sd = sb("sd", [P, NT])
        rstd = sb("rstd", [P, NT])
        bits = sb("bits", [P, NT])
        lowbits = sb("lowbits", [P, 1])
        anylow = sb("anylow", [1, 1], I32)
        const = sb("constants", [P, 2])
        eps, one = const[:, 0:1], const[:, 1:2]

        row = sb("row_values", [P, 2, 2 * NCH + 3])
        mx = [row[:, u, 0:NCH] for u in range(2)]
        rs = [row[:, u, NCH:2 * NCH] for u in range(2)]
        nmax = [row[:, u, 2 * NCH:2 * NCH + 1] for u in range(2)]
        rsum = [row[:, u, 2 * NCH + 1:2 * NCH + 2] for u in range(2)]
        rinv = [row[:, u, 2 * NCH + 2:2 * NCH + 3] for u in range(2)]
        dsq = sb("dsq", [P, NT])

        gat = ExitStack()
        xtall_h = sb("xtall_h", [P, KT, N], F32R, gat)
        xtall_l = sb("xtall_l", [P, KT, N], F32R, gat)
        wst_h = sb("wst_h", [P, KT, N], F32R, gat)
        wst_l = sb("wst_l", [P, KT, N], F32R, gat)
        val = sb("val", [P, NT, 2 * D], F32R, gat)
        wht = sb("wht", [P, KT, N], F32, gat)
        prob = [sb(f"prob{u}", [P, N], F32, gat) for u in range(2)]
        arow = [sb(f"arow{u}", [P, N], F32, gat) for u in range(2)]
        whs_h = [sb(f"whs_h{u}", [P, KT, P], F32R, gat) for u in range(2)]
        whs_l = [sb(f"whs_l{u}", [P, KT, P], F32R, gat) for u in range(2)]
        wht_g = sb("wht_g", [P, KT, CH], F32, gat)
        wg_h = sb("wg_h", [P, KT, 2 * D], F32R, gat)
        wg_l = sb("wg_l", [P, KT, 2 * D], F32R, gat)
        wg_raw = prob[0][:, 0:KT * 2 * D].rearrange("p (k n) -> p k n", k=KT)
        wn_raw = arow[0][:, 0:KT * D].rearrange("p (k n) -> p k n", k=KT)
        ws_raw = arow[0][:, KT * D:2 * KT * D].rearrange("p (k n) -> p k n", k=KT)
        w1_raw = arow[0][:, 2 * KT * D:3 * KT * D].rearrange("p (k n) -> p k n", k=KT)
        w3a_raw = arow[0][:, 3 * KT * D:3 * KT * D + KT * HID].rearrange("p (k n) -> p k n", k=KT)
        w3b_raw = arow[0][:, 3 * KT * D + KT * HID:3 * KT * D + KT * HID + D]
        bs_raw = arow[1][:, 0:D]
        gat.close()

        pm = sb("pm", [P, NT, 2 * D], F32R)
        adjt = sb("adjt", [P, NT, N])
        nat = [adjt[:, NT - 1, c * CH:(c + 1) * CH] for c in range(NCH)]
        rst = sb("rst", [P, D])
        weight = ExitStack()
        w1h = sb("w1h", [P, KT, D], F32R, weight)
        w1l = sb("w1l", [P, KT, D], F32R, weight)
        weight.close()
        rin = [sb(f"rin{u}", [P, D]) for u in range(2)]
        bout = sb("bout", [P, D])
        bhid = sb("bhid", [P, HID])

        scores = ctx.enter_context(nc.psum_tensor("scores", [P, N], F32))
        tb = [ctx.enter_context(nc.psum_tensor(f"tb{i}", [P, CH], F32)) for i in range(2)]
        ob0 = ctx.enter_context(nc.psum_tensor("ob0", [P, CH], F32))
        xb0 = ctx.enter_context(nc.psum_tensor("xb0", [P, CH], F32))
        ob = [ob0, scores[:, 0:CH]]
        xb = [xb0, scores[:, CH:2 * CH]]
        jb = [scores[:, 2 * CH:3 * CH], scores[:, 3 * CH:4 * CH]]

        passed = {e: sem(f"waits_passed_{e}") for e in ("sync", "gpsimd", "scalar", "vector")}
        s_id = sem("identity_ready")
        s_idr = sem("identity_r_ready")
        s_cst = sem("constants_ready")
        s_x = [sem(f"features_loaded_{g}") for g in range(NCH)]
        s_wraw = sem("weights_loaded")
        s_bias = sem("self_biases_loaded")
        s_bsum = sem("self_bias_sum_ready")
        s_wh = sem("weights_hi_ready")
        s_wl = sem("weights_lo_ready")
        s_w2t = sem("block2_weights_transposed")
        s_w2h = sem("block2_weights_hi_ready")
        s_w2l = sem("block2_weights_lo_ready")
        s_x0t = sem("input_transposed")
        s_x0h = sem("input_transposed_hi")
        s_x0l = sem("input_transposed_lo")
        s_wgraw = [sem(f"gat_weight_loaded_{l}") for l in range(LAYERS)]
        s_wgh = [sem(f"gat_weight_hi_{l}") for l in range(LAYERS)]
        s_wgl = [sem(f"gat_weight_lo_{l}") for l in range(LAYERS)]

        sems, counted = {}, {}

        def counter(name, total):
            if name not in sems:
                sems[name], counted[name] = sem(name), 0
            signal = Signal(sems[name], counted[name])
            counted[name] += total
            return signal

        class Gat:

            def __init__(self, l):
                def s(name, total):
                    return counter(f"gat_{name}", total)
                self.prod = s("projection_done", 4 * NCH + 1)
                self.staged = s("wht_staged", KT * NCH + 1)
                self.kept = s("wht_kept", NCH + 1)
                self.wsh = s("wst_hi", KT * NCH)
                self.wsl = s("wst_lo", KT * NCH + 1)
                self.vt = s("values_transposed", 2 * NCH)
                self.vh = s("values_hi", 2 * NCH)
                self.vl = s("values_lo", 2 * NCH + 1)
                self.adj = [s(f"adjacency_loaded_{u}", 8 * NT) for u in range(2)]
                self.xres = [s(f"residual_loaded_{u}", 8 * NT * (l == LAYERS - 1)) for u in range(2)]
                self.qh = s("query_hi", NT)
                self.q = s("query_ready", NT)
                self.sc = s("scores_ready", 4 * NT)
                self.mx = s("chunk_max", 4 * NT)
                self.nmax = s("row_max", NT)
                self.ex = s("exp_done", 4 * NT)
                self.msk = s("masked", 4 * NT)
                self.low = s("low_bits_masked", NT - 2 if l else 2)
                self.deg = s("degree_or_low_bits", NT - 2 if l else NT + 2)
                self.tr = s("probs_transposed", 4 * NT)
                self.ah = s("probs_hi", 4 * NT)
                self.al = s("probs_lo", 4 * NT)
                self.av = s("values_summed", 4 * NT)
                self.rsum = s("row_sum", NT)
                self.rinv = s("row_sum_inverse", NT)
                self.tmp = s("lo_half_scaled", NT)
                self.z = s("attention_scaled", NT)
                self.zx = s("residual_added", NT)
                self.new = s("rows_ready", NT)
                self.rows = s("rows_kept", NT)
                self.stat = s("statistics", NT * (l == LAYERS - 1))
                self.aggr = s("tile_mean_variance", NT * (l == LAYERS - 1))
                self.mv = s("mean_variance", NT * (l == LAYERS - 1))
                self.xtr = s("rows_transposed", NT * (l < LAYERS - 1))
                self.xth = s("rows_transposed_hi", NT * (l < LAYERS - 1))
                self.xtl = s("rows_transposed_lo", NT * (l < LAYERS - 1))

        G = [Gat(l) for l in range(LAYERS)]

        s_bits = sem("low_bits_ready")
        s_any = sem("low_bits_summed")
        s_flag = sem("low_bits_flag_ready")
        s_dpl = sem("degree_plus_eps")
        s_dsq = sem("degree_root")
        s_dinv = sem("degree_inverses")
        s_sd0 = sem("norm0_deviation")
        s_rstd0 = sem("norm0_inverse")
        n_new = sem("norm0_rows")
        n_out = [sem(f"norm0_rows_stored_{c}") for c in range(NCH)]
        n_xtr = sem("norm0_transposed")
        n_xth = sem("norm0_hi")
        n_xtl = sem("norm0_lo")
        n_prj = sem("block1_projection")
        n_ph = sem("norm0_moving_hi")
        n_pl = sem("norm0_moving_lo")

        class Agg:

            def __init__(self, name, width, proj, norm, load_self, last):
                def s(what, total):
                    return counter(f"agg_{what}", total)
                c = name == "block1"
                self.name, self.w, self.proj, self.norm = name, width, proj, norm
                self.load_self, self.last = load_self, last
                self.nat = [s(f"adjacency_chunk{p}_loaded", 16 * NT * c) for p in range(NCH)]
                self.xres = [s(f"residual_loaded_{u}", 8 * NT * norm) for u in range(2)]
                self.rin = [s(f"self_term_loaded_{u}", 8 * NT * load_self) for u in range(2)]
                self.tr = s("adjacency_transposed", 4 * NT * c)
                self.kept = s("adjacency_kept", 4 * NT * c)
                self.front = s("front_half_ready", NT)
                self.back = s("back_half_ready", NT)
                self.ah = s("adjacency_hi", 4 * NT)
                self.al = s("adjacency_lo", 4 * NT)
                self.mm = s("sums_done", 4 * NT)
                self.tmp = s("lo_half_ready", NT)
                self.r = s("sum_ready", NT)
                self.rb = s("term_added", NT * (not c))
                self.y = s("residual_added", NT * norm)
                self.stat = s("statistics", NT * norm)
                self.mv = s("mean_variance", NT * norm)
                self.sd = s("deviation", NT * norm)
                self.rstd = s("deviation_inverse", NT * norm)
                self.new = s("rows_ready", NT)
                self.out = [s(f"rows_stored_{u}", 8 * NT * norm) for u in range(2)]
                self.xtr = s("rows_transposed", NT * bool(proj))
                self.xth = s("rows_hi", NT * bool(proj))
                self.xtl = s("rows_lo", NT * bool(proj))
                self.prj = s("projection_done", NT * bool(proj))
                self.pk = s("projection_kept", NT * bool(proj))
                self.rt = s("self_term_ready", NT * c)
                self.rout = s("self_term_stored", 16 * NT * c)
                self.ph = s("moving_hi", len(PIECES) * (not c))
                self.pl = s("moving_lo", len(PIECES) * (not c))

        C = Agg("block1", D, (w2h, w2l, KT, 2 * D), True, False, False)
        Dg = Agg("block2", D, (w3ah, w3al, KT, HID), True, True, False)
        E = Agg("block3a", HID, None, False, False, False)
        F = Agg("block3b", HID, (w3bh, w3bl, 1, D), True, False, True)
        aggs = [C, Dg, E, F]
        s_bt = sem("block3_biases_loaded")

        def attention_bank(b, u):
            return jb[1] if isinstance(b, int) and b + u == NT - 1 else ob0

        def middle(eng, a, slot):
            last = (NT - AHEAD) // 2 if a is C else NT // 2 - 1
            with eng.Fori(2, last) as half:
                slot(2 * half, 0)
                slot(2 * half, 1)
            if a is C:
                with eng.Fori(last, NT // 2 - 1) as half:
                    slot(2 * half, 0, fresh=False)
                    slot(2 * half, 1, fresh=False)

        block = ctx.enter_context(nc.Block())

        @block.sync
        def _(sp):
            per_k = "(k p) n -> p k n"
            for g in range(NCH):
                sp.dma_start(keep[:, g * TPC:(g + 1) * TPC, :], x_all[:, g * TPC:(g + 1) * TPC, :]).then_inc(s_x[g], 16)
                if g == 0:
                    sp.dma_start(wg_raw, w_gat[0].rearrange(per_k, p=P)).then_inc(s_wgraw[0], 16)
            sp.dma_start(wn_raw, w_neigh.rearrange(per_k, p=P)).then_inc(s_wraw, 16)
            sp.dma_start(ws_raw, w_self.rearrange(per_k, p=P)).then_inc(s_wraw, 16)
            sp.dma_start(w1_raw, w_gcn.rearrange(per_k, p=P)).then_inc(s_wraw, 16)
            sp.dma_start(w3a_raw, w1.rearrange(per_k, p=P)).then_inc(s_wraw, 16)
            sp.dma_start(w3b_raw, w2).then_inc(s_wraw, 16)
            sp.dma_start(bsum[:, :], b_neigh[None, :].to_broadcast([P, D])).then_inc(s_bias, 16)
            sp.dma_start(bs_raw, b_self[None, :].to_broadcast([P, D])).then_inc(s_bias, 16)

            for l, g in enumerate(G):
                if l:
                    ge(sp, G[l - 1].tr, 4 * (NT - 1))
                    sp.dma_start(wg_raw, w_gat[l].rearrange(per_k, p=P)).then_inc(s_wgraw[l], 16)

                def load(b, u):
                    t = b + u
                    ge(sp, g.msk, 4 * t - 4)
                    if not isinstance(t, int):
                        alone(sp, passed["sync"])
                    ge(sp, g.deg, t - 1)
                    if not isinstance(t, int):
                        alone(sp, passed["sync"])
                    sp.dma_start(arow[u][:, :], adj_rows[t]).then_inc(g.adj[u].sem, 16)
                    if l == LAYERS - 1:
                        ge(sp, g.rows, t - 1)
                        sp.dma_start(xres[u][:, :], x_rows[t]).then_inc(g.xres[u].sem, 16)

                if l == 0:
                    sp.wait_ge(s_wl, 3)
                    sp.wait_ge(s_w2t, 2)
                    sp.wait_ge(s_bsum, 1)
                else:
                    ge(sp, G[l - 1].msk, 4 * NT)
                    ge(sp, G[l - 1].deg, NT + 2)
                load(0, 0)
                load(0, 1)
                with sp.Fori(1, NT // 2) as half:
                    b = 2 * half
                    load(b, 0)
                    load(b, 1)

            def load_nat(t, c):
                ge(sp, C.tr, 4 * t + c - 3)
                sp.dma_start(nat[c], adj_rows[t][:, c * CH:(c + 1) * CH]).then_inc(C.nat[c].sem, 16)

            def store0(t, c):
                sp.wait_ge(n_new, t + 1)
                sp.dma_start(xs_rows[t], nrow[c][:, :]).then_inc(n_out[c], 16)

            ge(sp, G[-1].prod, 4 * NCH + 1)
            for c in range(NCH):
                load_nat(0, c)
            with sp.Fori(0, NT // NCH) as q:
                for c in range(NCH):
                    store0(NCH * q + c, c)
                    load_nat(q + 1, c)
            for c in range(NCH):
                sp.wait_ge(n_out[c], 16 * NT // NCH)

            for k, a in enumerate(aggs):
                prev = aggs[k - 1] if k else None
                if a.load_self:
                    ge(sp, prev.rout, 16 * NT)
                if k == 0:
                    sp.wait_ge(n_prj, NT)
                    sp.dma_start(bout[:, :], b2[None, :].to_broadcast([P, D])).then_inc(s_bt, 16)
                    sp.dma_start(bhid[:, :], b1[None, :].to_broadcast([P, HID])).then_inc(s_bt, 16)

                def load_res(b, u):
                    t = b + u
                    if a is Dg and isinstance(t, int) and t < 2:
                        return
                    if a.norm:
                        ge(sp, a.y, t - 1)
                        sp.dma_start(xres[u][:, :], xs_rows[t]).then_inc(a.xres[u].sem, 16)
                    if a.load_self:
                        sp.dma_start(rin[u][:, :], rs_rows[t]).then_inc(a.rin[u].sem, 16)

                def store(b, u):
                    t = b + u
                    if a.norm:
                        ge(sp, a.new, t + 1)
                        dst = out_rows if a.last else xs_rows
                        sp.dma_start(dst[t], xs[u][:, :]).then_inc(a.out[u].sem, 16)

                def store_self(b, u):
                    t = b + u
                    if a is C:
                        ge(sp, a.rt, t + 1)
                        sp.dma_start(rs_rows[t], rst[:, :]).then_inc(a.rout.sem, 16)

                if k and a.norm:
                    src = aggs[k - 1] if aggs[k - 1].norm else aggs[k - 2]
                    for u in range(2):
                        ge(sp, src.out[u], 8 * NT)

                def slot(b, u, nat=True, fin=True):
                    if a.last:
                        if inside(*before(b, u, 4), NT):
                            store(*before(b, u, 4))
                        load_res(b, u)
                        return
                    if fin:
                        store(*before(b, u, 2))
                    load_res(b, u)
                    for c in range(NCH):
                        if a is C and nat:
                            load_nat(b + u + AHEAD + 1, c)
                        if c == 1 and fin:
                            store_self(*before(b, u, 2))

                slot(0, 0, fin=False)
                slot(0, 1, fin=False)
                slot(2, 0)
                slot(2, 1)
                last = (NT - AHEAD) // 2 - 1 if a is C else NT // 2
                with sp.Fori(2, last) as half:
                    slot(2 * half, 0)
                    slot(2 * half, 1)
                if a is C:
                    slot(2 * last, 0)
                    slot(2 * last, 1, nat=False)
                    with sp.Fori(last + 1, NT // 2) as half:
                        slot(2 * half, 0, nat=False)
                        slot(2 * half, 1, nat=False)
                if a.last:
                    store(NT - 4, 0)
                    store(NT - 4, 1)
                for u in range(2):
                    if a is C:
                        ge(sp, C.y, NT - 1 + u)
                        ge(sp, C.out[u], 16)
                        sp.dma_start(xres[u][:, :], xs_rows[u]).then_inc(Dg.xres[u].sem, 16)
                        ge(sp, C.rout, 16 * (u + 1))
                        sp.dma_start(rin[u][:, :], rs_rows[u]).then_inc(Dg.rin[u].sem, 16)
                    store(NT - 2, u)
                    store_self(NT - 2, u)
            for u in range(2):
                ge(sp, F.out[u], 8 * NT)
            ge(sp, C.rout, 16 * NT)

        @block.gpsimd
        def _(pool):
            nc.gpsimd.memset(ident[:, :], 0.0).then_inc(s_id, 1)
            pool.wait_ge(s_id, 1)
            nc.gpsimd.affine_select(out=ident[:, :], in_=ident[:, :], compare_op=ALU.not_equal, fill=1.0, base=0,
                                    pattern=[[-1, P]], channel_multiplier=1).then_inc(s_id, 1)
            nc.gpsimd.memset(eps[:, :], LN_EPS).then_inc(s_cst, 1)
            nc.gpsimd.memset(one[:, :], 1.0).then_inc(s_cst, 1)
            pool.wait_ge(s_bias, 32)
            nc.gpsimd.tensor_tensor(bsum[:, :], bsum[:, :], bs_raw, ALU.add).then_inc(s_bsum, 1)

            for l, g in enumerate(G):
                def query(b, u):
                    t = b + u
                    ge(pool, g.sc, 4 * t - 4)
                    if not isinstance(t, int):
                        alone(pool, passed["gpsimd"])
                    src = wht[:, :, bass.ts(t, P)]
                    nc.gpsimd.tensor_copy(whs_h[u][:, :, :], src).then_inc(g.qh.sem, 1)
                    ge(pool, g.qh, t + 1)
                    alone(pool, passed["gpsimd"])
                    nc.gpsimd.tensor_tensor(whs_l[u][:, :, :], src, whs_h[u][:, :, :].bitcast(F32),
                                            ALU.subtract).then_inc(g.q.sem, 1)

                def mask(b, u):
                    t = b + u
                    ge(pool, g.adj[u], 8 * b + 16)
                    for c in range(NCH):
                        ge(pool, g.ex, 4 * t + c + 1)
                        cs = slice(c * CH, (c + 1) * CH)
                        nc.gpsimd.tensor_tensor(prob[u][:, cs], prob[u][:, cs], arow[u][:, cs],
                                                ALU.mult).then_inc(g.msk.sem, 1)

                def residual(b, u):
                    t = b + u
                    ge(pool, g.z, t + 1)
                    alone(pool, passed["gpsimd"])
                    nc.gpsimd.tensor_tensor(zb[u][:, :], zb[u][:, :], keep[:, t, :], ALU.add).then_inc(g.zx.sem, 1)

                def keep_rows(b, u):
                    if l < LAYERS - 1:
                        ge(pool, g.new, b + u + 1)
                        alone(pool, passed["gpsimd"])
                        nc.gpsimd.tensor_copy(keep[:, b + u, :], xs[u][:, :]).then_inc(g.rows.sem, 1)

                def slot(b, u, main=True, nxt=True, av=True, fin=True):
                    if fin:
                        keep_rows(*before(b, u, 2))
                    if nxt:
                        query(*after(b, u))
                    if main:
                        mask(b, u)
                    if av:
                        residual(*before(b, u))

                ge(pool, g.kept, 2)
                query(0, 0)
                slot(0, 0, av=False, fin=False)
                ge(pool, g.kept, NCH + 1)
                slot(0, 1, fin=False)
                with pool.Fori(1, NT // 2 - 1) as half:
                    b = 2 * half
                    slot(b, 0)
                    slot(b, 1)
                slot(NT - 2, 0)
                slot(NT - 2, 1, nxt=False)
                slot(NT, 0, main=False, nxt=False)
                slot(NT, 1, main=False, nxt=False, av=False)

            def term(a, b, u):
                t = b + u
                if a is not F:
                    ge(pool, a.r, t + 1)
                if a is Dg:
                    ge(pool, a.rin[u], 8 * b + 16)
                    nc.gpsimd.tensor_tensor(zb[u][:, :], zb[u][:, :], rin[u][:, :], ALU.add).then_inc(a.rb.sem, 1)
                elif a is E:
                    nc.gpsimd.tensor_tensor(zb[u][:, 0:HID], zb[u][:, 0:HID], bhid[:, :], ALU.add).then_inc(a.rb.sem, 1)
                else:
                    ge(pool, a.xres[u], 8 * b + 16)
                    nc.gpsimd.tensor_tensor(xres[u][:, :], xres[u][:, :], bout[:, :], ALU.add).then_inc(a.rb.sem, 1)

            pool.wait_ge(s_bt, 32)
            for a in (Dg, E, F):
                with pool.Fori(0, NT // 2) as half:
                    b = 2 * half
                    term(a, b, 0)
                    term(a, b, 1)

        @block.scalar
        def _(act):
            def copy(dst, src, **kw):
                return nc.scalar.activation(dst, src, ACT.Copy, **kw)

            def features(i):
                for k in range(KT):
                    act.wait_ge(s_x0t, KT * i + k + 1)
                    copy(xtall_h[:, k, i * CH:(i + 1) * CH], tb[k][:, :]).then_inc(s_x0h, 1)

            def weights():
                act.wait_ge(s_wraw, 5 * 16)
                copy(w1h[:, :, :], w1_raw).then_inc(s_wh, 1)
                copy(w3ah[:, :, :], w3a_raw).then_inc(s_wh, 1)
                copy(w3bh[:, :], w3b_raw).then_inc(s_wh, 1)
                for k in range(KT):
                    act.wait_ge(s_w2t, k + 1)
                    copy(w2h[:, k, :], tb[k][:, :]).then_inc(s_w2h, 1)

            features(0)
            act.wait_ge(s_wgraw[0], 16)
            copy(wg_h[:, :, :], wg_raw).then_inc(s_wgh[0], 1)
            features(1)

            def layer(l, g, previous):
                def weight_hi(n):
                    act.wait_ge(s_wgraw[n], 16)
                    ge(act, g.prod, 4 * NCH + 1)
                    copy(wg_h[:, :, :], wg_raw).then_inc(s_wgh[n], 1)

                act.sem_inc(g.kept.sem, 1)

                def group(i):
                    ge(act, g.kept, i + 1)
                    for o in range(KT):
                        ge(act, g.prod, 4 * i + o + 2)
                        copy(wht_g[:, o, :], scores[:, o * CH:(o + 1) * CH]).then_inc(g.staged.sem, 1)
                    if not l and i in (1, 2):
                        features(i + 1)
                    if not l and i == 3:
                        weights()
                    for o in range(KT):
                        ge(act, g.prod, 4 * i + KT + o + 2)
                        if not isinstance(i, int):
                            alone(act, passed["scalar"])
                        copy(wst_h[:, o, bass.ts(i, CH)], scores[:, (KT + o) * CH:(KT + o + 1) * CH])\
                            .then_inc(g.wsh.sem, 1)
                    for h in range(2):
                        if l and h == 0:
                            ge(act, G[l - 1].av, 4 * (NT - 1) + i + 1)
                            if not isinstance(i, int):
                                alone(act, passed["scalar"])
                        ge(act, g.vt, 2 * i + h + 1)
                        if not isinstance(i, int):
                            alone(act, passed["scalar"])
                        copy(val[:, bass.ds(i * TPC + 2 * h, 2), 0:D],
                             tb[h][:, :].rearrange("p (a d) -> p a d", a=2)).then_inc(g.vh.sem, 1)

                if l:
                    group(0)
                    group(1)
                    previous[0](NT, 1, main=False, av=False)
                    with act.Fori(2, NCH) as i:
                        group(i)
                else:
                    for i in range(NCH):
                        group(i)

                def hi(b, u, c):
                    n = 4 * (b + u) + c
                    ge(act, g.tr, n + 1)
                    ge(act, g.av, n - 3)
                    copy(ringh[c], tb[c % 2][:, :]).then_inc(g.ah.sem, 1)

                def exp(b, u, c):
                    t = b + u
                    if c == 0:
                        ge(act, g.nmax, t + 1)
                        ge(act, g.tr, 4 * t - 4)
                        ge(act, g.rsum, t - 1)
                    cs = slice(c * CH, (c + 1) * CH)
                    nc.scalar.activation(prob[u][:, cs], scores[:, cs], ACT.Exp, bias=nmax[u][:, :],
                                         accum_out=rs[u][:, c:c + 1]).then_inc(g.ex.sem, 1)

                def lo_half(b, u):
                    t = b + u
                    ge(act, g.av, 4 * t + 4)
                    ge(act, g.rinv, t + 1)
                    ge(act, g.z, t)
                    copy(tmp[:, :], attention_bank(b, u)[:, D:2 * D], scale=rinv[u][:, :]).then_inc(g.tmp.sem, 1)

                def rows_hi(b, u):
                    if l < LAYERS - 1:
                        t = b + u
                        ge(act, g.xtr, t + 1)
                        alone(act, passed["scalar"])
                        copy(xtall_h[:, :, bass.ts(t, P)],
                             xb0[:, 0:D].rearrange("p (k i) -> p k i", k=KT)).then_inc(g.xth.sem, 1)

                def slot(b, u, main=True, av=True, fin=True, last=False):
                    p = before(b, u)
                    if av:
                        hi(*p, 0)
                        hi(*p, 1)
                    if fin:
                        rows_hi(*before(b, u, 2))
                    if av:
                        hi(*p, 2)
                    if main:
                        exp(b, u, 0)
                    if av:
                        hi(*p, 3)
                    if main:
                        exp(b, u, 1)
                        exp(b, u, 2)
                        exp(b, u, 3)
                    if last:
                        hi(b, u, 0)
                        hi(b, u, 1)
                    if av:
                        lo_half(*p)

                slot(0, 0, av=False, fin=False)
                slot(0, 1, fin=False)
                slot(2, 0)
                slot(2, 1)
                with act.Fori(2, NT // 2 - 1) as half:
                    b = 2 * half
                    slot(b, 0)
                    slot(b, 1)
                slot(NT - 2, 0)
                slot(NT - 2, 1, last=True)
                if l < LAYERS - 1:
                    weight_hi(l + 1)
                    hi(NT - 2, 1, 2)
                    rows_hi(NT - 2, 0)
                    hi(NT - 2, 1, 3)
                    lo_half(NT - 2, 1)
                return slot, hi, lo_half

            last_layer = None
            for l, g in enumerate(G):
                last_layer = layer(l, g, last_layer)
            _, hi, lo_half = last_layer

            def n_deviation(first, last):
                ge(act, G[-1].mv, last)
                nc.scalar.activation(sd[:, first:last], mv[:, first:last, 1], ACT.Sqrt, bias=eps[:, :])\
                    .then_inc(s_sd0, 1)

            def n_hi(t, u):
                act.wait_ge(n_xtr, t + 1)
                ge(act, n_prj, t - 1)
                copy(xt_h[u][:, :, :], xb[u][:, 0:D].rearrange("p (k i) -> p k i", k=KT)).then_inc(n_xth, 1)

            def n_moving(t, u):
                act.wait_ge(n_prj, t + 1)
                if not isinstance(t, int):
                    alone(act, passed["scalar"])
                copy(pm[:, t, 0:D], jb[u][:, 0:D], scale=dinv[:, bass.ds(t, 1)]).then_inc(n_ph, 1)

            def keep_adj(t, c):
                ge(act, C.tr, 4 * t + c + 1)
                if not isinstance(t, int):
                    alone(act, passed["scalar"])
                copy(adjt[:, t, c * CH:(c + 1) * CH], tb[c % 2][:, :]).then_inc(C.kept.sem, 1)

            act.wait_ge(s_cst, 2)
            ge(act, G[0].deg, NT)
            nc.scalar.activation(dsq[:, :], deg[:, :], ACT.Sqrt, bias=one[:, :]).then_inc(s_dsq, 1)
            hi(NT - 2, 1, 2)
            n_deviation(0, NT - 2)
            hi(NT - 2, 1, 3)
            n_hi(0, 0)
            lo_half(NT - 2, 1)
            act.wait_ge(s_dinv, 2)
            keep_adj(0, 0)
            n_hi(1, 1)
            keep_adj(0, 1)
            n_moving(0, 0)
            n_hi(2, 0)
            keep_adj(0, 2)
            n_moving(1, 1)
            n_deviation(NT - 2, NT)
            n_hi(3, 1)
            keep_adj(0, 3)
            n_moving(2, 0)

            def n_step(q, c):
                n_hi(NCH * q + c, c % 2)
                keep_adj(q, c)
                n_moving(NCH * q + c - 1, 1 - c % 2)

            with act.Fori(1, AHEAD) as q:
                for c in range(NCH):
                    n_step(q, c)
            copy(stat[0][:, 0:N // 2], adjt[:, 0, 0:N // 2]).then_inc(C.front.sem, 1)
            n_moving(NT - 1, 1)

            def parts(k, a):
                w, prev = a.w, aggs[k - 1] if k else None

                def split(q):
                    js = slice(*PIECES[q])
                    ge(act, prev.mm, 4 * (NT - 1) + min(q + 1, NCH))
                    ge(act, prev.pk if prev.proj else prev.new, js.stop)
                    copy(pm[:, js, 0:w], keep[:, js, 0:w]).then_inc(a.ph.sem, 1)

                def rows_hi(b, u):
                    t = b + u
                    if a.proj:
                        kt = a.proj[2]
                        ge(act, a.xtr, t + 1)
                        ge(act, a.prj, t - 1)
                        copy(xt_h[u][:, 0:kt, :], xb[u][:, 0:kt * P].rearrange("p (k i) -> p k i", k=kt))\
                            .then_inc(a.xth.sem, 1)

                def lo_half(b, u):
                    t = b + u
                    ge(act, a.mm, 4 * t + 4)
                    ge(act, a.r, t)
                    alone(act, passed["scalar"])
                    kw = {}
                    if a is C:
                        kw = {"scale": dinv[:, bass.ds(t, 1)]}
                    elif a is Dg:
                        kw = {"scale": rdeg[:, bass.ds(t, 1)]}
                    copy(tmp[:, 0:w], ob[u][:, w:2 * w], **kw).then_inc(a.tmp.sem, 1)

                def deviation(b, u):
                    t = b + u
                    if a.norm:
                        ge(act, a.mv, t + 1)
                        nc.scalar.activation(sd[:, u:u + 1], mv[:, u, 1:2], ACT.Sqrt, bias=eps[:, :])\
                            .then_inc(a.sd.sem, 1)

                def keep_proj(b, u):
                    t = b + u
                    if a.proj and not a.last:
                        width = min(D, a.proj[3])
                        ge(act, a.prj, t + 1)
                        alone(act, passed["scalar"])
                        copy(keep[:, t, 0:width], jb[u][:, 0:width]).then_inc(a.pk.sem, 1)

                return split, rows_hi, lo_half, deviation, keep_proj

            def general():
                for k, a in enumerate(aggs):
                    split, rows_hi, lo_half, deviation, keep_proj = parts(k, a)

                    def hi(t, c):
                        n = 4 * t + c
                        if a is C:
                            ge(act, a.kept, n + 1)
                        ge(act, a.mm, n - 3)
                        alone(act, passed["scalar"])
                        copy(ringh[c], adjt[:, t, c * CH:(c + 1) * CH]).then_inc(a.ah.sem, 1)

                    def slot(b, u, main=True, nxt=True, ep=True, fin=True, fresh=True):
                        t = b + u
                        p, pp = before(b, u), before(b, u, 2)
                        fresh = fresh and a is C
                        if fin:
                            rows_hi(*pp)
                        if ep:
                            lo_half(*p)
                        if main:
                            hi(t, 2)
                        if fresh:
                            keep_adj(t + AHEAD, 0)
                        if a is not F and ep:
                            deviation(*p)
                        if a is F and inside(*before(b, u, 3), NT):
                            deviation(*before(b, u, 3))
                        if main:
                            hi(t, 3)
                        if fresh:
                            keep_adj(t + AHEAD, 1)
                        if fin:
                            keep_proj(*pp)
                        if nxt:
                            hi(t + 1, 0)
                        if fresh:
                            keep_adj(t + AHEAD, 2)
                        if nxt:
                            hi(t + 1, 1)
                        if fresh:
                            keep_adj(t + AHEAD, 3)

                    if k:
                        for q in range(len(PIECES)):
                            split(q)
                    if not k:
                        ge(act, C.front, 1)
                        ge(act, C.back, 1)
                    hi(0, 0)
                    hi(0, 1)
                    slot(0, 0, ep=False, fin=False)
                    slot(0, 1, fin=False)
                    slot(2, 0)
                    slot(2, 1)
                    middle(act, a, slot)
                    slot(NT - 2, 0, fresh=False)
                    slot(NT - 2, 1, nxt=False, fresh=False)
                    slot(NT, 0, main=False, nxt=False, fresh=False)
                    slot(NT, 1, main=False, nxt=False, ep=False, fresh=False)
                    if a is F:
                        slot(NT + 2, 0, main=False, nxt=False, ep=False, fin=False, fresh=False)

            def exact():
                def front(k, b, u):
                    a, t = aggs[k], b + u
                    if k and isinstance(t, int) and t < 2:
                        ge(act, aggs[k - 1].mm, 4 * (NT - 2 + t) + 2)
                    if a is C:
                        ge(act, a.kept, 4 * t + 2)
                    ge(act, a.mm, 4 * t - 6)
                    alone(act, passed["scalar"])
                    copy(stat[u][:, 0:N // 2], adjt[:, t, 0:N // 2]).then_inc(a.front.sem, 1)

                for k, a in enumerate(aggs):
                    _, rows_hi, lo_half, deviation, keep_proj = parts(k, a)

                    def slot(b, u, nxt=True, ep=True, fin=True, fresh=True):
                        p, pp, n = before(b, u), before(b, u, 2), after(b, u)
                        if ep:
                            lo_half(*p)
                        if a is F and fin:
                            rows_hi(*pp)
                        if a is F and inside(*before(b, u, 4), NT):
                            deviation(*before(b, u, 4))
                        if a is not C:
                            if nxt:
                                front(k, *n)
                        elif fresh:
                            keep_adj(b + u + AHEAD, 0)
                        if a is not F and fin:
                            rows_hi(*pp)
                        if a is not F and ep:
                            deviation(*p)
                        if a is C:
                            if fresh:
                                keep_adj(b + u + AHEAD, 1)
                            front(k, *n)
                            if fresh:
                                keep_adj(b + u + AHEAD, 2)
                        if fin:
                            keep_proj(*pp)
                        if a is C and fresh:
                            keep_adj(b + u + AHEAD, 3)

                    if k == 0:
                        slot(0, 0, ep=False, fin=False)
                        slot(0, 1, fin=False)
                    else:
                        lo_half(0, 0)
                        if a is not F:
                            deviation(0, 0)
                    slot(2, 0)
                    slot(2, 1)
                    middle(act, a, slot)
                    slot(NT - 2, 0, fresh=False)
                    if a.last:
                        slot(NT - 2, 1, nxt=False)
                        slot(NT, 0, nxt=False)
                        slot(NT, 1, nxt=False, ep=False)
                        slot(NT + 2, 0, nxt=False, ep=False, fin=False)
                        slot(NT + 2, 1, nxt=False, ep=False, fin=False)
                        continue
                    lo_half(NT - 2, 0)
                    split = parts(k + 1, aggs[k + 1])[0]
                    split(0)
                    rows_hi(NT - 4, 1)
                    front(k + 1, 0, 0)
                    if a is C:
                        split(1)
                    deviation(NT - 2, 0)
                    keep_proj(NT - 4, 1)
                    if a is not C:
                        split(1)
                    lo_half(NT - 2, 1)
                    front(k + 1, 0, 1)
                    rows_hi(NT - 2, 0)
                    split(2)
                    deviation(NT - 2, 1)
                    keep_proj(NT - 2, 0)
                    split(3)
                    rows_hi(NT - 2, 1)
                    front(k + 1, 2, 0)
                    keep_proj(NT - 2, 1)
                    split(4)

            act.wait_ge(s_flag, 1)
            low = act.value_load(anylow[0:1, 0:1])
            with act.If(low > 0):
                general()
            with act.Else():
                exact()

        @block.vector
        def _(dve):
            dve.wait_ge(s_id, 2)
            nc.vector.tensor_copy(identr[:, :], ident[:, :]).then_inc(s_idr, 1)

            def rest(dst, v, h):
                return nc.vector.tensor_tensor(dst, v, h.bitcast(F32), ALU.subtract)

            def features(i):
                for k in range(KT):
                    dve.wait_ge(s_x0h, KT * i + k + 1)
                    gs = slice(i * CH, (i + 1) * CH)
                    rest(xtall_l[:, k, gs], tb[k][:, :], xtall_h[:, k, gs]).then_inc(s_x0l, 1)

            def weights():
                dve.wait_ge(s_wh, 3)
                rest(w1l[:, :, :], w1_raw, w1h[:, :, :]).then_inc(s_wl, 1)
                rest(w3al[:, :, :], w3a_raw, w3ah[:, :, :]).then_inc(s_wl, 1)
                rest(w3bl[:, :], w3b_raw, w3bh[:, :]).then_inc(s_wl, 1)
                for k in range(KT):
                    dve.wait_ge(s_w2h, k + 1)
                    rest(w2l[:, k, :], tb[k][:, :], w2h[:, k, :]).then_inc(s_w2l, 1)

            features(0)
            dve.wait_ge(s_wgh[0], 1)
            rest(wg_l[:, :, :], wg_raw, wg_h[:, :, :]).then_inc(s_wgl[0], 1)
            features(1)

            def layer(l, g, previous):
                def weight_lo(n):
                    dve.wait_ge(s_wgh[n], 1)
                    rest(wg_l[:, :, :], wg_raw, wg_h[:, :, :]).then_inc(s_wgl[n], 1)

                def group(i):
                    ge(dve, g.staged, KT * i + KT + 1)
                    nc.vector.tensor_copy(wht[:, :, bass.ts(i, CH)], wht_g[:, :, :]).then_inc(g.kept.sem, 1)
                    if not l and i in (1, 2):
                        features(i + 1)
                    if not l and i == 3:
                        weights()
                    for o in range(KT):
                        ge(dve, g.wsh, KT * i + o + 1)
                        rest(wst_l[:, o, bass.ts(i, CH)], scores[:, (KT + o) * CH:(KT + o + 1) * CH],
                             wst_h[:, o, bass.ts(i, CH)]).then_inc(g.wsl.sem, 1)
                    for h in range(2):
                        ge(dve, g.vh, 2 * i + h + 1)
                        two = bass.ds(i * TPC + 2 * h, 2)
                        rest(val[:, two, D:2 * D], tb[h][:, :].rearrange("p (a d) -> p a d", a=2),
                             val[:, two, 0:D]).then_inc(g.vl.sem, 1)

                if l:
                    end_tile, end_rows, end_low_bits = previous[0]
                    group(0)
                    end_tile(NT - 2, 1)
                    end_low_bits(NT - 2, 0)
                    group(1)
                    end_rows(NT - 2, 1)
                    end_low_bits(NT - 2, 1)
                    with dve.Fori(2, NCH) as i:
                        group(i)
                else:
                    for i in range(NCH):
                        group(i)

                def chunk_max(b, u, c):
                    n = 4 * (b + u) + c
                    ge(dve, g.sc, n + 1)
                    if c == 0:
                        ge(dve, g.nmax, b + u - 1)
                    nc.vector.reduce_max(mx[u][:, c:c + 1], scores[:, c * CH:(c + 1) * CH], AX.X)\
                        .then_inc(g.mx.sem, 1)

                def row_max(b, u):
                    t = b + u
                    ge(dve, g.mx, 4 * t + 4)
                    ge(dve, g.ex, 4 * t - 4)
                    nc.vector.reduce_max(nmax[u][:, :], mx[u][:, :], AX.X, negate=True).then_inc(g.nmax.sem, 1)

                def lo(b, u, c):
                    n = 4 * (b + u) + c
                    ge(dve, g.ah, n + 1)
                    ge(dve, g.av, n - 3)
                    rest(ringl[c], tb[c % 2][:, :], ringh[c]).then_inc(g.al.sem, 1)

                def row_sum(b, u):
                    t = b + u
                    ge(dve, g.ex, 4 * t + 4)
                    nc.vector.reduce_sum(rsum[u][:, :], rs[u][:, :], AX.X).then_inc(g.rsum.sem, 1)
                    ge(dve, g.rsum, t + 1)
                    ge(dve, g.tmp, t - 1)
                    nc.vector.reciprocal(rinv[u][:, :], rsum[u][:, :]).then_inc(g.rinv.sem, 1)

                def degree(b, u):
                    if l == 0:
                        t = b + u
                        ge(dve, g.adj[u], 8 * b + 16)
                        nc.vector.reduce_sum(deg[:, bass.ds(t, 1)], arow[u][:, :], AX.X).then_inc(g.deg.sem, 1)

                def low_bits(b, u):
                    t = b + u
                    if l or (isinstance(t, int) and t >= NT - 2):
                        if not l:
                            ge(dve, g.deg, NT)
                        ge(dve, g.msk, 4 * t + 4)
                        raw = arow[u][:, :].bitcast(I32)
                        nc.vector.tensor_scalar(raw, raw, LO_BITS, None, ALU.bitwise_and).then_inc(g.low.sem, 1)
                        ge(dve, g.low, t + 1 if l else t - NT + 3)
                        nc.vector.tensor_reduce(bits[:, bass.ds(t, 1)], raw, AX.X, ALU.max).then_inc(g.deg.sem, 1)

                def scaled(b, u):
                    t = b + u
                    ge(dve, g.tmp, t + 1)
                    ge(dve, g.rinv, t + 1)
                    ge(dve, g.new, t - 1)
                    nc.vector.scalar_tensor_tensor(zb[u][:, :], attention_bank(b, u)[:, 0:D], rinv[u][:, :], tmp[:, :],
                                                   ALU.mult, ALU.add).then_inc(g.z.sem, 1)

                def finish(b, u):
                    t = b + u
                    ge(dve, g.zx, t + 1)
                    if l == LAYERS - 1:
                        nc.vector.scalar_tensor_tensor(keep[:, t, :], zb[u][:, :], SLOPE, zb[u][:, :],
                                                       ALU.mult, ALU.max).then_inc(g.new.sem, 1)
                        return
                    ge(dve, g.rows, t - 1)
                    ge(dve, g.xtr, t - 1)
                    nc.vector.scalar_tensor_tensor(xs[u][:, :], zb[u][:, :], SLOPE, zb[u][:, :],
                                                   ALU.mult, ALU.max).then_inc(g.new.sem, 1)

                def finish2(b, u):
                    t = b + u
                    ge(dve, g.new, t + 1)
                    ge(dve, g.xres[u], 8 * b + 16)
                    nc.vector.tensor_tensor(keep[:, t, :], keep[:, t, :], xres[u][:, :], ALU.add)\
                        .then_inc(g.rows.sem, 1)

                def finish3(b, u):
                    t = b + u
                    ge(dve, g.rows, t + 1)
                    ge(dve, g.aggr, t - 1)
                    alone(dve, passed["vector"])
                    nc.vector.bn_stats(stats[u][:, :], keep[:, t, :]).then_inc(g.stat.sem, 1)

                def finish4(b, u):
                    t = b + u
                    ge(dve, g.stat, t + 1)
                    ge(dve, g.mv, t - 1)
                    alone(dve, passed["vector"])
                    nc.vector.bn_aggr(mvt[u][:, :], stats[u][:, :]).then_inc(g.aggr.sem, 1)

                def finish5(b, u):
                    t = b + u
                    ge(dve, g.aggr, t + 1)
                    nc.vector.tensor_copy(mv[:, t, :], mvt[u][:, :]).then_inc(g.mv.sem, 1)

                def rows_lo(b, u):
                    if l < LAYERS - 1:
                        t = b + u
                        ge(dve, g.xth, t + 1)
                        cols = bass.ts(t, P)
                        rest(xtall_l[:, :, cols], xb0[:, 0:D].rearrange("p (k i) -> p k i", k=KT),
                             xtall_h[:, :, cols]).then_inc(g.xtl.sem, 1)

                def slot(b, u, main=True, av=True, fin=True, last=False):
                    p, pp = before(b, u), before(b, u, 2)
                    norm = fin and l == LAYERS - 1
                    if main:
                        chunk_max(b, u, 0)
                    if av:
                        lo(*p, 0)
                        lo(*p, 1)
                    if fin:
                        finish(*pp)
                    if main:
                        chunk_max(b, u, 1)
                    if norm:
                        finish2(*pp)
                    if main:
                        chunk_max(b, u, 2)
                    if fin:
                        rows_lo(*pp)
                    if norm:
                        finish3(*pp)
                    if main:
                        chunk_max(b, u, 3)
                        row_max(b, u)
                    if av:
                        lo(*p, 2)
                    if norm:
                        finish4(*pp)
                    if av:
                        lo(*p, 3)
                    if norm:
                        finish5(*pp)
                    if av:
                        row_sum(*p)
                    if main and not last:
                        degree(b, u)
                    if av:
                        if l and not last:
                            low_bits(*p)
                        if last:
                            lo(b, u, 0)
                            lo(b, u, 1)
                        scaled(*p)

                slot(0, 0, av=False, fin=False)
                slot(0, 1, fin=False)
                slot(2, 0)
                slot(2, 1)
                with dve.Fori(2, NT // 2 - 1) as half:
                    b = 2 * half
                    slot(b, 0)
                    slot(b, 1)
                slot(NT - 2, 0)
                slot(NT - 2, 1, last=True)
                if l < LAYERS - 1:
                    finish(NT - 2, 0)
                    weight_lo(l + 1)
                    lo(NT - 2, 1, 2)
                    rows_lo(NT - 2, 0)
                    lo(NT - 2, 1, 3)
                    row_sum(NT - 2, 1)
                    scaled(NT - 2, 1)
                    degree(NT - 2, 1)
                return (finish, rows_lo, low_bits), (lo, finish, finish2, finish3, finish4, finish5, row_sum, scaled)

            last_layer = None
            for l, g in enumerate(G):
                last_layer = layer(l, g, last_layer)
            lo, finish, finish2, finish3, finish4, finish5, row_sum, scaled = last_layer[1]

            def n_inverse(first, last, times):
                dve.wait_ge(s_sd0, times)
                nc.vector.reciprocal(rstd[:, first:last], sd[:, first:last]).then_inc(s_rstd0, 1)

            def n_rows(t, c):
                if isinstance(t, int):
                    dve.wait_ge(s_rstd0, 1 if t < NT - 2 else 2)
                    if 2 <= t < NCH:
                        ge(dve, G[-1].new, NT - 3 + t)
                ge(dve, n_xtr, t - NCH + 1)
                ge(dve, n_out[c], 4 * (t - c))
                nc.vector.tensor_scalar(nrow[c][:, :], keep[:, t, :], mv[:, t, 0:1], rstd[:, bass.ds(t, 1)],
                                        ALU.subtract, ALU.mult).then_inc(n_new, 1)

            def n_lo(t, u):
                dve.wait_ge(n_xth, t + 1)
                ge(dve, n_prj, t - 1)
                rest(xt_l[u][:, :, :], xb[u][:, 0:D].rearrange("p (k i) -> p k i", k=KT), xt_h[u][:, :, :])\
                    .then_inc(n_xtl, 1)

            def n_moving(t, u):
                dve.wait_ge(n_ph, t + 1)
                nc.vector.scalar_tensor_tensor(pm[:, t, D:2 * D], jb[u][:, 0:D], dinv[:, bass.ds(t, 1)],
                                               pm[:, t, 0:D].bitcast(F32), ALU.mult, ALU.subtract)\
                    .then_inc(n_pl, 1)

            ge(dve, G[1].deg, NT - 2)
            nc.vector.tensor_reduce(lowbits[:, :], bits[:, :], AX.X, ALU.max).then_inc(s_bits, 1)
            nc.vector.tensor_scalar(rdeg[:, :], deg[:, :], DEG_EPS, None, ALU.add).then_inc(s_dpl, 1)
            finish(NT - 2, 0)
            dve.wait_ge(s_dpl, 1)
            nc.vector.reciprocal(rdeg[:, :], rdeg[:, :]).then_inc(s_dinv, 1)
            dve.wait_ge(s_dsq, 1)
            nc.vector.reciprocal(dinv[:, :], dsq[:, :]).then_inc(s_dinv, 1)
            finish2(NT - 2, 0)
            row_sum(NT - 2, 1)
            lo(NT - 2, 1, 2)
            n_inverse(0, NT - 2, 1)
            finish3(NT - 2, 0)
            ge(dve, G[0].rows, NT)
            ge(dve, G[0].xtr, NT)
            n_rows(0, 0)
            lo(NT - 2, 1, 3)
            n_rows(1, 1)
            finish4(NT - 2, 0)
            n_lo(0, 0)
            finish5(NT - 2, 0)
            scaled(NT - 2, 1)
            dve.wait_ge(s_dinv, 2)
            n_rows(2, 2)
            n_lo(1, 1)
            n_moving(0, 0)
            finish(NT - 2, 1)
            finish2(NT - 2, 1)
            n_rows(3, 3)
            n_lo(2, 0)
            finish3(NT - 2, 1)
            n_moving(1, 1)
            finish4(NT - 2, 1)
            finish5(NT - 2, 1)

            def n_step(q, c, ahead=True):
                n_lo(NCH * q + c - 1, 1 - c % 2)
                if ahead:
                    n_rows(NCH * q + c + 1, (c + 1) % NCH)
                n_moving(NCH * q + c - 2, c % 2)

            n_rows(NCH, 0)
            with dve.Fori(1, AHEAD - 1) as q:
                for c in range(NCH):
                    n_step(q, c)
            n_inverse(NT - 2, NT, 2)
            dve.wait_ge(s_any, 1)
            nc.vector.tensor_copy(anylow[:, :], ob[0][0:1, 0:1]).then_inc(s_flag, 1)
            for c in range(NCH):
                n_step(AHEAD - 1, c, ahead=c < NCH - 1)
            n_lo(NT - 1, 1)
            n_moving(NT - 2, 0)
            ge(dve, C.kept, 4)
            nc.vector.tensor_copy(stat[0][:, N // 2:N], adjt[:, 0, N // 2:N]).then_inc(C.back.sem, 1)
            n_moving(NT - 1, 1)

            def parts(k, a):
                w, prev = a.w, aggs[k - 1] if k else None

                def split(q):
                    js = slice(*PIECES[q])
                    ge(dve, a.ph, q + 1)
                    rest(pm[:, js, w:2 * w], keep[:, js, 0:w], pm[:, js, 0:w]).then_inc(a.pl.sem, 1)

                def rows_lo(b, u):
                    t = b + u
                    if a.proj:
                        kt = a.proj[2]
                        ge(dve, a.xth, t + 1)
                        ge(dve, a.prj, t - 1)
                        rest(xt_l[u][:, 0:kt, :], xb[u][:, 0:kt * P].rearrange("p (k i) -> p k i", k=kt),
                             xt_h[u][:, 0:kt, :]).then_inc(a.xtl.sem, 1)

                def total(b, u):
                    t = b + u
                    ge(dve, a.tmp, t + 1)
                    dst, o = zb[u][:, 0:w], ob[u][:, 0:w]
                    if a is F:
                        ge(dve, a.xtr, t - 1)
                        dst = rin[u][:, 0:w]
                    if a in (C, Dg):
                        d = dinv if a is C else rdeg
                        nc.vector.scalar_tensor_tensor(dst, o, d[:, bass.ds(t, 1)], tmp[:, 0:w],
                                                       ALU.mult, ALU.add).then_inc(a.r.sem, 1)
                    else:
                        nc.vector.tensor_tensor(dst, o, tmp[:, 0:w], ALU.add).then_inc(a.r.sem, 1)

                def rows_free(b, u):
                    if isinstance(b, int) and b == 0:
                        if not k:
                            dve.wait_ge(n_xtr, NT)
                            for c in range(NCH):
                                dve.wait_ge(n_out[c], 16 * NT // NCH)
                        else:
                            last = prev if prev.norm else aggs[k - 2]
                            ge(dve, last.out[u], 8 * NT)
                            ge(dve, last.xtr, NT)

                def residual(b, u):
                    with_residual(b, u)
                    if a.norm:
                        statistics(b, u)
                        mean_variance(b, u)

                def with_residual(b, u):
                    t = b + u
                    if a is C:
                        ge(dve, a.r, t + 1)
                    else:
                        ge(dve, a.rb, t + 1)
                    if not a.norm:
                        nc.vector.tensor_scalar(keep[:, t, 0:w], zb[u][:, 0:w], 0.0, None, ALU.max)\
                            .then_inc(a.new.sem, 1)
                        return
                    if a.last:
                        ge(dve, a.prj, t + 1)
                        ge(dve, a.new, t - 1)
                        nc.vector.tensor_tensor(zb[u][:, :], jb[u][:, 0:D], xres[u][:, :], ALU.add)\
                            .then_inc(a.y.sem, 1)
                    else:
                        ge(dve, a.xres[u], 8 * b + 16)
                        nc.vector.scalar_tensor_tensor(zb[u][:, :], zb[u][:, :], 0.0, xres[u][:, :],
                                                       ALU.max, ALU.add).then_inc(a.y.sem, 1)

                def statistics(b, u):
                    t = b + u
                    ge(dve, a.y, t + 1)
                    nc.vector.bn_stats(stats[u][:, :], zb[u][:, :]).then_inc(a.stat.sem, 1)

                def mean_variance(b, u):
                    t = b + u
                    ge(dve, a.stat, t + 1)
                    ge(dve, a.sd, t - 1)
                    alone(dve, passed["vector"])
                    nc.vector.bn_aggr(mv[:, u, :], stats[u][:, :]).then_inc(a.mv.sem, 1)

                def norm(b, u):
                    if a.norm:
                        inverse(b, u)
                        normed(b, u)

                def inverse(b, u):
                    t = b + u
                    ge(dve, a.sd, t + 1)
                    nc.vector.reciprocal(rstd[:, u:u + 1], sd[:, u:u + 1]).then_inc(a.rstd.sem, 1)

                def normed(b, u):
                    t = b + u
                    ge(dve, a.rstd, t + 1)
                    rows_free(b, u)
                    if a.proj and not a.last:
                        ge(dve, a.xtr, t - 1)
                    ge(dve, a.out[u], 8 * b)
                    nc.vector.tensor_scalar(xs[u][:, :], zb[u][:, :], mv[:, u, 0:1], rstd[:, u:u + 1],
                                            ALU.subtract, ALU.mult).then_inc(a.new.sem, 1)

                def self_term(b, u):
                    t = b + u
                    if a is C:
                        ge(dve, a.prj, t + 1)
                        ge(dve, a.pk, t + 1)
                        ge(dve, a.rout, 16 * t)
                        nc.vector.tensor_tensor(rst[:, :], jb[u][:, D:2 * D], bsum[:, :], ALU.add)\
                            .then_inc(a.rt.sem, 1)

                steps = (with_residual, statistics, mean_variance, inverse, normed)
                return split, rows_lo, total, residual, norm, self_term, steps

            def general():
                for k, a in enumerate(aggs):
                    split, rows_lo, total, residual, norm, self_term, _ = parts(k, a)

                    def lo(t, c):
                        n = 4 * t + c
                        ge(dve, a.ah, n + 1)
                        ge(dve, a.mm, n - 3)
                        rest(ringl[c], adjt[:, t, c * CH:(c + 1) * CH], ringh[c]).then_inc(a.al.sem, 1)

                    def slot(b, u, main=True, nxt=True, ep=True, fin=True, fresh=True):
                        t = b + u
                        p, pp = before(b, u), before(b, u, 2)
                        if fin:
                            rows_lo(*pp)
                        if ep:
                            total(*p)
                        if main:
                            lo(t, 2)
                        e = before(b, u, 3) if a is F else p
                        ended = inside(*e, NT) if a is F else ep
                        if ended:
                            residual(*e)
                        if main:
                            lo(t, 3)
                        if ended:
                            norm(*e)
                        if fin:
                            self_term(*pp)
                        if nxt:
                            lo(t + 1, 0)
                            lo(t + 1, 1)

                    if k:
                        for q in range(len(PIECES)):
                            split(q)
                    lo(0, 0)
                    lo(0, 1)
                    slot(0, 0, ep=False, fin=False)
                    slot(0, 1, fin=False)
                    slot(2, 0)
                    slot(2, 1)
                    middle(dve, a, slot)
                    slot(NT - 2, 0)
                    slot(NT - 2, 1, nxt=False)
                    slot(NT, 0, main=False, nxt=False)
                    slot(NT, 1, main=False, nxt=False, ep=False)
                    if a is F:
                        slot(NT + 2, 0, main=False, nxt=False, ep=False, fin=False)

            def exact():
                def back(k, b, u):
                    a, t = aggs[k], b + u
                    if k and isinstance(t, int) and t < 2:
                        ge(dve, aggs[k - 1].mm, 4 * (NT - 2 + t) + 4)
                    if a is C:
                        ge(dve, a.kept, 4 * t + 4)
                    ge(dve, a.mm, 4 * t - 4)
                    nc.vector.tensor_copy(stat[u][:, N // 2:N], adjt[:, t, N // 2:N]).then_inc(a.back.sem, 1)

                for k, a in enumerate(aggs):
                    _, rows_lo, total, residual, norm, self_term, steps = parts(k, a)
                    with_residual, statistics, mean_variance, inverse, normed = steps

                    def slot(b, u, nxt=True, ep=True, fin=True, fresh=True):
                        p, pp, n = before(b, u), before(b, u, 2), after(b, u)
                        if ep:
                            total(*p)
                        if a is F:
                            y, z = before(b, u, 3), before(b, u, 4)
                            summed, ended = inside(*y, NT), inside(*z, NT)
                            if fin:
                                rows_lo(*pp)
                            if summed:
                                with_residual(*y)
                            if ended:
                                inverse(*z)
                            if summed:
                                statistics(*y)
                            if ended:
                                normed(*z)
                            if summed:
                                mean_variance(*y)
                            if nxt:
                                back(k, *n)
                            return
                        if a is C:
                            if ep:
                                residual(*p)
                            if fin:
                                rows_lo(*pp)
                        else:
                            back(k, *n)
                            if fin:
                                rows_lo(*pp)
                            if ep:
                                residual(*p)
                        if ep:
                            norm(*p)
                        if a is C:
                            back(k, *n)
                        if fin:
                            self_term(*pp)

                    if k == 0:
                        slot(0, 0, ep=False, fin=False)
                    slot(0, 1, fin=False)
                    slot(2, 0)
                    slot(2, 1)
                    middle(dve, a, slot)
                    slot(NT - 2, 0, fresh=False)
                    if a.last:
                        slot(NT - 2, 1, nxt=False)
                        slot(NT, 0, nxt=False)
                        slot(NT, 1, nxt=False, ep=False)
                        slot(NT + 2, 0, nxt=False, ep=False, fin=False)
                        slot(NT + 2, 1, nxt=False, ep=False, fin=False)
                        continue
                    total(NT - 2, 0)
                    split = parts(k + 1, aggs[k + 1])[0]
                    rows_lo(NT - 4, 1)
                    residual(NT - 2, 0)
                    split(0)
                    norm(NT - 2, 0)
                    self_term(NT - 4, 1)
                    split(1)
                    back(k + 1, 0, 0)
                    total(NT - 2, 1)
                    rows_lo(NT - 2, 0)
                    residual(NT - 2, 1)
                    norm(NT - 2, 1)
                    split(2)
                    self_term(NT - 2, 0)
                    back(k + 1, 0, 1)
                    rows_lo(NT - 2, 1)
                    split(3)
                    self_term(NT - 2, 1)
                    split(4)

            dve.wait_ge(s_flag, 1)
            low = dve.value_load(anylow[0:1, 0:1])
            with dve.If(low > 0):
                general()
            with dve.Else():
                exact()

        @block.tensor
        def _(pe):
            def mm(o, l, r, start, stop):
                return nc.tensor.matmul(o, l, r, start=start, stop=stop)

            def exact3(o, pairs):
                terms = [p for sh, sl, mh, ml in pairs for p in ((sh, mh), (sh, ml), (sl, mh))]
                for i, (s, m) in enumerate(terms):
                    last = mm(o, s, m, i == 0, i == len(terms) - 1)
                return last

            pe.wait_ge(s_id, 2)
            def features(i):
                pe.wait_ge(s_x[i], 16)
                for k in range(KT):
                    if i == 1:
                        pe.wait_ge(s_x0l, k + 1)
                    elif i:
                        ge(pe, G[0].vl, 2 * (i - 1) + 1)
                    for a in range(TPC):
                        last = nc.tensor.transpose(tb[k][:, a * P:(a + 1) * P],
                                                   keep[:, i * TPC + a, k * P:(k + 1) * P], ident[:, :])
                    last.then_inc(s_x0t, 1)

            def weights():
                pe.wait_ge(s_wraw, 5 * 16)
                ge(pe, G[0].vl, 2 * (NCH - 1) + 1)
                for k in range(KT):
                    for i, raw in enumerate((wn_raw, ws_raw)):
                        for o in range(KT):
                            at = i * D + o * P
                            last = nc.tensor.transpose(tb[k][:, at:at + P], raw[:, o, k * P:(k + 1) * P],
                                                       ident[:, :])
                    last.then_inc(s_w2t, 1)

            features(0)
            features(1)

            def layer(l, g, previous):
                pe.wait_ge(s_wgl[l], 1)
                if l:
                    ge(pe, G[l - 1].ex, 4 * NT)
                pe.sem_inc(g.prod.sem, 1)
                pe.sem_inc(g.wsl.sem, 1)
                pe.sem_inc(g.staged.sem, 1)
                pe.sem_inc(g.vl.sem, 1)

                def project(i):
                    if l:
                        ge(pe, G[l - 1].xtl, TPC * i + TPC)
                    else:
                        ge(pe, s_x0l, KT * (i + 1))
                    gs = bass.ts(i, CH)
                    for o in range(2 * KT):
                        if not l and o == KT:
                            if i in (1, 2):
                                features(i + 1)
                            if i == 3:
                                weights()
                        if o < KT:
                            ge(pe, g.staged, KT * i + 1)
                        else:
                            ge(pe, g.wsl, KT * i + 1)
                        if l and o == 2 * KT - 1:
                            ge(pe, G[l - 1].z, NT)
                        os = slice(o * P, (o + 1) * P)
                        exact3(scores[:, o * CH:(o + 1) * CH],
                               [(wg_h[:, k, os], wg_l[:, k, os], xtall_h[:, k, gs], xtall_l[:, k, gs])
                                for k in range(KT)]).then_inc(g.prod.sem, 1)

                def values(i, h):
                    if h == 0:
                        if l:
                            ge(pe, G[l - 1].al, 4 * NT)
                        if not l:
                            ge(pe, s_x0l, KT * min(i + 2, NCH))
                            if i == NCH - 1:
                                ge(pe, s_w2l, KT)
                        ge(pe, g.staged, KT * i + KT + 1)
                        ge(pe, g.vl, 2 * i + 1)
                    for a in range(2):
                        for k in range(KT):
                            at = a * D + k * P
                            last = nc.tensor.transpose(tb[h][:, at:at + P],
                                                       wht_g[:, k, (2 * h + a) * P:(2 * h + a + 1) * P],
                                                       ident[:, :])
                    last.then_inc(g.vt.sem, 1)

                def score(b, u, c):
                    t = b + u
                    if c == 0:
                        ge(pe, g.q, t + 1)
                    if isinstance(t, int) and t == 0:
                        ge(pe, g.wsl, KT * (c + 1) + 1 if c < KT else KT * NCH + 1)
                        ge(pe, g.staged, KT * NCH + 1)
                    ge(pe, g.ex, 4 * t + c - 3)
                    cs = slice(c * CH, (c + 1) * CH)
                    exact3(scores[:, cs], [(whs_h[u][:, k, :], whs_l[u][:, k, :], wst_h[:, k, cs], wst_l[:, k, cs])
                                           for k in range(KT)]).then_inc(g.sc.sem, 1)

                def turn(b, u, c):
                    n = 4 * (b + u) + c
                    ge(pe, g.msk, n + 1)
                    ge(pe, g.al, n - 1)
                    for q in range(TPC):
                        j = c * TPC + q
                        last = nc.tensor.transpose(tb[c % 2][:, q * P:(q + 1) * P], prob[u][:, j * P:(j + 1) * P],
                                                   ident[:, :])
                    last.then_inc(g.tr.sem, 1)

                def attend(b, u, c):
                    t = b + u
                    ge(pe, g.al, 4 * t + c + 1)
                    bank = attention_bank(b, u)
                    if c == 0 and bank is ob0:
                        ge(pe, g.z, t)
                    elif c == 0:
                        ge(pe, g.ex, 4 * NT)
                    for q in range(TPC):
                        j = c * TPC + q
                        qs = slice(q * P, (q + 1) * P)
                        mm(bank[:, 0:2 * D], ringh[c][:, qs], val[:, j, :], j == 0, False)
                        last = mm(bank[:, 0:D], ringl[c][:, qs], val[:, j, 0:D], False, j == NT - 1)
                    last.then_inc(g.av.sem, 1)

                def rows(b, u):
                    if l < LAYERS - 1:
                        t = b + u
                        ge(pe, g.new, t + 1)
                        ge(pe, g.xtl, t)
                        for k in range(KT):
                            last = nc.tensor.transpose(xb0[:, k * P:(k + 1) * P], xs[u][:, k * P:(k + 1) * P],
                                                       ident[:, :])
                        last.then_inc(g.xtr.sem, 1)

                def slot(b, u, main=True, av=True, fin=True, last=False):
                    p = before(b, u)
                    if main:
                        score(b, u, 0)
                    if av:
                        turn(*p, 0)
                        turn(*p, 1)
                    if main:
                        score(b, u, 1)
                        score(b, u, 2)
                    if fin:
                        rows(*before(b, u, 2))
                    if main:
                        score(b, u, NCH - 1)
                    if av:
                        turn(*p, 2)
                        attend(*p, 0)
                        turn(*p, 3)
                        attend(*p, 1)
                        if last:
                            turn(b, u, 0)
                        attend(*p, 2)
                        if last:
                            turn(b, u, 1)
                        attend(*p, 3)

                def whole(i):
                    project(i)
                    values(i, 0)
                    values(i, 1)

                if l:
                    with pe.Fori(0, NCH - 2) as i:
                        whole(i)
                    previous[0](NT, 1, main=False, av=False)
                    whole(NCH - 2)
                else:
                    for i in range(NCH - 1):
                        whole(i)
                project(NCH - 1)
                score(0, 0, 0)
                values(NCH - 1, 0)
                values(NCH - 1, 1)
                for c in range(1, NCH):
                    score(0, 0, c)
                ge(pe, g.vl, 2 * NCH + 1)
                slot(0, 1, fin=False)
                slot(2, 0)
                slot(2, 1)
                with pe.Fori(2, NT // 2 - 1) as half:
                    b = 2 * half
                    slot(b, 0)
                    slot(b, 1)
                slot(NT - 2, 0)
                slot(NT - 2, 1, last=True)
                if l < LAYERS - 1:
                    turn(NT - 2, 1, 2)
                    attend(NT - 2, 1, 0)
                    turn(NT - 2, 1, 3)
                    attend(NT - 2, 1, 1)
                    rows(NT - 2, 0)
                    attend(NT - 2, 1, 2)
                    attend(NT - 2, 1, 3)
                return slot, turn, attend

            last_layer = None
            for l, g in enumerate(G):
                last_layer = layer(l, g, last_layer)
            _, turn, attend = last_layer

            def n_rows(t, c):
                u = c % 2
                pe.wait_ge(n_new, t + 1)
                ge(pe, n_xtl, t - 1)
                if isinstance(t, int) and t < 2:
                    ge(pe, G[-1].ex, 4 * NT)
                for k in range(KT):
                    last = nc.tensor.transpose(xb[u][:, k * P:(k + 1) * P], nrow[c][:, k * P:(k + 1) * P],
                                               ident[:, :])
                last.then_inc(n_xtr, 1)

            def n_proj(t, u):
                pe.wait_ge(n_xtl, t + 1)
                ge(pe, n_pl, t - 1)
                exact3(jb[u][:, 0:D], [(xt_h[u][:, k, :], xt_l[u][:, k, :], w1h[:, k, :], w1l[:, k, :])
                                       for k in range(KT)]).then_inc(n_prj, 1)

            def turn_adj(t, c):
                n = 4 * t + c
                ge(pe, C.nat[c], 16 * t + 16)
                ge(pe, C.kept, n - 1)
                if isinstance(n, int) and n < 2:
                    ge(pe, G[-1].al, 4 * NT)
                for q in range(TPC):
                    last = nc.tensor.transpose(tb[c % 2][:, q * P:(q + 1) * P], nat[c][:, q * P:(q + 1) * P],
                                               ident[:, :])
                last.then_inc(C.tr.sem, 1)

            turn(NT - 2, 1, 2)
            attend(NT - 2, 1, 0)
            turn(NT - 2, 1, 3)
            attend(NT - 2, 1, 1)
            attend(NT - 2, 1, 2)
            n_rows(0, 0)
            attend(NT - 2, 1, 3)
            turn_adj(0, 0)
            n_rows(1, 1)
            turn_adj(0, 1)
            n_proj(0, 0)
            n_rows(2, 2)
            turn_adj(0, 2)
            n_proj(1, 1)
            n_rows(3, 3)
            turn_adj(0, 3)
            n_proj(2, 0)
            pe.wait_ge(s_bits, 1)
            pe.wait_ge(s_cst, 2)
            mm(ob[0][0:1, 0:1], lowbits[:, :], one[:, :], True, True).then_inc(s_any, 1)

            def n_step(q, c):
                n_rows(NCH * q + c, c)
                turn_adj(q, c)
                n_proj(NCH * q + c - 1, 1 - c % 2)

            with pe.Fori(1, AHEAD - 1) as q:
                for c in range(NCH):
                    n_step(q, c)
            for c in range(NCH):
                n_step(AHEAD - 1, c)
            n_proj(NT - 1, 1)
            pe.wait_ge(s_idr, 1)

            def parts(k, a):
                prev = aggs[k - 1] if k else None

                def begin(b, u, c):
                    t = b + u
                    if not k and isinstance(t, int) and t < 2:
                        ge(pe, n_pl, TPC * (c + 1))
                        ge(pe, s_flag, 1)
                    if k and isinstance(t, int) and t < 2:
                        ge(pe, prev.r, NT - 1 + t)
                        ge(pe, a.pl, c + 1 + c // (NCH - 1))
                    if c == 0:
                        ge(pe, a.r, t - 1)

                def rows(b, u):
                    t = b + u
                    if a.proj:
                        ge(pe, a.r if a.last else a.new, t + 1)
                        src = rin[u] if a.last else xs[u]
                        if k and isinstance(t, int) and t < 2 and prev.proj:
                            ge(pe, prev.xtl, NT)
                        ge(pe, a.xtl, t - 1)
                        for h in range(a.proj[2]):
                            hs = slice(h * P, (h + 1) * P)
                            last = nc.tensor.transpose(xb[u][:, hs], src[:, hs], ident[:, :])
                        last.then_inc(a.xtr.sem, 1)

                def project(b, u):
                    t = b + u
                    if a.proj:
                        wh, wl, kt, width = a.proj
                        wh3 = wh[:, :, :] if kt > 1 else wh[:, :].rearrange("p (k n) -> p k n", k=1)
                        wl3 = wl[:, :, :] if kt > 1 else wl[:, :].rearrange("p (k n) -> p k n", k=1)
                        ge(pe, a.xtl, t + 1)
                        if k and isinstance(t, int) and t < 2 and prev.proj:
                            ge(pe, prev.pk, NT)
                            if prev is C:
                                ge(pe, prev.rt, NT)
                        ge(pe, a.y if a.last else a.pk, t - 1)
                        if a is C:
                            ge(pe, a.rt, t - 1)
                        exact3(jb[u][:, 0:width], [(xt_h[u][:, h, :], xt_l[u][:, h, :], wh3[:, h, :], wl3[:, h, :])
                                                   for h in range(kt)]).then_inc(a.prj.sem, 1)

                return begin, rows, project

            def general():
                for k, a in enumerate(aggs):
                    begin, rows, project = parts(k, a)
                    w = a.w

                    def main_sum(b, u, c):
                        t = b + u
                        begin(b, u, c)
                        ge(pe, a.al, 4 * t + c + 1)
                        for q in range(TPC):
                            j = c * TPC + q
                            qs = slice(q * P, (q + 1) * P)
                            end = j == NT - 1
                            mm(ob[u][:, 0:2 * w], ringh[c][:, qs], pm[:, j, 0:2 * w], j == 0, False)
                            last = mm(ob[u][:, 0:w], ringl[c][:, qs], pm[:, j, 0:w], False, end and a is not C)
                        if c == NCH - 1 and a is C:
                            last = mm(ob[u][:, 0:2 * w], identr[:, :], pm[:, t, :], False, True)
                        last.then_inc(a.mm.sem, 1)

                    def slot(b, u, main=True, ep=True, fin=True, fresh=True):
                        for c in range(NCH):
                            if main:
                                main_sum(b, u, c)
                            if a is C and fresh:
                                turn_adj(b + u + AHEAD, c)
                            if c == 1 and fin:
                                project(*before(b, u, 2))
                        if ep:
                            rows(*before(b, u))

                    slot(0, 0, ep=False, fin=False)
                    slot(0, 1, fin=False)
                    slot(2, 0)
                    slot(2, 1)
                    middle(pe, a, slot)
                    slot(NT - 2, 0, fresh=False)
                    slot(NT - 2, 1, fresh=False)
                    slot(NT, 0, main=False, fresh=False)
                    slot(NT, 1, main=False, ep=False, fresh=False)

            def exact():
                def main_sum(k, b, u, c, signals=1):
                    a, t = aggs[k], b + u
                    w = a.w
                    parts(k, a)[0](b, u, c)
                    if c == 0:
                        ge(pe, a.front, t + 1)
                    elif c == NCH // 2:
                        ge(pe, a.back, t + 1)
                    for q in range(TPC):
                        j = c * TPC + q
                        last = mm(ob[u][:, 0:2 * w], stat[u][:, j * P:(j + 1) * P], pm[:, j, 0:2 * w], j == 0,
                                  j == NT - 1 and a is not C)
                        if TPC - signals <= q < TPC - 1:
                            last.then_inc(a.mm.sem, 1)
                    if c == NCH - 1 and a is C:
                        last = mm(ob[u][:, 0:2 * w], identr[:, :], pm[:, t, :], False, True)
                    if signals:
                        last.then_inc(a.mm.sem, 1)

                for k, a in enumerate(aggs):
                    _, rows, project = parts(k, a)

                    def slot(b, u, fin=True, fresh=True, late=False):
                        if a is F and fin:
                            rows(*before(b, u, 2))
                        for c in range(NCH):
                            main_sum(k, b, u, c)
                            if late and u and c == 0:
                                project(0, 0)
                            if late and not u and c == NCH - 1:
                                rows(0, 0)
                            if late and u and c == 1:
                                rows(0, 1)
                            if late and u and c == NCH - 1:
                                project(0, 1)
                            if a is C and fresh:
                                turn_adj(b + u + AHEAD, c)
                            if a is not F and c == 0 and fin:
                                rows(*before(b, u, 2))
                            if c == NCH - 2 and fin:
                                project(*before(b, u, 2))

                    if k == 0:
                        slot(0, 0, fin=False)
                        slot(0, 1, fin=False)
                    slot(2, 0, fin=not k, late=k > 0)
                    slot(2, 1, fin=not k, late=k > 0)
                    middle(pe, a, slot)
                    slot(NT - 2, 0, fresh=False)
                    slot(NT - 2, 1, fresh=False)
                    if a.last:
                        for u in range(2):
                            rows(NT - 2, u)
                            project(NT - 2, u)
                        continue
                    main_sum(k + 1, 0, 0, 0)
                    rows(NT - 2, 0)
                    main_sum(k + 1, 0, 0, 1)
                    main_sum(k + 1, 0, 1, 0, signals=0)
                    project(NT - 2, 0)
                    main_sum(k + 1, 0, 1, 1, signals=0)
                    rows(NT - 2, 1)
                    main_sum(k + 1, 0, 0, 2)
                    project(NT - 2, 1)
                    main_sum(k + 1, 0, 1, 2, signals=0)
                    main_sum(k + 1, 0, 0, NCH - 1)
                    main_sum(k + 1, 0, 1, NCH - 1, signals=NCH)

            pe.wait_ge(s_flag, 1)
            low = pe.value_load(anylow[0:1, 0:1])
            with pe.If(low > 0):
                general()
            with pe.Else():
                exact()


_INS = ["x", "adj", "L0_gnn_W_stack", "L1_gnn_W", "L2_gnn_W_neigh", "L2_gnn_b_neigh", "L2_gnn_W_self",
        "L2_gnn_b_self", "L3_gnn_W1", "L3_gnn_b1", "L3_gnn_W2", "L3_gnn_b2"]


def kernel(**inputs):
    import numpy as _np
    import concourse.bacc as _bacc
    from concourse import mybir as _mybir
    from concourse.bass_utils import run_bass_kernel_spmd as _run

    nc = _bacc.Bacc("TRN2", target_bir_lowering=False, num_devices=1, dynamic_dma_scratch_size=1024)
    arrays, args = {}, []
    for name in _INS:
        a = _np.ascontiguousarray(inputs[name])
        arrays[f"in_{name}"] = a
        args.append(nc.dram_tensor(f"in_{name}", a.shape, _mybir.dt.from_np(a.dtype), kind="ExternalInput").ap())
    shape = inputs["x"].shape
    args.append(nc.dram_tensor("out_rows", shape, _mybir.dt.float32, kind="ExternalOutput").ap())
    adjacency_resnet(nc, *args)
    r = _run(nc, [arrays], core_ids=[0])
    return r.results[0]["out_rows"]
```
